# Optimizing a Trainium2 kernel written in Bass

```python
import numpy as np
import jax
import jax.numpy as jnp

def _softmax(x, axis=-1):
    return jax.nn.softmax(x, axis=axis)

def _gelu(x):
    return jax.nn.gelu(x, approximate=True)

def _silu(x):
    return jax.nn.silu(x)

def _sigmoid(x):
    return jax.nn.sigmoid(x)

def _layernorm(x, axis=-1, eps=1e-05):
    m = jnp.mean(x, axis=axis, keepdims=True)
    v = jnp.var(x, axis=axis, keepdims=True)
    return (x - m) / jnp.sqrt(v + eps)

def _scatter_add(tgt, idx, src, axis=0):
    return tgt.at[idx].add(src)

def _segment_sum(src, seg, n):
    return jax.ops.segment_sum(src, seg, n)
kernel_name = 'mk_audio_tower_d1_tok_audfeat256_r4_011a84'

def setup_inputs(seed: int=0):
    np.random.seed(seed)
    _w = jnp.asarray

    def _rec_inputs():
        import jax
        import jax.numpy as jnp
        _rk = jax.random.key(seed)
        x = -0.000292821 + 1.00034 * jax.random.normal(jax.random.fold_in(_rk, 1), (8, 375, 64), jnp.float32)
        return x
    x = _rec_inputs()

    def _L0_tok_setup():
        import jax, jax.numpy as jnp
        import numpy as np
        NHEAD = 8
        KSIZE = 32
        EPS = 1e-05
        DIV_BASE = 10.0

        def _pos_encoding(S, D):
            pos = np.arange(S)[:, None].astype(np.float64)
            div = np.exp(np.arange(0, D, 2) * (-np.log(10000.0) / D))
            pe = np.zeros((S, D), np.float32)
            pe[:, 0::2] = np.sin(pos * div)
            pe[:, 1::2] = np.cos(pos * div)
            return jnp.asarray(pe)

        def _layer_norm(x, g, b):
            m = x.mean(-1, keepdims=True)
            v = ((x - m) ** 2).mean(-1, keepdims=True)
            return (x - m) / jnp.sqrt(v + EPS) * g + b

        def _mha(x, in_w, in_b, out_w, out_b):
            B, S, D = x.shape
            dh = D // NHEAD
            qkv = x @ in_w.T + in_b
            q, k, v = jnp.split(qkv, 3, axis=-1)
            sp = lambda t: t.reshape(B, S, NHEAD, dh).transpose(0, 2, 1, 3)
            q, k, v = (sp(q), sp(k), sp(v))
            att = jax.nn.softmax(jnp.einsum('bhqd,bhkd->bhqk', q, k) / jnp.sqrt(jnp.float32(dh)), axis=-1)
            o = jnp.einsum('bhqk,bhkd->bhqd', att, v).transpose(0, 2, 1, 3).reshape(B, S, D)
            return o @ out_w.T + out_b

        def _forward(x, l_in_w, l_in_b, l_out_w, l_out_b, ln1_g, ln1_b, ff_w1, ff_b1, ff_w2, ff_b2, ln2_g, ln2_b, m_in_w, m_in_b, m_out_w, m_out_b):
            B, L, D = x.shape
            amp = jnp.abs(jnp.fft.rfft(x, axis=1))
            feat = jax.lax.stop_gradient(jnp.concatenate([x[:, -1:, :], amp], axis=1))
            src = feat + _pos_encoding(feat.shape[1], D)[None]
            a = _mha(src, l_in_w, l_in_b, l_out_w, l_out_b)
            src = _layer_norm(src + a, ln1_g, ln1_b)
            ff = jax.nn.relu(src @ ff_w1.T + ff_b1) @ ff_w2.T + ff_b2
            src = _layer_norm(src + ff, ln2_g, ln2_b)
            out = _mha(src, m_in_w, m_in_b, m_out_w, m_out_b)
            tau = jnp.clip(jax.nn.softplus(out[:, -1:, :]) / DIV_BASE, 0.01, 1.0)
            Lout = L - KSIZE + 1
            idx = jnp.arange(Lout)[:, None] + jnp.arange(KSIZE)[None, :]
            xw = x[:, idx, :]
            seq = jnp.arange(KSIZE - 1, -1, -1, dtype=x.dtype)
            powers = tau[:, 0, :, None] ** seq
            w = powers / powers.sum(-1, keepdims=True)
            return jnp.einsum('bdk,blkd->bld', w, xw)
        key = jax.random.key(seed)
        ks = jax.random.split(key, 12)
        B, L, D = (128, 128, 64)
        Dff = 4 * D
        s = 0.02
        inp = {'x': jax.random.normal(ks[0], (B, L, D), jnp.float32), 'l_in_w': jax.random.normal(ks[1], (3 * D, D), jnp.float32) * s, 'l_in_b': jnp.zeros((3 * D,), jnp.float32), 'l_out_w': jax.random.normal(ks[2], (D, D), jnp.float32) * s, 'l_out_b': jnp.zeros((D,), jnp.float32), 'ln1_g': jnp.ones((D,), jnp.float32), 'ln1_b': jnp.zeros((D,), jnp.float32), 'ff_w1': jax.random.normal(ks[3], (Dff, D), jnp.float32) * s, 'ff_b1': jnp.zeros((Dff,), jnp.float32), 'ff_w2': jax.random.normal(ks[4], (D, Dff), jnp.float32) * s, 'ff_b2': jnp.zeros((D,), jnp.float32), 'ln2_g': jnp.ones((D,), jnp.float32), 'ln2_b': jnp.zeros((D,), jnp.float32), 'm_in_w': jax.random.normal(ks[5], (3 * D, D), jnp.float32) * s, 'm_in_b': jnp.zeros((3 * D,), jnp.float32), 'm_out_w': jax.random.normal(ks[6], (D, D), jnp.float32) * s, 'm_out_b': jnp.zeros((D,), jnp.float32)}
        return inp
    _L0_tok_all = _L0_tok_setup()
    _L0_tok_in = {k: v for k, v in _L0_tok_all.items() if k in ('l_in_w', 'l_in_b', 'l_out_w', 'l_out_b', 'ln1_g', 'ln1_b', 'ff_w1', 'ff_b1', 'ff_w2', 'ff_b2', 'ln2_g', 'ln2_b', 'm_in_w', 'm_in_b', 'm_out_w', 'm_out_b')}
    del _L0_tok_all

    def _L0_attn_setup():
        import jax, jax.numpy as jnp
        import numpy as np
        GAMMA = 0.96875
        ROPE_THETA = 10000.0

        def _rope(x):
            B, S, d = x.shape
            inv_freq = 1.0 / ROPE_THETA ** (jnp.arange(0, d, 2, dtype=jnp.float32) / d)
            angles = jnp.arange(S, dtype=jnp.float32)[:, None] * inv_freq[None, :]
            cos = jnp.cos(angles).astype(x.dtype)
            sin = jnp.sin(angles).astype(x.dtype)
            xs = x.reshape(B, S, d // 2, 2)
            x0, x1 = (xs[..., 0], xs[..., 1])
            out = jnp.stack([x0 * cos - x1 * sin, x1 * cos + x0 * sin], axis=-1)
            return out.reshape(B, S, d)

        def _decay_mask(S, dtype):
            n = jnp.arange(S)[:, None]
            m = jnp.arange(S)[None, :]
            diff = n - m
            D = jnp.exp(jnp.maximum(diff, 0).astype(jnp.float32) * np.log(GAMMA))
            return jnp.where(diff >= 0, D, 0.0).astype(dtype)
        key = jax.random.key(seed)
        k1, k2, k3, k4 = jax.random.split(key, 4)
        H = 64
        X = jax.random.normal(k1, (4, 2048, H), dtype=jnp.float32)
        W_Q = jax.random.normal(k2, (H, H), dtype=jnp.float32) / H
        W_K = jax.random.normal(k3, (H, H), dtype=jnp.float32) / H
        W_V = jax.random.normal(k4, (H, H), dtype=jnp.float32) / H
        return {'X': X, 'W_Q': W_Q, 'W_K': W_K, 'W_V': W_V}
    _L0_attn_all = _L0_attn_setup()
    _L0_attn_in = {k: v for k, v in _L0_attn_all.items() if k in ('W_Q', 'W_K', 'W_V')}
    del _L0_attn_all

    def _L0_ffn_setup():
        import jax, jax.numpy as jnp
        import numpy as np
        DIM = 64
        HEADS = 8
        NUM_KEYS = 64
        NUM_KV = NUM_KEYS ** 2
        PK_TOPK = 16
        FINAL_TOPK = 16
        DIM_KEY = DIM // 2
        P = 2

        def _pk(x, Wq_pk, pk_keys):
            b, n, _ = x.shape
            q = (x @ Wq_pk).reshape(b, n, P, HEADS, DIM_KEY).transpose(2, 0, 1, 3, 4)
            sim = jnp.einsum('pbnhd,pkhd->pbnhk', q, pk_keys)
            scores, idx = jax.lax.top_k(sim, PK_TOPK)
            idx0 = idx[0]
            idx1 = idx[1] * NUM_KEYS
            index = (idx0[..., :, None] + idx1[..., None, :]).reshape(b, n, HEADS, PK_TOPK * PK_TOPK)
            score = (scores[0][..., :, None] + scores[1][..., None, :]).reshape(b, n, HEADS, PK_TOPK * PK_TOPK)
            final_scores, pk_idx = jax.lax.top_k(score, FINAL_TOPK)
            final_indices = jnp.take_along_axis(index, pk_idx, axis=-1)
            final_scores = jax.nn.softmax(final_scores, axis=-1)
            return (final_scores, final_indices)
        key = jax.random.key(seed)
        ks = jax.random.split(key, 7)
        b, n = (2, 256)
        std = 0.02
        x = jax.random.normal(ks[0], (b, n, DIM), dtype=jnp.float32)
        Wq_pk = jax.random.normal(ks[1], (DIM, P * HEADS * DIM_KEY), dtype=jnp.float32) * std
        pk_keys = jax.random.normal(ks[2], (P, NUM_KEYS, HEADS, DIM_KEY), dtype=jnp.float32) * std
        Wq = jax.random.normal(ks[3], (DIM, HEADS * DIM), dtype=jnp.float32) * std
        keys_table = jax.random.normal(ks[4], (NUM_KV * HEADS, DIM), dtype=jnp.float32) * std
        values_table = jax.random.normal(ks[5], (NUM_KV * HEADS, DIM), dtype=jnp.float32) * std
        Wo = jax.random.normal(ks[6], (DIM * HEADS, DIM), dtype=jnp.float32) * std
        return {'x': x, 'Wq_pk': Wq_pk, 'pk_keys': pk_keys, 'Wq': Wq, 'keys_table': keys_table, 'values_table': values_table, 'Wo': Wo}
    _L0_ffn_all = _L0_ffn_setup()
    _L0_ffn_in = {k: v for k, v in _L0_ffn_all.items() if k in ('Wq_pk', 'pk_keys', 'Wq', 'keys_table', 'values_table', 'Wo')}
    del _L0_ffn_all
    return {'x': x, 'L0_tok_l_in_w': _L0_tok_in['l_in_w'], 'L0_tok_l_in_b': _L0_tok_in['l_in_b'], 'L0_tok_l_out_w': _L0_tok_in['l_out_w'], 'L0_tok_l_out_b': _L0_tok_in['l_out_b'], 'L0_tok_ln1_g': _L0_tok_in['ln1_g'], 'L0_tok_ln1_b': _L0_tok_in['ln1_b'], 'L0_tok_ff_w1': _L0_tok_in['ff_w1'], 'L0_tok_ff_b1': _L0_tok_in['ff_b1'], 'L0_tok_ff_w2': _L0_tok_in['ff_w2'], 'L0_tok_ff_b2': _L0_tok_in['ff_b2'], 'L0_tok_ln2_g': _L0_tok_in['ln2_g'], 'L0_tok_ln2_b': _L0_tok_in['ln2_b'], 'L0_tok_m_in_w': _L0_tok_in['m_in_w'], 'L0_tok_m_in_b': _L0_tok_in['m_in_b'], 'L0_tok_m_out_w': _L0_tok_in['m_out_w'], 'L0_tok_m_out_b': _L0_tok_in['m_out_b'], 'L0_attn_W_Q': _L0_attn_in['W_Q'], 'L0_attn_W_K': _L0_attn_in['W_K'], 'L0_attn_W_V': _L0_attn_in['W_V'], 'L0_ffn_Wq_pk': _L0_ffn_in['Wq_pk'], 'L0_ffn_pk_keys': _L0_ffn_in['pk_keys'], 'L0_ffn_Wq': _L0_ffn_in['Wq'], 'L0_ffn_keys_table': _L0_ffn_in['keys_table'], 'L0_ffn_values_table': _L0_ffn_in['values_table'], 'L0_ffn_Wo': _L0_ffn_in['Wo']}

def reference(x, L0_tok_l_in_w, L0_tok_l_in_b, L0_tok_l_out_w, L0_tok_l_out_b, L0_tok_ln1_g, L0_tok_ln1_b, L0_tok_ff_w1, L0_tok_ff_b1, L0_tok_ff_w2, L0_tok_ff_b2, L0_tok_ln2_g, L0_tok_ln2_b, L0_tok_m_in_w, L0_tok_m_in_b, L0_tok_m_out_w, L0_tok_m_out_b, L0_attn_W_Q, L0_attn_W_K, L0_attn_W_V, L0_ffn_Wq_pk, L0_ffn_pk_keys, L0_ffn_Wq, L0_ffn_keys_table, L0_ffn_values_table, L0_ffn_Wo):
    import jax
    import jax.numpy as jnp

    def _L0_tok_ref(x, l_in_w, l_in_b, l_out_w, l_out_b, ln1_g, ln1_b, ff_w1, ff_b1, ff_w2, ff_b2, ln2_g, ln2_b, m_in_w, m_in_b, m_out_w, m_out_b):
        import jax, jax.numpy as jnp
        import numpy as np
        NHEAD = 8
        KSIZE = 32
        EPS = 1e-05
        DIV_BASE = 10.0

        def _pos_encoding(S, D):
            pos = np.arange(S)[:, None].astype(np.float64)
            div = np.exp(np.arange(0, D, 2) * (-np.log(10000.0) / D))
            pe = np.zeros((S, D), np.float32)
            pe[:, 0::2] = np.sin(pos * div)
            pe[:, 1::2] = np.cos(pos * div)
            return jnp.asarray(pe)

        def _layer_norm(x, g, b):
            m = x.mean(-1, keepdims=True)
            v = ((x - m) ** 2).mean(-1, keepdims=True)
            return (x - m) / jnp.sqrt(v + EPS) * g + b

        def _mha(x, in_w, in_b, out_w, out_b):
            B, S, D = x.shape
            dh = D // NHEAD
            qkv = x @ in_w.T + in_b
            q, k, v = jnp.split(qkv, 3, axis=-1)
            sp = lambda t: t.reshape(B, S, NHEAD, dh).transpose(0, 2, 1, 3)
            q, k, v = (sp(q), sp(k), sp(v))
            att = jax.nn.softmax(jnp.einsum('bhqd,bhkd->bhqk', q, k) / jnp.sqrt(jnp.float32(dh)), axis=-1)
            o = jnp.einsum('bhqk,bhkd->bhqd', att, v).transpose(0, 2, 1, 3).reshape(B, S, D)
            return o @ out_w.T + out_b

        def _forward(x, l_in_w, l_in_b, l_out_w, l_out_b, ln1_g, ln1_b, ff_w1, ff_b1, ff_w2, ff_b2, ln2_g, ln2_b, m_in_w, m_in_b, m_out_w, m_out_b):
            B, L, D = x.shape
            amp = jnp.abs(jnp.fft.rfft(x, axis=1))
            feat = jax.lax.stop_gradient(jnp.concatenate([x[:, -1:, :], amp], axis=1))
            src = feat + _pos_encoding(feat.shape[1], D)[None]
            a = _mha(src, l_in_w, l_in_b, l_out_w, l_out_b)
            src = _layer_norm(src + a, ln1_g, ln1_b)
            ff = jax.nn.relu(src @ ff_w1.T + ff_b1) @ ff_w2.T + ff_b2
            src = _layer_norm(src + ff, ln2_g, ln2_b)
            out = _mha(src, m_in_w, m_in_b, m_out_w, m_out_b)
            tau = jnp.clip(jax.nn.softplus(out[:, -1:, :]) / DIV_BASE, 0.01, 1.0)
            Lout = L - KSIZE + 1
            idx = jnp.arange(Lout)[:, None] + jnp.arange(KSIZE)[None, :]
            xw = x[:, idx, :]
            seq = jnp.arange(KSIZE - 1, -1, -1, dtype=x.dtype)
            powers = tau[:, 0, :, None] ** seq
            w = powers / powers.sum(-1, keepdims=True)
            return jnp.einsum('bdk,blkd->bld', w, xw)
        return _forward(x, l_in_w, l_in_b, l_out_w, l_out_b, ln1_g, ln1_b, ff_w1, ff_b1, ff_w2, ff_b2, ln2_g, ln2_b, m_in_w, m_in_b, m_out_w, m_out_b)

    def _L0_attn_ref(X, W_Q, W_K, W_V):
        import jax, jax.numpy as jnp
        import numpy as np
        GAMMA = 0.96875
        ROPE_THETA = 10000.0

        def _rope(x):
            B, S, d = x.shape
            inv_freq = 1.0 / ROPE_THETA ** (jnp.arange(0, d, 2, dtype=jnp.float32) / d)
            angles = jnp.arange(S, dtype=jnp.float32)[:, None] * inv_freq[None, :]
            cos = jnp.cos(angles).astype(x.dtype)
            sin = jnp.sin(angles).astype(x.dtype)
            xs = x.reshape(B, S, d // 2, 2)
            x0, x1 = (xs[..., 0], xs[..., 1])
            out = jnp.stack([x0 * cos - x1 * sin, x1 * cos + x0 * sin], axis=-1)
            return out.reshape(B, S, d)

        def _decay_mask(S, dtype):
            n = jnp.arange(S)[:, None]
            m = jnp.arange(S)[None, :]
            diff = n - m
            D = jnp.exp(jnp.maximum(diff, 0).astype(jnp.float32) * np.log(GAMMA))
            return jnp.where(diff >= 0, D, 0.0).astype(dtype)
        B, S, _ = X.shape
        D = _decay_mask(S, X.dtype)
        Q = _rope(X @ W_Q)
        K = _rope(X @ W_K)
        V = X @ W_V
        ret = jnp.einsum('bqd,bkd->bqk', Q, K) * D[None]
        return ret @ V

    def _L0_ffn_ref(x, Wq_pk, pk_keys, Wq, keys_table, values_table, Wo):
        import jax, jax.numpy as jnp
        import numpy as np
        DIM = 64
        HEADS = 8
        NUM_KEYS = 64
        NUM_KV = NUM_KEYS ** 2
        PK_TOPK = 16
        FINAL_TOPK = 16
        DIM_KEY = DIM // 2
        P = 2

        def _pk(x, Wq_pk, pk_keys):
            b, n, _ = x.shape
            q = (x @ Wq_pk).reshape(b, n, P, HEADS, DIM_KEY).transpose(2, 0, 1, 3, 4)
            sim = jnp.einsum('pbnhd,pkhd->pbnhk', q, pk_keys)
            scores, idx = jax.lax.top_k(sim, PK_TOPK)
            idx0 = idx[0]
            idx1 = idx[1] * NUM_KEYS
            index = (idx0[..., :, None] + idx1[..., None, :]).reshape(b, n, HEADS, PK_TOPK * PK_TOPK)
            score = (scores[0][..., :, None] + scores[1][..., None, :]).reshape(b, n, HEADS, PK_TOPK * PK_TOPK)
            final_scores, pk_idx = jax.lax.top_k(score, FINAL_TOPK)
            final_indices = jnp.take_along_axis(index, pk_idx, axis=-1)
            final_scores = jax.nn.softmax(final_scores, axis=-1)
            return (final_scores, final_indices)
        b, n, d = x.shape
        q = (x @ Wq).reshape(b, n, HEADS, DIM) * DIM ** (-0.5)
        kv_scores, indices = _pk(x, Wq_pk, pk_keys)
        offsets = jnp.arange(HEADS, dtype=indices.dtype) * NUM_KV
        ind = indices + offsets[None, None, :, None]
        k = jnp.einsum('bnhk,bnhkd->bnhd', kv_scores, keys_table[ind])
        v = jnp.einsum('bnhk,bnhkd->bnhd', kv_scores, values_table[ind])
        sim = jnp.einsum('bihd,bjhd->bhij', q, k)
        neg = -jnp.finfo(sim.dtype).max
        causal = jnp.tril(jnp.ones((n, n), dtype=bool))
        sim = jnp.where(causal, sim, neg)
        attn = jax.nn.softmax(sim, axis=-1)
        out = jnp.einsum('bhij,bjhd->bhid', attn, v)
        out = out.transpose(0, 2, 1, 3).reshape(b, n, HEADS * DIM)
        return out @ Wo
    h = _L0_tok_ref(x, L0_tok_l_in_w, L0_tok_l_in_b, L0_tok_l_out_w, L0_tok_l_out_b, L0_tok_ln1_g, L0_tok_ln1_b, L0_tok_ff_w1, L0_tok_ff_b1, L0_tok_ff_w2, L0_tok_ff_b2, L0_tok_ln2_g, L0_tok_ln2_b, L0_tok_m_in_w, L0_tok_m_in_b, L0_tok_m_out_w, L0_tok_m_out_b)
    h = h + _L0_attn_ref(_layernorm(h, axis=-1), L0_attn_W_Q, L0_attn_W_K, L0_attn_W_V)
    h = h + _L0_ffn_ref(_layernorm(h, axis=-1), L0_ffn_Wq_pk, L0_ffn_pk_keys, L0_ffn_Wq, L0_ffn_keys_table, L0_ffn_values_table, L0_ffn_Wo)
    return h

_drawn_inputs = setup_inputs


def setup_inputs(seed=0):
    import zlib

    import numpy as np

    out = dict(_drawn_inputs(seed))
    spreads = {'L0_tok_l_in_b': (0.0, 2.0),
     'L0_tok_l_out_b': (0.0, 2.0),
     'L0_tok_ln1_g': (1.0, 0.6),
     'L0_tok_ln1_b': (0.0, 0.8),
     'L0_tok_ff_b1': (0.0, 0.8),
     'L0_tok_ff_b2': (0.0, 0.8),
     'L0_tok_ln2_g': (1.0, 0.6),
     'L0_tok_ln2_b': (0.0, 0.8),
     'L0_tok_m_in_b': (0.0, 0.8),
     'L0_tok_m_out_b': (0.0, 0.8)}
    factors = {'L0_tok_l_in_w': 8.0,
     'L0_tok_l_out_w': 8.0,
     'L0_tok_ff_w1': 8.0,
     'L0_tok_ff_w2': 8.0,
     'L0_tok_m_in_w': 8.0,
     'L0_tok_m_out_w': 8.0,
     'L0_ffn_Wq_pk': 8.0,
     'L0_ffn_pk_keys': 8.0,
     'L0_ffn_Wq': 64.0,
     'L0_ffn_keys_table': 64.0,
     'L0_ffn_values_table': 8.0,
     'L0_ffn_Wo': 8.0}
    for name, (base, spread) in spreads.items():
        noise = np.random.default_rng([zlib.crc32(name.encode()), seed]).standard_normal(out[name].shape)
        drawn = base * np.exp(spread * noise) if base else spread * noise
        out[name] = jnp.asarray(drawn.astype(out[name].dtype))
    for name, factor in factors.items():
        out[name] = (out[name] * factor).astype(out[name].dtype)
    return out
```

```python
from contextlib import ExitStack

import concourse.bass as bass
from concourse import mybir
import numpy as np

ALU = mybir.AluOpType
ACT = mybir.ActivationFunctionType
AX = mybir.AxisListType
F32 = mybir.dt.float32
F16 = mybir.dt.float16
BF16 = mybir.dt.bfloat16

B, L, D = 8, 375, 64
NPAIR = B // 2
KSIZE = 32
LOUT = L - KSIZE + 1
NF = L // 2 + 1
S = NF + 1
XCH = 3
XROWS = L // XCH
H = 8
DH = D // H
QT = ((0, 95), (95, 94))
EPS = 1e-5
TT = ((0, 128), (128, 128), (256, 88))
NT = len(TT)
DFF = 4 * D
NKEY = 64
TOPK = 16
DKEY = 32
NCH = NKEY * NKEY // 128
NCAND = 100
NEG = -3.0e38
FAR = -30000.0
DELTA = 1.5e-6

CONST = {}
_at = 0
for _n, _w in (("dft", XCH * 2 * NF), ("pe", S), ("eye", 128), ("mean", 128), ("head", H), ("rot", 128),
               ("cos", LOUT), ("sin", LOUT), ("decay", LOUT), ("causal", 128), ("sel", 2 * 8 * 128)):
    CONST[_n] = (_at, _at + _w)
    _at += _w
NCONST = _at
WT = {}
_at = 0
for _n, _w in (("q1", 128), ("k1", 128), ("v1", 128), ("o1", 128), ("q2", 128), ("k2", 128), ("v2", 128),
               ("o2", 128), ("f1", DFF), ("f2", 2 * D), ("rq", 128), ("rk", 128), ("rv", 128)):
    WT[_n] = (_at, _at + _w)
    _at += _w
NWT = _at
BIAS = {n: i for i, n in enumerate(("bq1", "bk1", "bv1", "bo1", "g1", "b1", "fb1a", "fb1b", "fb2", "g2", "b2",
                                    "bq2", "bk2", "bv2", "bo2"))}
NBIAS = len(BIAS)


def audio_tower(nc, consts, xrows, xcols, weights, biases, pkw, wq, wo, tables, out):
    with ExitStack() as ctx:
        def sb(name, shape, dt=F32):
            return ctx.enter_context(nc.sbuf_tensor(name, shape, dt))

        ps = ctx.enter_context(nc.psum_tensor("ps", [128, 8, 512], F32))
        hT = sb("hT", [128, NPAIR, LOUT])
        cst = sb("cst", [128, NCONST])
        wts = sb("wts", [128, NWT])
        bia = sb("bia", [128, NBIAS])
        epst = sb("epst", [128, 1])
        x2T = sb("x2T", [128, NPAIR, LOUT])

        def const(name):
            return cst[:, CONST[name][0]:CONST[name][1]]

        def weight(name):
            return wts[:, WT[name][0]:WT[name][1]]

        def bias(name):
            return bia[:, BIAS[name]:BIAS[name] + 1]

        token_mixer(nc, ps, hT, const, weight, bias, epst, cst, wts, bia, consts, xrows, xcols, weights, biases)
        retention(nc, ps, hT, x2T, epst, const, weight)
        product_key_attention(nc, ps, hT, x2T, const, pkw, wq, wo, tables, out)


def token_mixer(nc, ps, hT, const, weight, bias, epst, cst, wts, bia, consts, xrows, xcols, weights, biases):
    with ExitStack() as ctx:
        def sb(name, shape, dt=F32):
            return ctx.enter_context(nc.sbuf_tensor(name, shape, dt))

        def sem(name):
            return ctx.enter_context(nc.semaphore(name))

        xr = sb("xr", [XROWS, XCH, B * D])
        xT = sb("xT", [128, NPAIR, L])
        sq = sb("sq", [128, NPAIR, 2 * NF])
        amp = sb("amp", [128, NPAIR, NF])
        src = sb("src", [128, NPAIR, S])
        qT = sb("qT", [128, NPAIR, S])
        kT = sb("kT", [128, NPAIR, S])
        vt = sb("vt", [95, 2, NPAIR * 128])
        qz = sb("qz", [128, H, S])
        kp = sb("kp", [128, S])
        negmax = sb("negmax", [95, 2, 4])
        ebias = sb("ebias", [95, 2, 4])
        P = sb("P", [95, 2, 4, S])
        Z = sb("Z", [95, 2, 4])
        rz = sb("rz", [95, 2, 4])
        PT = sb("PT", [95, 2, 2, 4 * 95])
        On = sb("On", [95, 128])
        oT = sb("oT", [128, NPAIR, S])
        x1 = sb("x1", [128, NPAIR, S])
        cen = sb("cen", [128, NPAIR, S])
        sqr = sb("sqr", [128, NPAIR, S])
        rstd = sb("rstd", [128, NPAIR, S])
        hff = sb("hff", [128, 2, 2, NPAIR * S])
        q2 = sb("q2", [128, NPAIR])
        q2z = sb("q2z", [128, NPAIR, H])
        s2 = sb("s2", [H, B, S])
        m2 = sb("m2", [H, B])
        z2 = sb("z2", [H, B])
        p2T = sb("p2T", [95, 2, B * H])
        om = sb("om", [128, NPAIR, H])
        o2 = sb("o2", [128, NPAIR])
        sp = sb("sp", [128, 8, NPAIR])
        tau = sb("tau", [128, 5, NPAIR])
        tsum = sb("tsum", [128, 6, NPAIR])
        win = sb("win", [128, 2, NPAIR, L])

        s_const, s_x, s_w = sem("s_const"), sem("s_x"), sem("s_w")
        dft_done, sq_done, power_done, amp_done = sem("dft_done"), sem("sq_done"), sem("power_done"), sem("amp_done")
        last_done, src_done = sem("last_done"), sem("src_done")
        qk_mm, v_mm, q_ready, k_ready, v_ready = sem("qk_mm"), sem("v_mm"), sem("q_ready"), sem("k_ready"), sem("v_ready")
        qz_ready, score_done, max_done, ebias_done = sem("qz_ready"), sem("score_done"), sem("max_done"), sem("ebias_done")
        exp_done, ptr_done, pt_ready, rz_ready = sem("exp_done"), sem("ptr_done"), sem("pt_ready"), sem("rz_ready")
        pv_done, on_ready, ot_mm, oT_ready = sem("pv_done"), sem("on_ready"), sem("ot_mm"), sem("oT_ready")
        proj_mm, res_done = sem("proj_mm"), sem("res_done")
        mean_mm, cen_done, sqr_done, var_mm, rstd_done, norm_done, gain_done, ln_done = (
            sem("mean_mm"), sem("cen_done"), sem("sqr_done"), sem("var_mm"), sem("rstd_done"), sem("norm_done"),
            sem("gain_done"), sem("ln_done"))
        ff1_mm, relu_done, ff2_mm = sem("ff1_mm"), sem("relu_done"), sem("ff2_mm")
        kv2_mm, q2_mm, kv2_ready, q2_ready, q2z_ready = sem("kv2_mm"), sem("q2_mm"), sem("kv2_ready"), sem("q2_ready"), sem("q2z_ready")
        s2_mm, soft2, p2_mm, p2T_ready, o2_mm, om_done, o2_ready, tau_mm = (
            sem("s2_mm"), sem("soft2"), sem("p2_mm"), sem("p2T_ready"), sem("o2_mm"), sem("om_done"), sem("o2_ready"), sem("tau_mm"))
        plus_done, tau_step, win_step, tsum_step, mix_done = sem("plus_done"), sem("tau_step"), sem("win_step"), sem("tsum_step"), sem("mix_done")
        zero_done, kp_ready, std_done = sem("zero_done"), sem("kp_ready"), sem("std_done")

        ahead = (score_done, on_ready, oT_ready, pt_ready, ptr_done, rz_ready, exp_done, ot_mm)
        two = [slice(0, 2), slice(2, 4)]

        def bank2(b, width=S):
            return ps[:, b, 0:2 * width].rearrange("p (a s) -> p a s", a=2)

        with nc.Block() as block:

            @block.sync
            def _(sp_):
                for count in ahead:
                    sp_.sem_inc(count, 1)
                sp_.dma_start(xr[:, :, :].rearrange("p c n -> p (c n)"), xrows.rearrange("p c b d -> p (c b d)")).then_inc(s_x, 16)
                sp_.dma_start(cst[:, :], consts).then_inc(s_const, 16)
                sp_.dma_start(xT[:, :, :], xcols).then_inc(s_x, 16)

            @block.gpsimd
            def _(pool):
                pool.wait_ge(s_x, 32)
                nc.gpsimd.tensor_copy(src[:, :, 0:1], xT[:, :, L - 1:L]).then_inc(last_done, 1)
                pool.wait_ge(k_ready, 2)
                with pool.Fori(0, NPAIR) as p:
                    pool.wait_ge(score_done, 8 * p + 1)
                    nc.gpsimd.tensor_copy(kp[:, :], kT[:, bass.ds(p, 1), :].rearrange("p a s -> p (a s)")).then_inc(kp_ready, 1)

            @block.tensor
            def _(pe):
                def layer_norm(k, x, ready, n_ready, n):
                    for g in range(2):
                        pe.wait_ge(ready, n_ready + g)
                        nc.tensor.matmul(ps[:, g, 0:2 * S], const("mean"), x[:, two[g], :], start=True, stop=True).then_inc(mean_mm, 1)
                    for g in range(2):
                        pe.wait_ge(sqr_done, 2 * k + g + 1)
                        nc.tensor.matmul(ps[:, 2 + g, 0:2 * S], const("mean"), sqr[:, two[g], :], start=True, stop=True).then_inc(var_mm, 1)

                pe.wait_ge(s_x, 32)
                pe.wait_ge(s_const, 16)
                pe.wait_ge(zero_done, 2)
                for p in range(NPAIR):
                    for c in range(XCH):
                        mm = nc.tensor.matmul(ps[:, p, 0:2 * NF], xr[:, c, 128 * p:128 * p + 128],
                                              const("dft")[0:XROWS, 2 * NF * c:2 * NF * (c + 1)],
                                              start=(c == 0), stop=(c == XCH - 1))
                    mm.then_inc(dft_done, 1)
                pe.wait_ge(s_w, 32)
                pe.wait_ge(src_done, 1)
                for g in range(2):
                    nc.tensor.matmul(ps[:, 4 + g, 0:2 * S], weight("q1"), src[:, two[g], :], start=True, stop=True).then_inc(qk_mm, 1)
                for g in range(2):
                    nc.tensor.matmul(ps[:, 6 + g, 0:2 * S], weight("k1"), src[:, two[g], :], start=True, stop=True).then_inc(qk_mm, 1)
                for kt, (k0, kn) in enumerate(QT):
                    for p in range(NPAIR):
                        mm = nc.tensor.matmul(ps[0:kn, kt, 128 * p:128 * p + 128], src[:, p, k0:k0 + kn], weight("v1"),
                                              start=True, stop=True)
                    mm.then_inc(v_mm, 1)
                pe.wait_ge(v_ready, 1)
                with pe.Fori(0, NPAIR) as p:
                    def scores(t):
                        qt, b2, hf = t // 4, (t // 2) % 2, t % 2
                        q0, n = QT[qt]
                        rows = slice(64 * b2, 64 * b2 + 64)
                        for j in range(4):
                            mm = nc.tensor.matmul(ps[0:n, 2 * hf + j // 2, (j % 2) * S:(j % 2 + 1) * S],
                                                  qz[rows, 4 * hf + j, q0:q0 + n], kp[rows, :],
                                                  start=True, stop=True)
                        mm.then_inc(score_done, 1)

                    def values(t):
                        qt, b2, hf = t // 4, (t // 2) % 2, t % 2
                        n = QT[qt][1]
                        pe.wait_ge(pt_ready, 8 * p + t + 2)
                        pe.wait_ge(on_ready, 8 * p + max(t - 1, 0) + 1)
                        if t in (1, 5):
                            pe.wait_ge(oT_ready, 2 * p + t // 4 + 1)
                        for j in range(4):
                            col = DH * j
                            for kt, (k0, kn) in enumerate(QT):
                                mm = nc.tensor.matmul(ps[0:n, 6 + hf, col:col + DH], PT[0:kn, hf, kt, 95 * j:95 * j + n],
                                                      vt[0:kn, kt, bass.ds(p * 128 + 64 * b2 + DH * (4 * hf + j), DH)],
                                                      start=(kt == 0), stop=(kt == 1))
                        mm.then_inc(pv_done, 1)
                        if t % 4 == 3:
                            pe.wait_ge(on_ready, 8 * p + t + 2)
                            nc.tensor.transpose(ps[:, 7, 0:n], On[0:n, :], const("eye")[0:n, 0:n]).then_inc(ot_mm, 1)

                    pe.wait_ge(qz_ready, p + 1)
                    pe.wait_ge(kp_ready, p + 1)
                    scores(0)
                    scores(1)
                    for t in range(8):
                        hf, n = t % 2, QT[t // 4][1]
                        pe.wait_ge(exp_done, 8 * p + t + 2)
                        if t + 2 < 8:
                            scores(t + 2)
                        pe.wait_ge(pt_ready, 8 * p + t + 1)
                        for j in range(4):
                            for kt, (k0, kn) in enumerate(QT):
                                mm = nc.tensor.transpose(ps[0:kn, 4 + kt, 95 * j:95 * j + n],
                                                         P[0:n, hf, j, k0:k0 + kn], const("eye")[0:n, 0:n])
                        mm.then_inc(ptr_done, 1)
                        if t >= 1:
                            values(t - 1)
                    values(7)
                pe.wait_ge(oT_ready, 2 * NPAIR + 1)
                for g in range(2):
                    nc.tensor.matmul(ps[:, 4 + g, 0:2 * S], weight("o1"), oT[:, two[g], :], start=True, stop=True).then_inc(proj_mm, 1)
                layer_norm(0, x1, res_done, 1, 2)
                for b2 in range(2):
                    for hf in range(2):
                        for g in range(2):
                            if b2 == 0 and hf == 0:
                                pe.wait_ge(ln_done, g + 1)
                            bank = (4 * b2 + 2 * hf + g + 4) % 8
                            nc.tensor.matmul(ps[:, bank, 0:2 * S], weight("f1")[64 * b2:64 * b2 + 64, 128 * hf:128 * hf + 128],
                                             x1[64 * b2:64 * b2 + 64, two[g], :], start=True, stop=True).then_inc(ff1_mm, 1)
                for g in range(2):
                    for b2 in range(2):
                        pe.wait_ge(relu_done, 8)
                        for hf in range(2):
                            mm = nc.tensor.matmul(ps[64 * b2:64 * b2 + 64, 4 + g, 0:2 * S], weight("f2")[:, 64 * hf:64 * hf + 64],
                                                  hff[:, b2, hf, 2 * S * g:2 * S * (g + 1)], start=(hf == 0), stop=(hf == 1))
                        mm.then_inc(ff2_mm, 1)
                layer_norm(1, x1, res_done, 3, 2)
                pe.wait_ge(ln_done, 4)
                for g in range(2):
                    nc.tensor.matmul(ps[:, 4 + g, 0:2 * S], weight("k2"), x1[:, two[g], :], start=True, stop=True).then_inc(kv2_mm, 1)
                for kt, (k0, kn) in enumerate(QT):
                    for p in range(NPAIR):
                        mm = nc.tensor.matmul(ps[0:kn, kt, 128 * p:128 * p + 128], x1[:, p, k0:k0 + kn], weight("v2"),
                                              start=True, stop=True)
                    mm.then_inc(kv2_mm, 1)
                nc.tensor.matmul(ps[:, 6, 0:NPAIR], weight("q2"), x1[:, :, S - 1:S].rearrange("p a s -> p (a s)"), start=True, stop=True).then_inc(q2_mm, 1)
                pe.wait_ge(kv2_ready, 2)
                pe.wait_ge(q2z_ready, 1)
                for b2 in range(2):
                    for p in range(NPAIR):
                        rows = slice(64 * b2, 64 * b2 + 64)
                        mm = nc.tensor.matmul(ps[0:H, [4, 5, 2, 3][2 * b2 + p // 2], (p % 2) * S:(p % 2 + 1) * S],
                                              q2z[rows, p, :], kT[rows, p, :], start=True, stop=True)
                        if p % 2 == 1:
                            mm.then_inc(s2_mm, 1)
                pe.wait_ge(soft2, 6)
                for kt, (k0, kn) in enumerate(QT):
                    for b in range(B):
                        mm = nc.tensor.transpose(ps[0:kn, 6 + kt, H * b:H * b + H], s2[:, b, k0:k0 + kn], const("eye")[0:H, 0:H])
                mm.then_inc(p2_mm, 1)
                pe.wait_ge(p2T_ready, 2)
                pe.wait_ge(kv2_ready, 4)
                for b in range(B):
                    p, b2 = b // 2, b % 2
                    for kt, (k0, kn) in enumerate(QT):
                        mm = nc.tensor.matmul(ps[64 * b2:64 * b2 + 64, b2, H * p:H * p + H],
                                              vt[0:kn, kt, 128 * p + 64 * b2:128 * p + 64 * b2 + 64],
                                              p2T[0:kn, kt, H * (4 * b2 + p):H * (4 * b2 + p) + H], start=(kt == 0), stop=(kt == 1))
                mm.then_inc(o2_mm, 1)
                pe.wait_ge(o2_ready, 2)
                nc.tensor.matmul(ps[:, 2, 0:NPAIR], weight("o2"), o2[:, :], start=True, stop=True).then_inc(tau_mm, 1)

            @block.scalar
            def _(act):
                def deviations(k):
                    for g in range(2):
                        act.wait_ge(cen_done, 2 * k + g + 1)
                        nc.scalar.activation(sqr[:, two[g], :], cen[:, two[g], :], ACT.Square).then_inc(sqr_done, 1)
                    for g in range(2):
                        act.wait_ge(var_mm, 2 * k + g + 1)
                        nc.scalar.activation(rstd[:, two[g], :], bank2(2 + g), ACT.Sqrt, bias=epst[:, :]).then_inc(std_done, 1)

                act.dma_start(wts[:, :], weights).then_inc(s_w, 16)
                act.dma_start(bia[:, :], biases).then_inc(s_w, 16)
                for p in range(NPAIR):
                    act.wait_ge(dft_done, p + 1)
                    nc.scalar.activation(sq[:, p, :], ps[:, p, 0:2 * NF], ACT.Square).then_inc(sq_done, 1)
                act.wait_ge(power_done, NPAIR)
                nc.scalar.activation(src[:, :, 1:S], amp[:, :, :], ACT.Sqrt).then_inc(amp_done, 1)
                act.wait_ge(s_w, 32)
                for g in range(2):
                    act.wait_ge(qk_mm, g + 1)
                    nc.scalar.activation(qT[:, two[g], :], bank2(4 + g), ACT.Identity, bias=bias("bq1")).then_inc(q_ready, 1)
                act.wait_ge(v_mm, 2)
                nc.scalar.activation(vt[0:95, :, :], ps[0:95, 0:2, :], ACT.Copy).then_inc(v_ready, 1)
                with act.Fori(0, NPAIR) as p:
                    for t in range(8):
                        qt, b2, hf = t // 4, (t // 2) % 2, t % 2
                        n = QT[qt][1]
                        act.wait_ge(ebias_done, 8 * p + t + 1)
                        act.wait_ge(ptr_done, 8 * p + max(t - 1, 0) + 1)
                        act.wait_ge(rz_ready, 8 * p + max(t - 1, 0) + 1)
                        for j in range(4):
                            a = nc.scalar.activation(P[0:n, hf, j, :], ps[0:n, 2 * hf + j // 2, (j % 2) * S:(j % 2 + 1) * S],
                                                     ACT.Exp, bias=ebias[0:n, hf, j:j + 1], scale=DH ** -0.5,
                                                     accum_out=Z[0:n, hf, j:j + 1])
                        a.then_inc(exp_done, 1)
                        if t in (5, 7):
                            qq = (t - 5) // 2
                            q0, m = QT[qq]
                            act.wait_ge(ot_mm, 2 * p + qq + 2)
                            nc.scalar.activation(oT[:, bass.ds(p, 1), q0:q0 + m].rearrange("p a s -> p (a s)"),
                                                 ps[:, 7, 0:m], ACT.Identity, bias=bias("bv1")).then_inc(oT_ready, 1)
                act.wait_ge(zero_done, 2)
                deviations(0)
                for k in range(8):
                    b2, hf, g = k // 4, (k // 2) % 2, k % 2
                    act.wait_ge(ff1_mm, k + 1)
                    nc.scalar.activation(hff[:, b2, hf, 2 * S * g:2 * S * (g + 1)], ps[:, (k + 4) % 8, 0:2 * S], ACT.Relu,
                                         bias=bias(("fb1a", "fb1b")[hf])).then_inc(relu_done, 1)
                deviations(1)
                for g in range(2):
                    act.wait_ge(kv2_mm, g + 1)
                    nc.scalar.activation(kT[:, two[g], :], bank2(4 + g), ACT.Identity, bias=bias("bk2")).then_inc(kv2_ready, 1)
                act.wait_ge(kv2_mm, 4)
                for kt in range(2):
                    nc.scalar.activation(vt[0:QT[kt][1], kt, :], ps[0:QT[kt][1], kt, :], ACT.Copy).then_inc(kv2_ready, 1)
                act.wait_ge(soft2, 2)
                nc.scalar.activation(s2[:, :, :], s2[:, :, :], ACT.Exp, scale=DH ** -0.5).then_inc(soft2, 1)
                act.wait_ge(plus_done, 3)
                nc.scalar.activation(sp[:, 3, :], sp[:, 2, :], ACT.Exp, scale=-1.0).then_inc(plus_done, 1)
                act.wait_ge(plus_done, 4)
                nc.scalar.activation(sp[:, 4, :], sp[:, 3, :], ACT.Ln, bias=1.0).then_inc(plus_done, 1)

            @block.vector
            def _(dve):
                V = nc.vector

                def layer_norm(k, gain, shift):
                    for g in range(2):
                        dve.wait_ge(mean_mm, 2 * k + g + 1)
                        V.tensor_tensor(cen[:, two[g], :], x1[:, two[g], :], bank2(g), ALU.subtract).then_inc(cen_done, 1)
                    for g in range(2):
                        dve.wait_ge(std_done, 2 * k + g + 1)
                        V.reciprocal(rstd[:, two[g], :], rstd[:, two[g], :]).then_inc(rstd_done, 1)
                        dve.wait_ge(rstd_done, 2 * k + g + 1)
                        V.scalar_tensor_tensor(sqr[:, two[g], :], cen[:, two[g], :], gain, rstd[:, two[g], :], ALU.mult, ALU.mult).then_inc(norm_done, 1)
                        dve.wait_ge(norm_done, 2 * k + g + 1)
                        V.tensor_scalar(x1[:, two[g], :], sqr[:, two[g], :], shift, None, ALU.add).then_inc(ln_done, 1)

                V.memset(epst[:, :], EPS).then_inc(zero_done, 1)
                V.memset(ps[:, :, :], 0.0).then_inc(zero_done, 1)
                for p in range(NPAIR):
                    dve.wait_ge(sq_done, p + 1)
                    V.tensor_tensor(amp[:, p, :], sq[:, p, 0:NF], sq[:, p, NF:2 * NF], ALU.add).then_inc(power_done, 1)
                dve.wait_ge(amp_done, 1)
                dve.wait_ge(last_done, 1)
                dve.wait_ge(s_const, 16)
                V.tensor_tensor(src[:, :, :], src[:, :, :], const("pe")[:, None, :].to_broadcast([128, NPAIR, S]), ALU.add).then_inc(src_done, 1)
                dve.wait_ge(s_w, 32)
                for g in range(2):
                    dve.wait_ge(qk_mm, 3 + g)
                    V.tensor_scalar(kT[:, two[g], :], bank2(6 + g), bias("bk1"), None, ALU.add).then_inc(k_ready, 1)
                dve.wait_ge(q_ready, 2)
                with dve.Fori(0, NPAIR) as p:
                    dve.wait_ge(score_done, 8 * p + 1)
                    V.tensor_tensor(qz[:, :, :], qT[:, bass.ds(p, 1), :].to_broadcast([128, H, S]),
                                    const("head")[:, :, None].to_broadcast([128, H, S]), ALU.mult).then_inc(qz_ready, 1)

                    def normalise(t):
                        qt, b2, hf = t // 4, (t // 2) % 2, t % 2
                        n = QT[qt][1]
                        dve.wait_ge(pv_done, 8 * p + t + 1)
                        if t % 4 == 0:
                            dve.wait_ge(ot_mm, 2 * p + t // 4 + 1)
                        V.tensor_tensor(On[0:n, 64 * b2 + 32 * hf:64 * b2 + 32 * hf + 32].rearrange("p (h d) -> p h d", h=4),
                                        ps[0:n, 6 + hf, 0:32].rearrange("p (h d) -> p h d", h=4),
                                        rz[0:n, hf, :, None].to_broadcast([n, 4, DH]), ALU.mult).then_inc(on_ready, 1)

                    def spread(t):
                        n = QT[t // 4][1]
                        hf = t % 2
                        dve.wait_ge(exp_done, 8 * p + t + 2)
                        V.reciprocal(rz[0:n, hf, :], Z[0:n, hf, :]).then_inc(rz_ready, 1)
                        dve.wait_ge(ptr_done, 8 * p + t + 2)
                        V.tensor_copy(PT[:, hf, :, :], ps[0:95, 4:6, 0:380]).then_inc(pt_ready, 1)

                    for t in range(8):
                        hf, n = t % 2, QT[t // 4][1]
                        dve.wait_ge(score_done, 8 * p + t + 2)
                        V.tensor_reduce(negmax[0:n, hf, :].rearrange("p (b h) -> p b h", b=2),
                                        ps[0:n, 2 * hf:2 * hf + 2, 0:2 * S].rearrange("p b (h k) -> p b h k", h=2),
                                        AX.X, ALU.max, negate=True).then_inc(max_done, 1)
                        dve.wait_ge(max_done, 8 * p + t + 1)
                        dve.wait_ge(exp_done, 8 * p + max(t - 1, 0) + 1)
                        V.tensor_scalar(ebias[0:n, hf, :], negmax[0:n, hf, :], DH ** -0.5, None, ALU.mult).then_inc(ebias_done, 1)
                        if t >= 2:
                            normalise(t - 2)
                        if t >= 1:
                            spread(t - 1)
                    normalise(6)
                    spread(7)
                    normalise(7)
                for g in range(2):
                    dve.wait_ge(proj_mm, g + 1)
                    V.scalar_tensor_tensor(x1[:, two[g], :], bank2(4 + g), bias("bo1"), src[:, two[g], :], ALU.add, ALU.add).then_inc(res_done, 1)
                layer_norm(0, bias("g1"), bias("b1"))
                for g in range(2):
                    dve.wait_ge(ff2_mm, 2 * g + 2)
                    V.scalar_tensor_tensor(x1[:, two[g], :], bank2(4 + g), bias("fb2"), x1[:, two[g], :], ALU.add, ALU.add).then_inc(res_done, 1)
                layer_norm(1, bias("g2"), bias("b2"))
                dve.wait_ge(q2_mm, 1)
                V.tensor_scalar(q2[:, :], ps[:, 6, 0:NPAIR], bias("bq2"), None, ALU.add).then_inc(q2_ready, 1)
                dve.wait_ge(q2_ready, 1)
                V.tensor_tensor(q2z[:, :, :], q2[:, :, None].to_broadcast([128, NPAIR, H]),
                                const("head")[:, None, :].to_broadcast([128, NPAIR, H]), ALU.mult).then_inc(q2z_ready, 1)
                for k, bank in enumerate((4, 5, 2, 3)):
                    dve.wait_ge(s2_mm, k + 1)
                    cp = V.tensor_copy(s2[:, 2 * k:2 * k + 2, :], ps[0:H, bank, 0:2 * S].rearrange("p (a s) -> p a s", a=2))
                cp.then_inc(om_done, 1)
                dve.wait_ge(om_done, 1)
                V.tensor_reduce(m2[:, :], s2[:, :, :], AX.X, ALU.max).then_inc(soft2, 1)
                dve.wait_ge(soft2, 1)
                V.tensor_tensor(s2[:, :, :], s2[:, :, :], m2[:, :, None].to_broadcast([H, B, S]), ALU.subtract).then_inc(soft2, 1)
                dve.wait_ge(soft2, 3)
                V.tensor_reduce(z2[:, :], s2[:, :, :], AX.X, ALU.add).then_inc(soft2, 1)
                dve.wait_ge(soft2, 4)
                V.reciprocal(m2[:, :], z2[:, :]).then_inc(soft2, 1)
                dve.wait_ge(soft2, 5)
                V.tensor_tensor(s2[:, :, :], s2[:, :, :], m2[:, :, None].to_broadcast([H, B, S]), ALU.mult).then_inc(soft2, 1)
                dve.wait_ge(p2_mm, 1)
                for kt, (k0, kn) in enumerate(QT):
                    V.tensor_copy(p2T[0:kn, kt, :], ps[0:kn, 6 + kt, 0:B * H]).then_inc(p2T_ready, 1)
                dve.wait_ge(o2_mm, 1)
                for b2 in range(2):
                    rows = slice(64 * b2, 64 * b2 + 64)
                    V.tensor_tensor(om[rows, :, :], ps[rows, b2, 0:NPAIR * H].rearrange("p (a h) -> p a h", a=NPAIR),
                                    const("head")[rows, None, :].to_broadcast([64, NPAIR, H]), ALU.mult).then_inc(om_done, 1)
                dve.wait_ge(om_done, 3)
                V.tensor_reduce(o2[:, :], om[:, :, :], AX.X, ALU.add).then_inc(o2_ready, 1)
                dve.wait_ge(o2_ready, 1)
                V.tensor_scalar(o2[:, :], o2[:, :], bias("bv2"), None, ALU.add).then_inc(o2_ready, 1)
                dve.wait_ge(tau_mm, 1)
                V.tensor_scalar(sp[:, 0, :], ps[:, 2, 0:NPAIR], bias("bo2"), None, ALU.add).then_inc(plus_done, 1)
                dve.wait_ge(plus_done, 1)
                V.tensor_scalar(sp[:, 1, :], sp[:, 0, :], 0.0, None, ALU.max).then_inc(plus_done, 1)
                dve.wait_ge(plus_done, 2)
                V.scalar_tensor_tensor(sp[:, 2, :], sp[:, 1, :], 2.0, sp[:, 0, :], ALU.mult, ALU.subtract).then_inc(plus_done, 1)
                dve.wait_ge(plus_done, 5)
                V.tensor_tensor(sp[:, 5, :], sp[:, 4, :], sp[:, 1, :], ALU.add).then_inc(plus_done, 1)
                dve.wait_ge(plus_done, 6)
                V.tensor_scalar(sp[:, 6, :], sp[:, 5, :], 0.1, 0.01, ALU.mult, ALU.max).then_inc(plus_done, 1)
                dve.wait_ge(plus_done, 7)
                V.tensor_scalar(tau[:, 0, :], sp[:, 6, :], 1.0, None, ALU.min).then_inc(tau_step, 1)
                for k in range(5):
                    n = 1 << k
                    dve.wait_ge(tau_step, k + 1)
                    if k < 4:
                        V.tensor_tensor(tau[:, k + 1, :], tau[:, k, :], tau[:, k, :], ALU.mult).then_inc(tau_step, 1)
                    if k == 0:
                        V.tensor_scalar(tsum[:, 0, :], tau[:, 0, :], 1.0, None, ALU.add).then_inc(tsum_step, 1)
                    else:
                        dve.wait_ge(tsum_step, k)
                        V.scalar_tensor_tensor(tsum[:, k, :], tau[:, k, :], 1.0, tsum[:, k - 1, :], ALU.add, ALU.mult).then_inc(tsum_step, 1)
                    width = L - 2 * n + 1
                    frm = xT if k == 0 else win[:, (k - 1) % 2]
                    if k > 0:
                        dve.wait_ge(win_step, NPAIR * k)
                    for p in range(NPAIR):
                        V.scalar_tensor_tensor(win[:, k % 2, p, 0:width], frm[:, p, 0:width], tau[:, k, p:p + 1],
                                               frm[:, p, n:n + width], ALU.mult, ALU.add).then_inc(win_step, 1)
                dve.wait_ge(tsum_step, 5)
                V.reciprocal(tsum[:, 5, :], tsum[:, 4, :]).then_inc(tsum_step, 1)
                dve.wait_ge(tsum_step, 6)
                dve.wait_ge(win_step, 5 * NPAIR)
                for p in range(NPAIR):
                    V.tensor_scalar(hT[:, p, :], win[:, 0, p, 0:LOUT], tsum[:, 5, p:p + 1], None, ALU.mult).then_inc(mix_done, 1)


def retention(nc, ps, hT, x2T, epst, const, weight):
    with ExitStack() as ctx:
        def sb(name, shape, dt=F32):
            return ctx.enter_context(nc.sbuf_tensor(name, shape, dt))

        def sem(name):
            return ctx.enter_context(nc.semaphore(name))

        cen = sb("r_cen", [128, NPAIR, LOUT])
        sqr = sb("r_sqr", [128, NPAIR, LOUT])
        rstd = sb("r_rstd", [128, NPAIR, LOUT])
        raw = sb("r_raw", [128, 2, NPAIR, LOUT])
        rcos = sb("r_cos", [128, NPAIR, LOUT])
        rqk = sb("r_qk", [128, 2, NPAIR, LOUT])
        rv = sb("r_v", [128, NT, NPAIR * 128])
        dec = sb("r_dec", [128, 2, NT, LOUT])

        mean_mm, cen_done, sqr_done, var_mm, std_done, rstd_done, ln_done = (
            sem("r_mean_mm"), sem("r_cen"), sem("r_sqr"), sem("r_var_mm"), sem("r_std"), sem("r_rstd"), sem("r_ln"))
        raw_mm, raw_ready, rot_mm, cos_done, sin_done, rot_ready = (
            sem("r_raw_mm"), sem("r_raw_ready"), sem("r_rot_mm"), sem("r_cos"), sem("r_sin"), sem("r_rot"))
        v_mm, v_ready, score_mm, dec_ready, ret_mm, ret_done = (
            sem("r_v_mm"), sem("r_v_ready"), sem("r_score_mm"), sem("r_dec"), sem("r_ret_mm"), sem("r_ret"))

        def flat(a):
            return a.rearrange("p a s -> p (a s)")

        with nc.Block() as block:

            @block.tensor
            def _(pe):
                def layer_norm(k, ready, first):
                    for p in range(NPAIR):
                        if ready is not None:
                            pe.wait_ge(ready, first + 2 * p)
                        nc.tensor.matmul(ps[:, p, 0:LOUT], const("mean"), hT[:, p, :], start=True, stop=True).then_inc(mean_mm, 1)
                    for p in range(NPAIR):
                        pe.wait_ge(sqr_done, NPAIR * k + p + 1)
                        nc.tensor.matmul(ps[:, 4 + p, 0:LOUT], const("mean"), sqr[:, p, :], start=True, stop=True).then_inc(var_mm, 1)

                layer_norm(0, None, 0)
                for w in range(2):
                    for p in range(NPAIR):
                        pe.wait_ge(ln_done, p + 1)
                        if w == 1:
                            pe.wait_ge(std_done, NPAIR)
                        nc.tensor.matmul(ps[:, 4 * w + p, 0:LOUT], weight(("rq", "rk")[w]), x2T[:, p, :],
                                         start=True, stop=True).then_inc(raw_mm, 1)
                for w in range(2):
                    for p in range(NPAIR):
                        pe.wait_ge(raw_ready, NPAIR * w + p + 1)
                        nc.tensor.matmul(ps[:, 4 * w + p, 0:LOUT], const("rot"), raw[:, w, p, :],
                                         start=True, stop=True).then_inc(rot_mm, 1)
                for t, (t0, n) in enumerate(TT):
                    pe.wait_ge(sin_done, t + 1)
                    for p in range(NPAIR):
                        mm = nc.tensor.matmul(ps[0:n, t, 128 * p:128 * p + 128], x2T[:, p, t0:t0 + n], weight("rv"),
                                              start=True, stop=True)
                    mm.then_inc(v_mm, 1)

                def scores(b):
                    p, rows = b // 2, slice(64 * (b % 2), 64 * (b % 2) + 64)
                    pe.wait_ge(rot_ready, NPAIR + p + 1)
                    if b == 0:
                        pe.wait_ge(v_ready, NT)
                        pe.wait_ge(sin_done, 2 * NPAIR)
                    if b >= 2:
                        pe.wait_ge(dec_ready, NT * (b - 1))
                    for t, (t0, n) in enumerate(TT):
                        nc.tensor.matmul(ps[0:n, 3 * (b % 2) + t, 0:LOUT - t0], rqk[rows, 1, p, t0:t0 + n],
                                         rqk[rows, 0, p, t0:LOUT], start=True, stop=True).then_inc(score_mm, 1)

                def mix(b):
                    p, b2 = b // 2, b % 2
                    pe.wait_ge(dec_ready, NT * (b + 1))
                    if b >= 2:
                        pe.wait_ge(ret_done, b - 1)
                    for t, (t0, n) in enumerate(TT):
                        mm = nc.tensor.matmul(ps[64 * b2:64 * b2 + 64, 6 + b2, t0:LOUT],
                                              rv[0:n, t, 128 * p + 64 * b2:128 * p + 64 * b2 + 64],
                                              dec[0:n, b2, t, 0:LOUT - t0], start=(t == 0), stop=(t == NT - 1))
                    mm.then_inc(ret_mm, 1)

                scores(0)
                for b in range(B):
                    if b + 1 < B:
                        scores(b + 1)
                    mix(b)
                layer_norm(1, ret_done, 2)

            @block.scalar
            def _(act):
                def deviations(k):
                    for p in range(NPAIR):
                        act.wait_ge(cen_done, NPAIR * k + p + 1)
                        nc.scalar.activation(sqr[:, p, :], cen[:, p, :], ACT.Square).then_inc(sqr_done, 1)
                    for p in range(NPAIR):
                        act.wait_ge(var_mm, NPAIR * k + p + 1)
                        nc.scalar.activation(rstd[:, p, :], ps[:, 4 + p, 0:LOUT], ACT.Sqrt, bias=epst[:, :]).then_inc(std_done, 1)

                deviations(0)
                for w in range(2):
                    for p in range(NPAIR):
                        act.wait_ge(raw_mm, NPAIR * w + p + 1)
                        nc.scalar.activation(raw[:, w, p, :], ps[:, 4 * w + p, 0:LOUT], ACT.Copy).then_inc(raw_ready, 1)
                for t, (t0, n) in enumerate(TT):
                    act.wait_ge(v_mm, t + 1)
                    nc.scalar.activation(rv[0:n, t, :], ps[0:n, t, :], ACT.Copy).then_inc(v_ready, 1)
                deviations(1)

            @block.gpsimd
            def _(pool):
                for w in range(2):
                    for p in range(NPAIR):
                        pool.wait_ge(raw_ready, NPAIR * w + p + 1)
                        if w == 1:
                            pool.wait_ge(rot_ready, p + 1)
                        nc.gpsimd.tensor_tensor(rcos[:, p, :], raw[:, w, p, :], const("cos"), ALU.mult).then_inc(cos_done, 1)

            @block.vector
            def _(dve):
                V = nc.vector

                def layer_norm(k):
                    for p in range(NPAIR):
                        dve.wait_ge(mean_mm, NPAIR * k + p + 1)
                        V.tensor_tensor(cen[:, p, :], hT[:, p, :], ps[:, p, 0:LOUT], ALU.subtract).then_inc(cen_done, 1)
                    for p in range(NPAIR):
                        dve.wait_ge(std_done, NPAIR * k + p + 1)
                        V.reciprocal(rstd[:, p, :], rstd[:, p, :]).then_inc(rstd_done, 1)
                        dve.wait_ge(rstd_done, NPAIR * k + p + 1)
                        V.tensor_tensor(x2T[:, p, :], cen[:, p, :], rstd[:, p, :], ALU.mult).then_inc(ln_done, 1)

                layer_norm(0)
                for w in range(2):
                    for p in range(NPAIR):
                        dve.wait_ge(rot_mm, NPAIR * w + p + 1)
                        dve.wait_ge(cos_done, NPAIR * w + p + 1)
                        V.tensor_tensor(raw[:, w, p, :], ps[:, 4 * w + p, 0:LOUT], const("sin"), ALU.mult).then_inc(sin_done, 1)
                        dve.wait_ge(sin_done, NPAIR * w + p + 1)
                        V.tensor_tensor(rqk[:, w, p, :], raw[:, w, p, :], rcos[:, p, :], ALU.add).then_inc(rot_ready, 1)

                def decay(b):
                    for t, (t0, n) in enumerate(TT):
                        dve.wait_ge(score_mm, NT * b + t + 1)
                        if b >= 2:
                            dve.wait_ge(ret_mm, b - 1)
                        V.tensor_tensor(dec[0:n, b % 2, t, 0:LOUT - t0], ps[0:n, 3 * (b % 2) + t, 0:LOUT - t0],
                                        const("decay")[0:n, 0:LOUT - t0], ALU.mult).then_inc(dec_ready, 1)

                def add(b):
                    rows = slice(64 * (b % 2), 64 * (b % 2) + 64)
                    dve.wait_ge(ret_mm, b + 1)
                    V.tensor_tensor(hT[rows, b // 2, :], hT[rows, b // 2, :], ps[rows, 6 + b % 2, 0:LOUT], ALU.add).then_inc(ret_done, 1)

                for b in range(B):
                    decay(b)
                    if b >= 1:
                        add(b - 1)
                add(B - 1)
                layer_norm(1)


def product_key_attention(nc, ps, hT, x2T, const, pkw, wq, wo, tables, out):
    with ExitStack() as ctx:
        def sb(name, shape, dt=F32):
            return ctx.enter_context(nc.sbuf_tensor("k_" + name, shape, dt))

        def sem(name):
            return ctx.enter_context(nc.semaphore("k_" + name))

        NDC = NCH // 2
        WINDOW = (0, 2, 3, 1)
        MID0, MID1 = 6, 7

        tab = sb("tab", [128, 2, NCH, 128])
        wqh = sb("wqh", [64, 2, D])
        wos = sb("wos", [64, H, D])
        pkw_sb = sb("pkw_sb", [DKEY, 16, 128])
        wf = sb("wf", [64, H + 1, 2, NKEY])
        sel = sb("sel", [128, 2, 8, 128], F16)
        eye16 = sb("eye16", [128, 128], F16)
        eyeb = sb("eyeb", [128, 128], BF16)
        causb = sb("causb", [128, 128], BF16)
        y = sb("y", [128, B, NT, D])
        xs = sb("xs", [64, 2, LOUT])
        sS = sb("sS", [128, NT, 2, NKEY])
        rp = sb("rp", [128, NT, 2, NKEY])
        top = sb("top", [128, NT, 2, TOPK])
        cand = sb("cand", [128, NT, NCAND])
        rc = sb("rc", [128, NT, NCAND])
        fin = sb("fin", [128, NT, TOPK])
        small = sb("small", [128, 6, NT])
        off = sb("off", [128, NT, 2])
        ecs = sb("ecs", [128, NT, NCAND])
        zs = sb("zs", [128, NT])
        gain = sb("gain", [128, 2, NT])
        aS = sb("aS", [128, NT, 2, 2, 32])
        spl = sb("spl", [128, NT, 5, 2, 32], F16)
        X = sb("X", [128, 2, 4, LOUT], F16)
        E = sb("E", [128, 2, 2, LOUT])
        W = sb("W", [128, 4, 2, LOUT])
        kvs = sb("kvs", [128, LOUT])
        kv = sb("kv", [128, NT, 128])
        kT = sb("kT", [64, LOUT])
        qT = sb("qT", [64, 2, LOUT])
        P = sb("P", [128, NT, LOUT])
        nmax = sb("nmax", [128, NT])
        zz = sb("zz", [128, NT])
        rz = sb("rz", [128, NT])
        PT = sb("PT", [128, NT, LOUT])
        oT = sb("oT", [64, LOUT])

        s_tab = [sem("s_tab0"), sem("s_tab1")]
        s_load, s_out, passed = sem("s_load"), sem("s_out"), sem("passed")
        cast_done, zeroed, wf_mm, wf_ready, y_mm0, y_ready0 = (
            sem("cast_done"), sem("zeroed"), sem("wf_mm"), sem("wf_ready"), sem("y_mm0"), sem("y_ready0"))
        xs_ready, sim_mm, sim_ready, top_step, thr_ready, ecs_ready, z_done, rz_z, gain_ready = (
            sem("xs_ready"), sem("sim_mm"), sem("sim_ready"), sem("top_step"), sem("thr_ready"), sem("ecs_ready"),
            sem("z_done"), sem("rz_z"), sem("gain_ready"))
        a_step, low_step, high_ready, low_ready, x_mm, x_ready = (
            sem("a_step"), sem("low_step"), sem("high_ready"), sem("low_ready"), sem("x_mm"), sem("x_ready"))
        log_mm, e_done, w_done, main_done = sem("log_mm"), sem("e_done"), sem("w_done"), sem("main_done")
        kvs_ready, kvt_mm, kv_ready, kt_mm, kT_ready, q_mm, qT_ready = (
            sem("kvs_ready"), sem("kvt_mm"), sem("kv_ready"), sem("kt_mm"), sem("kT_ready"), sem("q_mm"), sem("qT_ready"))
        s_mm, nmax_done, p_done, rz_ready, pn_ready, pt_mm, pt_ready, pt1_ready = (
            sem("s_mm"), sem("nmax_done"), sem("p_done"), sem("prz_ready"), sem("pn_ready"), sem("ppt_mm"),
            sem("ppt_ready"), sem("pt1_ready"))
        o_mm, oT_ready, y_mm, y_done = sem("o_mm"), sem("poT_ready"), sem("y_mm"), sem("y_done")
        AHEAD = {q_mm: 1, gain_ready: 1, main_done: 4, kvs_ready: 1, y_done: 1}

        def ahead(s):
            return AHEAD[s]

        def wait_alone(eng, s, value):
            eng.wait_ge(s, value)
            eng.sem_inc(passed, 1)

        def rounds(eng, body):
            with eng.Fori(0, H // 2) as hh:
                for slot in range(2):
                    body.head(hh, slot)
                    with eng.Fori(0, NPAIR) as pair:
                        for par in range(2):
                            g = hh * 8 + pair + 4 * slot
                            i = hh * 16 + pair * 2 + (8 * slot + par)
                            body.item(i, slot, par, g, pair)

        with nc.Block() as block:

            @block.sync
            def _(sync):
                def load(slot, head):
                    if isinstance(head, int):
                        t, q = tables[head], wq[:, head, :]
                        sync.dma_start(tab[:, slot, :, :], t).then_inc(s_tab[slot], 16)
                        sync.dma_start(wqh[:, slot, :], q).then_inc(s_tab[slot], 16)
                    else:
                        sync.dma_start(tab[:, slot, :, :], tables[bass.ds(head, 1)].rearrange("a p c d -> p (a c) d")).then_inc(s_tab[slot], 16)
                        sync.dma_start(wqh[:, slot, :], wq[:, bass.ds(head, 1), :].rearrange("p a d -> p (a d)")).then_inc(s_tab[slot], 16)

                for s, n in AHEAD.items():
                    sync.sem_inc(s, n)
                sync.dma_start(pkw_sb[:, :, :].rearrange("p a b -> p (a b)"), pkw).then_inc(s_load, 16)
                sync.dma_start(wos[:, :, :], wo).then_inc(s_load, 16)
                load(0, 0)
                load(1, 1)
                with sync.Fori(0, H // 2 - 1) as hh:
                    for slot in range(2):
                        wait_alone(sync, main_done, hh * (16 * NDC) + (8 * NDC * (slot + 1) + ahead(main_done)))
                        wait_alone(sync, q_mm, hh * 16 + (8 * (slot + 1) + ahead(q_mm)))
                        load(slot, hh * 2 + (slot + 2))

            @block.tensor
            def _(pe):
                mm_, tr_ = nc.tensor.matmul, nc.tensor.transpose
                eye = const("eye")

                def similarities(n, par, head):
                    pe.wait_ge(xs_ready, n + 1)
                    for t, (t0, m) in enumerate(TT):
                        rhs = (wf[:, head, :, :] if isinstance(head, int) else wf[:, bass.ds(head, 1), :, :].rearrange("p a b k -> p (a b) k"))
                        mm = mm_(ps[0:m, MID0, 128 * t:128 * t + 128], xs[:, par, t0:t0 + m], rhs, start=True, stop=True)
                    mm.then_inc(sim_mm, 1)

                def turn_scores(n, r):
                    if r == 0:
                        pe.wait_ge(low_ready, n + 1)
                    else:
                        pe.wait_ge(x_ready, 2 * n + 1)
                    bank = ps[:, MID0, :].bitcast(F16)
                    for k in range(2):
                        for t, (t0, m) in enumerate(TT):
                            mm = tr_(bank[:, LOUT * k + t0:LOUT * k + t0 + m],
                                     spl[0:m, t, 2 * r + k:2 * r + k + 2, :, :].rearrange("p b x j -> p (b x j)"), eye16[0:m, 0:m])
                    mm.then_inc(x_mm, 1)

                def log_weights(i, par, d):
                    for k in range(2):
                        c = 2 * d + k
                        mm = mm_(ps[:, 2 * (d % 2) + k, 0:LOUT], sel[:, (c // 8) % 2, c % 8, :], X[:, par, c // 8, :], start=True, stop=True)
                    mm.then_inc(log_mm, 1)

                def table_sum(i, slot, par, d):
                    pe.wait_ge(w_done, i * NDC + (d + 1))
                    for k in range(2):
                        c = 2 * d + k
                        mm = mm_(ps[:, 4 + par, 0:LOUT], tab[:, slot, 8 * WINDOW[c // 8] + c % 8, :], W[:, d % 4, k, :], start=(c == 0), stop=(c == NCH - 1))
                    mm.then_inc(main_done, 1)

                def turn_kv(i):
                    pe.wait_ge(y_done, i + ahead(y_done))
                    pe.wait_ge(kvs_ready, i + (1 + ahead(kvs_ready)))
                    for t, (t0, m) in enumerate(TT):
                        mm = tr_(ps[0:m, MID1, 128 * t:128 * t + 128], kvs[:, t0:t0 + m], eye)
                    mm.then_inc(kvt_mm, 1)

                def turn_keys(i):
                    wait_alone(pe, kv_ready, i + 1)
                    for t, (t0, m) in enumerate(TT):
                        mm = tr_(ps[0:64, MID1, t0:t0 + m], kv[0:m, t, 0:64], eye[0:m, 0:m])
                    mm.then_inc(kt_mm, 1)

                def queries(i, slot, par):
                    wait_alone(pe, kT_ready, i + 1)
                    mm_(ps[0:64, MID1, 0:LOUT], wqh[:, slot, :], xs[:, par, :], start=True, stop=True).then_inc(q_mm, 1)

                def attention_scores(i, pj, last=False):
                    if last:
                        wait_alone(pe, kT_ready, i + 1)
                    else:
                        pe.wait_ge(sim_ready, i + 2)
                        pe.wait_ge(qT_ready, i + 1)
                    for t, (t0, m) in enumerate(TT):
                        keys = t0 + m
                        bank, c0 = ((MID0, 0), (MID0, 128), (MID1, 0))[t]
                        mm_(ps[0:m, bank, c0:c0 + keys], qT[:, pj, t0:t0 + m], kT[:, 0:keys], start=True, stop=False)
                        mm = mm_(ps[0:m, bank, c0 + t0:c0 + keys], eyeb[0:m, 0:m], causb[0:m, 0:m], start=False, stop=True)
                    mm.then_inc(s_mm, 1)

                def turn_probabilities(i):
                    pe.wait_ge(pn_ready, i + 1)
                    for kt, (k0, kn) in enumerate(TT):
                        bank, c0 = ((MID1, 0), (MID0, 0), (MID1, LOUT))[kt]
                        for t, (t0, m) in enumerate(TT):
                            if t >= kt:
                                mm = tr_(ps[0:kn, bank, c0 + t0 - k0:c0 + t0 - k0 + m], P[0:m, t, k0:k0 + kn], eye[0:m, 0:m])
                    mm.then_inc(pt_mm, 1)

                def attention_output(i):
                    pe.wait_ge(pt_ready, i + 1)
                    pe.wait_ge(pt1_ready, i + 1)
                    for kt, (k0, kn) in enumerate(TT):
                        mm = mm_(ps[0:64, MID1, k0:LOUT], kv[0:kn, kt, 64:128], PT[0:kn, kt, 0:LOUT - k0], start=(kt == 0), stop=(kt == NT - 1))
                    mm.then_inc(o_mm, 1)

                def project(i, head):
                    wait_alone(pe, oT_ready, i + 1)
                    rhs = wos[:, head, :] if isinstance(head, int) else wos[:, bass.ds(head, 1), :].rearrange("p a d -> p (a d)")
                    for t, (t0, m) in enumerate(TT):
                        mm = mm_(ps[0:m, MID1, 64 * t:64 * t + 64], oT[:, t0:t0 + m], rhs, start=True, stop=True)
                    mm.then_inc(y_mm, 1)

                pe.wait_ge(s_load, 32)
                for p in range(2):
                    for h in range(H):
                        mm = mm_(ps[0:64, p, 64 * h:64 * h + 64], pkw_sb[:, 8 * p + h, 0:64], pkw_sb[:, 8 * p + h, 64:128], start=True, stop=True)
                    mm.then_inc(wf_mm, 1)
                for t, (t0, m) in enumerate(TT):
                    for p in range(NPAIR):
                        mm = tr_(ps[0:m, 2 + t, 128 * p:128 * p + 128], hT[:, p, t0:t0 + m], eye)
                    mm.then_inc(y_mm0, 1)
                pe.wait_ge(cast_done, 4)
                pe.wait_ge(zeroed, 6)
                pe.wait_ge(wf_ready, 3)
                similarities(0, 0, 0)
                turn_scores(0, 0)
                turn_scores(0, 1)
                pe.wait_ge(y_ready0, NT)
                pe.wait_ge(x_ready, 2)
                log_weights(0, 0, 0)
                log_weights(0, 0, 1)

                class Body:
                    @staticmethod
                    def head(hh, slot):
                        wait_alone(pe, s_tab[slot], hh * 32 + 32)

                    @staticmethod
                    def item(i, slot, par, g, pair):
                        nj = 1 - par
                        pe.wait_ge(kvs_ready, i + ahead(kvs_ready))
                        for d in range(NDC):
                            table_sum(i, slot, par, d)
                            if d + 2 < NDC:
                                log_weights(i, par, d + 2)
                            else:
                                if d == NDC - 2:
                                    pe.wait_ge(x_ready, i * 2 + 3)
                                log_weights(i + 1, nj, d + 2 - NDC)
                            if d == 0:
                                turn_kv(i)
                            if d == 1:
                                similarities(i + 1, nj, (g + par) // 4 if par else g // 4)
                            if d == 2:
                                turn_keys(i)
                            if d == 3:
                                queries(i, slot, par)
                            if d == 5:
                                if par == 0:
                                    pe.wait_ge(x_ready, i * 2 + 2)
                                attention_scores(i, nj)
                            if d == 8:
                                turn_probabilities(i)
                            if d == 10:
                                attention_output(i)
                            if d == 12:
                                turn_scores(i + 1, 0)
                            if d == 13:
                                project(i, g // 4 if par else ((g + 31) // 4) % 8)
                            if d == 14:
                                turn_scores(i + 1, 1)

                rounds(pe, Body)
                n = H * B
                turn_kv(n)
                turn_keys(n)
                attention_scores(n, 1, last=True)
                turn_probabilities(n)
                attention_output(n)
                project(n, H - 1)

            @block.scalar
            def _(act):
                A = nc.scalar.activation

                def copy_similarities(n):
                    act.wait_ge(sim_mm, n + 1)
                    A(sS[:, 0:2, :, :], ps[:, MID0, 0:256], ACT.Copy)
                    A(sS[0:88, 2, :, :], ps[0:88, MID0, 256:384], ACT.Copy).then_inc(sim_ready, 1)

                def candidate_weights(n):
                    act.wait_ge(thr_ready, n * 6 + 6)
                    A(ecs[:, :, :], rc[:, :, :], ACT.Exp)
                    A(small[:, 4, :], small[:, 3, :], ACT.Exp).then_inc(ecs_ready, 1)

                def high_part(n):
                    act.wait_ge(a_step, n * 3 + 3)
                    A(spl[:, :, 0:4, 0, :], aS[:, :, :, :, :].rearrange("p t u a j -> p t (u a) j"), ACT.Copy).then_inc(high_ready, 1)

                def copy_turned(n, par, r):
                    act.wait_ge(x_mm, n * 2 + (r + 1))
                    A(X[:, par, 2 * r:2 * r + 2, :], ps[:, MID0, :].bitcast(F16)[:, 0:2 * LOUT], ACT.Copy).then_inc(x_ready, 1)

                def exponentials(i, d):
                    act.wait_ge(log_mm, i * NDC + (d + 1))
                    A(E[:, d % 2, :, :], ps[:, 2 * (d % 2):2 * (d % 2) + 2, 0:LOUT], ACT.Exp).then_inc(e_done, 1)

                def take_sums(i, pj):
                    act.wait_ge(main_done, i * NDC + ahead(main_done))
                    A(kvs[:, :], ps[:, 4 + pj, 0:LOUT], ACT.Copy).then_inc(kvs_ready, 1)

                def scale_kv(i, pj):
                    act.wait_ge(gain_ready, i + ahead(gain_ready))
                    act.wait_ge(kvt_mm, i + 1)
                    for t, (t0, m) in enumerate(TT):
                        a = A(kv[0:m, t, :], ps[0:m, MID1, 128 * t:128 * t + 128], ACT.Copy, scale=gain[0:m, pj, t:t + 1])
                    a.then_inc(kv_ready, 1)

                def copy_keys(i):
                    act.wait_ge(kt_mm, i + 1)
                    A(kT[:, :], ps[0:64, MID1, 0:LOUT], ACT.Copy).then_inc(kT_ready, 1)

                def copy_queries(i, par):
                    act.wait_ge(q_mm, i + (1 + ahead(q_mm)))
                    A(qT[:, par, :], ps[0:64, MID1, 0:LOUT], ACT.Copy, scale=D ** -0.5).then_inc(qT_ready, 1)

                def probabilities(i):
                    act.wait_ge(nmax_done, i * 3 + 3)
                    for t, (t0, m) in enumerate(TT):
                        bank, c0 = ((MID0, 0), (MID0, 128), (MID1, 0))[t]
                        a = A(P[0:m, t, 0:t0 + m], ps[0:m, bank, c0:c0 + t0 + m], ACT.Exp, bias=nmax[0:m, t:t + 1],
                              accum_out=zz[0:m, t:t + 1])
                    a.then_inc(p_done, 1)

                def copy_turned_probabilities(i):
                    act.wait_ge(pt_mm, i + 1)
                    A(PT[:, 0, :], ps[:, MID1, 0:LOUT], ACT.Copy)
                    A(PT[0:88, 2, 0:88], ps[0:88, MID1, LOUT:LOUT + 88], ACT.Copy).then_inc(pt_ready, 1)

                def copy_output(i):
                    act.wait_ge(o_mm, i + 1)
                    A(oT[:, :], ps[0:64, MID1, 0:LOUT], ACT.Copy).then_inc(oT_ready, 1)

                for p in range(2):
                    act.wait_ge(wf_mm, p + 1)
                    A(wf[:, 0:H, p, :], ps[0:64, p, :].rearrange("p (h k) -> p h k", h=H), ACT.Copy).then_inc(wf_ready, 1)
                for t, (t0, m) in enumerate(TT):
                    act.wait_ge(y_mm0, t + 1)
                    A(y[0:m, :, t, :], ps[0:m, 2 + t, :].rearrange("p (b d) -> p b d", b=B), ACT.Copy).then_inc(y_ready0, 1)
                act.wait_ge(zeroed, 6)
                copy_similarities(0)
                candidate_weights(0)
                high_part(0)
                copy_turned(0, 0, 0)
                copy_turned(0, 0, 1)

                class Body:
                    @staticmethod
                    def head(hh, slot):
                        pass

                    @staticmethod
                    def item(i, slot, par, g, pair):
                        nj = 1 - par
                        for d in range(NDC):
                            exponentials(i, d)
                            if d == 0:
                                take_sums(i, nj)
                            if d == 1:
                                scale_kv(i, nj)
                            if d == 2:
                                copy_similarities(i + 1)
                            if d == 3:
                                copy_keys(i)
                            if d == 4:
                                copy_queries(i, par)
                            if d == 7:
                                probabilities(i)
                            if d == 9:
                                copy_turned_probabilities(i)
                            if d == 10:
                                candidate_weights(i + 1)
                            if d == 11:
                                high_part(i + 1)
                                copy_output(i)
                            if d == 13:
                                copy_turned(i + 1, nj, 0)
                            if d == 15:
                                copy_turned(i + 1, nj, 1)

                rounds(act, Body)
                n = H * B
                take_sums(n, 1)
                scale_kv(n, 1)
                copy_keys(n)
                probabilities(n)
                copy_turned_probabilities(n)
                copy_output(n)
                act.wait_ge(y_done, n + 1 + ahead(y_done))
                for t, (t0, m) in enumerate(TT):
                    act.dma_start(out[:, t0:t0 + m, :].rearrange("b t d -> t b d"), y[0:m, :, t, :]).then_inc(s_out, 16)
                act.wait_ge(s_out, 16 * NT)

            @block.gpsimd
            def _(pool):
                G = nc.gpsimd

                def centre_scores(n):
                    pool.wait_ge(thr_ready, n * 6 + 6)
                    for a in range(2):
                        G.tensor_tensor(aS[:, :, :, a, :], sS[:, :, a, :].rearrange("p t (u j) -> p t u j", u=2),
                                        off[:, :, a, None, None].to_broadcast([128, NT, 2, 32]), ALU.subtract).then_inc(a_step, 1)
                    wait_alone(pool, a_step, n * 3 + 2)
                    G.tensor_scalar(aS[:, :, :, :, :], aS[:, :, :, :, :], FAR, None, ALU.max).then_inc(a_step, 1)
                    pool.wait_ge(high_ready, n + 1)
                    G.tensor_tensor(spl[:, :, 0:4, 1, :], aS[:, :, :, :, :].rearrange("p t u a j -> p t (u a) j"),
                                    spl[:, :, 0:4, 0, :], ALU.subtract).then_inc(low_step, 1)
                    wait_alone(pool, low_step, n + 1)
                    G.tensor_copy(spl[:, :, 4, :, :], spl[:, :, 0, :, :]).then_inc(low_ready, 1)

                def normalise(i):
                    wait_alone(pool, rz_ready, i + 1)
                    for t, (t0, m) in enumerate(TT):
                        a = G.tensor_scalar(P[0:m, t, 0:t0 + m], P[0:m, t, 0:t0 + m], rz[0:m, t:t + 1], None, ALU.mult)
                    a.then_inc(pn_ready, 1)

                pool.wait_ge(zeroed, 6)
                centre_scores(0)

                class Body:
                    @staticmethod
                    def head(hh, slot):
                        pass

                    @staticmethod
                    def item(i, slot, par, g, pair):
                        normalise(i)
                        centre_scores(i + 1)

                rounds(pool, Body)
                normalise(H * B)

            @block.vector
            def _(dve):
                V = nc.vector
                MX, AM, LOW, DT, EDT = 0, 1, 2, 3, 4

                def take_tokens(par, pair):
                    s = x2T[64 * par:64 * par + 64, pair, :] if isinstance(pair, int) else \
                        x2T[64 * par:64 * par + 64, bass.ds(pair, 1), :].rearrange("p a s -> p (a s)")
                    V.tensor_copy(xs[:, par, :], s).then_inc(xs_ready, 1)

                STEPS = 6 + 6 + 6 + 2 + 3 + 3 + 3

                def halves_max(n, second):
                    if second:
                        wait_alone(dve, top_step, n * STEPS + 12)
                    else:
                        wait_alone(dve, sim_ready, n + 1)
                    for t, (t0, m) in enumerate(TT):
                        for p in range(2):
                            o = top[0:m, t, p, 8:16] if second else top[0:m, t, p, 0:8]
                            V.max(o, (rp if second else sS)[0:m, t, p, :]).then_inc(top_step, 1)

                def halves_drop(n):
                    wait_alone(dve, top_step, n * STEPS + 6)
                    for t, (t0, m) in enumerate(TT):
                        for p in range(2):
                            V.match_replace(rp[0:m, t, p, :], top[0:m, t, p, 0:8], sS[0:m, t, p, :], NEG).then_inc(top_step, 1)

                def candidates(n):
                    dve.wait_ge(top_step, n * STEPS + 18)
                    for r, c, lo, hi, k in ((0, 0, 0, 4, 16), (1, 64, 4, 16, 3)):
                        V.tensor_tensor(cand[:, :, c:c + (hi - lo) * k].rearrange("p t (a b) -> p t a b", b=k),
                                        top[:, :, 1, lo:hi, None].to_broadcast([128, NT, hi - lo, k]),
                                        top[:, :, 0, None, 0:k].to_broadcast([128, NT, hi - lo, k]), ALU.add).then_inc(top_step, 1)

                def sums_max(n, second):
                    wait_alone(dve, top_step, n * STEPS + (26 if second else 20))
                    for t in range(NT):
                        o = fin[:, t, 8:16] if second else fin[:, t, 0:8]
                        V.max(o, (rc if second else cand)[:, t, :]).then_inc(top_step, 1)

                def sums_drop(n):
                    wait_alone(dve, top_step, n * STEPS + 23)
                    for t in range(NT):
                        V.match_replace(rc[:, t, :], fin[:, t, 0:8], cand[:, t, :], NEG).then_inc(top_step, 1)

                def threshold(n):
                    dve.wait_ge(top_step, n * STEPS + STEPS)
                    mx = fin[:, :, 0]
                    V.tensor_reduce(small[:, AM, :], top[:, :, :, :].rearrange("p t a k -> p t (a k)"), AX.X, ALU.max,
                                    apply_absolute_value=True).then_inc(thr_ready, 1)
                    V.tensor_tensor(rc[:, :, :], cand[:, :, :], fin[:, :, 0:1].to_broadcast([128, NT, NCAND]), ALU.subtract).then_inc(thr_ready, 1)
                    dve.wait_ge(thr_ready, n * 6 + 1)
                    V.scalar_tensor_tensor(small[:, LOW, :], small[:, AM, :], -DELTA, fin[:, :, 15], ALU.mult, ALU.add).then_inc(thr_ready, 1)
                    dve.wait_ge(thr_ready, n * 6 + 3)
                    V.scalar_tensor_tensor(small[:, MX, :], mx, -80.0, small[:, LOW, :], ALU.add, ALU.max).then_inc(thr_ready, 1)
                    dve.wait_ge(thr_ready, n * 6 + 4)
                    V.tensor_tensor(small[:, DT, :], small[:, MX, :], mx, ALU.subtract)
                    V.tensor_copy(off[:, :, 1], top[:, :, 1, 0]).then_inc(thr_ready, 1)
                    V.tensor_tensor(off[:, :, 0], small[:, MX, :], top[:, :, 1, 0], ALU.subtract).then_inc(thr_ready, 1)

                def softmax_sum(n):
                    dve.wait_ge(ecs_ready, n + 1)
                    for t in range(NT):
                        V.scalar_tensor_tensor(ecs[:, t, :], cand[:, t, :], small[:, MX, t:t + 1], ecs[:, t, :], ALU.is_ge, ALU.mult,
                                               accum_out=zs[:, t:t + 1]).then_inc(z_done, 1)

                def token_gain(n, par):
                    dve.wait_ge(z_done, n * 3 + 3)
                    V.reciprocal(zs[:, :], zs[:, :]).then_inc(rz_z, 1)
                    dve.wait_ge(rz_z, n + 1)
                    V.tensor_tensor(gain[:, par, :], small[:, EDT, :], zs[:, :], ALU.mult).then_inc(gain_ready, 1)

                def weights(i, d):
                    dve.wait_ge(main_done, i * NDC + (d - 3 + ahead(main_done)))
                    dve.wait_ge(e_done, i * NDC + (d + 1))
                    V.scalar_tensor_tensor(W[:, d % 4, :, :], ps[:, 2 * (d % 2):2 * (d % 2) + 2, 0:LOUT], 0.0, E[:, d % 2, :, :],
                                           ALU.is_ge, ALU.mult).then_inc(w_done, 1)

                def row_max(i):
                    dve.wait_ge(s_mm, i + 1)
                    for t, (t0, m) in enumerate(TT):
                        bank, c0 = ((MID0, 0), (MID0, 128), (MID1, 0))[t]
                        V.tensor_reduce(nmax[0:m, t:t + 1], ps[0:m, bank, c0:c0 + t0 + m], AX.X, ALU.max, negate=True).then_inc(nmax_done, 1)

                def row_sum(i):
                    dve.wait_ge(p_done, i + 1)
                    V.reciprocal(rz[:, :], zz[:, :]).then_inc(rz_ready, 1)

                def copy_turned_probabilities(i):
                    dve.wait_ge(pt_mm, i + 1)
                    V.tensor_copy(PT[:, 1, 0:216], ps[:, MID0, 0:216]).then_inc(pt1_ready, 1)

                def add_output(i, b):
                    dve.wait_ge(y_mm, i + 1)
                    if isinstance(b, int):
                        full, part = y[:, b, 0:2, :], y[0:88, b, 2, :]
                    else:
                        full = y[:, bass.ds(b, 1), 0:2, :].rearrange("p a t d -> p (a t) d")
                        part = y[0:88, bass.ds(b, 1), 2, :].rearrange("p a d -> p (a d)")
                    V.tensor_tensor(full, full, ps[:, MID1, 0:128].rearrange("p (t d) -> p t d", t=2), ALU.add)
                    V.tensor_tensor(part, part, ps[0:88, MID1, 128:192], ALU.add).then_inc(y_done, 1)

                def cast(o, name):
                    V.tensor_copy(o, const(name)).then_inc(cast_done, 1)

                cast(sel[:, :, :, :].rearrange("p w c m -> p (w c m)"), "sel")
                cast(eye16[:, :], "eye")
                cast(eyeb[:, :], "eye")
                cast(causb[:, :], "causal")
                V.memset(wf[:, H, :, :], 0.0).then_inc(wf_ready, 1)
                V.memset(ps[:, 5, :], 0.0).then_inc(zeroed, 1)
                V.memset(qT[:, 1, :], 0.0).then_inc(zeroed, 1)
                V.memset(sS[:, 2, :, :], 0.0).then_inc(zeroed, 1)
                V.memset(top[:, 2, :, :], 0.0).then_inc(zeroed, 1)
                V.memset(gain[:, :, :], 0.0).then_inc(zeroed, 1)
                V.memset(zz[:, :], 1.0).then_inc(zeroed, 1)
                dve.wait_ge(zeroed, 6)
                take_tokens(0, 0)
                halves_max(0, False)
                halves_drop(0)
                halves_max(0, True)
                candidates(0)
                sums_max(0, False)
                sums_drop(0)
                sums_max(0, True)
                threshold(0)
                softmax_sum(0)
                token_gain(0, 0)

                class Body:
                    @staticmethod
                    def head(hh, slot):
                        pass

                    @staticmethod
                    def item(i, slot, par, g, pair):
                        nj = 1 - par
                        for d in range(NDC):
                            weights(i, d)
                            if d == 0:
                                dve.wait_ge(q_mm, i + ahead(q_mm))
                                take_tokens(nj, (pair + 1) % 4 if par else pair)
                            if d == 3:
                                halves_max(i + 1, False)
                            if d == 4:
                                halves_drop(i + 1)
                            if d == 5:
                                halves_max(i + 1, True)
                            if d == 6:
                                row_max(i)
                                candidates(i + 1)
                            if d == 7:
                                sums_max(i + 1, False)
                            if d == 8:
                                row_sum(i)
                                sums_drop(i + 1)
                            if d == 9:
                                sums_max(i + 1, True)
                                copy_turned_probabilities(i)
                            if d == 10:
                                threshold(i + 1)
                            if d == 12:
                                softmax_sum(i + 1)
                            if d == 13:
                                token_gain(i + 1, nj)
                            if d == 14:
                                add_output(i, pair * 2 if par else ((pair + 3) % 4) * 2 + 1)

                rounds(dve, Body)
                n = H * B
                row_max(n)
                row_sum(n)
                copy_turned_probabilities(n)
                add_output(n, B - 1)


def _constants():
    c = np.zeros((128, NCONST), np.float32)

    def put(name, a):
        lo, hi = CONST[name]
        a = np.asarray(a, np.float64 if a.dtype == np.float64 else np.float32)
        c[:a.shape[0], lo:hi] = a.reshape(a.shape[0], -1)

    l = np.arange(L).reshape(XCH, XROWS)[:, :, None]
    ang = 2.0 * np.pi * ((l * np.arange(NF)[None, None, :]) % L) / L
    put("dft", np.concatenate([np.cos(ang), np.sin(ang)], 2).transpose(1, 0, 2))
    pos = np.arange(S)[:, None].astype(np.float64)
    div = np.exp(np.arange(0, D, 2) * (-np.log(10000.0) / D))
    pe = np.zeros((S, D), np.float32)
    pe[:, 0::2] = np.sin(pos * div)
    pe[:, 1::2] = np.cos(pos * div)
    put("pe", np.concatenate([pe.T, pe.T], 0))
    put("eye", np.eye(128, dtype=np.float32))
    p = np.arange(128)
    put("mean", (p[:, None] // D == p[None, :] // D) / np.float32(D))
    put("head", ((p[:, None] % D) // DH == np.arange(H)[None, :]).astype(np.float32))
    rot = np.zeros((128, 128), np.float32)
    rot[p[1::2], p[0::2]] = -1.0
    rot[p[0::2], p[1::2]] = 1.0
    put("rot", rot)
    inv = (np.float32(1.0) / np.float32(10000.0) ** (np.arange(0, D, 2, dtype=np.float32) / np.float32(D))).astype(np.float32)
    angles = np.arange(LOUT, dtype=np.float32)[None, :] * np.repeat(inv, 2)[:, None]
    put("cos", np.tile(np.cos(angles), (2, 1)))
    put("sin", np.tile(np.sin(angles), (2, 1)))
    diff = np.arange(LOUT)[None, :] - p[:, None]
    put("decay", np.where(diff >= 0, np.exp(np.maximum(diff, 0).astype(np.float32) * np.float32(np.log(0.96875))), 0.0).astype(np.float32))
    put("causal", np.where(p[None, :] > p[:, None], -1.0e30, 0.0).astype(np.float32))
    m = np.arange(128)
    sel = np.zeros((128, 2, 8, 128), np.float32)
    for swapped in range(2):
        for c8 in range(8):
            for part in (0, 32):
                sel[64 * swapped + part + m % 32, swapped, c8, m] = 1.0
                sel[64 * (1 - swapped) + part + 4 * c8 + m // 32, swapped, c8, m] = 1.0
    put("sel", sel)
    return c


def _pair(w):
    z = np.zeros((128, 128), w.dtype)
    z[:64, :64] = w
    z[64:, 64:] = w
    return z


def _twice(w):
    return np.concatenate([w, w], 0)


def _arrays(i):
    t = {k[7:]: np.asarray(v) for k, v in i.items() if k.startswith("L0_tok_")}
    x = np.asarray(i["x"])
    a = {}
    a["consts"] = _constants()
    a["xrows"] = x.reshape(B, XCH, XROWS, D).transpose(2, 1, 0, 3)
    a["xcols"] = x.transpose(0, 2, 1).reshape(NPAIR, 128, L).transpose(1, 0, 2)
    li, mi = t["l_in_w"], t["m_in_w"]
    blocks = {
        "q1": _pair(li[:D].T), "k1": _pair(li[D:2 * D].T), "v1": _pair(li[2 * D:].T), "o1": _pair(t["l_out_w"].T),
        "q2": _pair(mi[:D].T), "k2": _pair(mi[D:2 * D].T), "v2": _pair(mi[2 * D:].T), "o2": _pair(t["m_out_w"].T),
        "f1": _twice(t["ff_w1"].T), "f2": t["ff_w2"].T.reshape(2, 128, D).transpose(1, 0, 2).reshape(128, 2 * D),
        "rq": _pair(np.asarray(i["L0_attn_W_Q"])), "rk": _pair(np.asarray(i["L0_attn_W_K"])),
        "rv": _pair(np.asarray(i["L0_attn_W_V"])),
    }
    a["weights"] = np.concatenate([blocks[n] for n in WT], 1)
    lb, mb = t["l_in_b"], t["m_in_b"]
    cols = {
        "bq1": lb[:D], "bk1": lb[D:2 * D], "bv1": lb[2 * D:], "bo1": t["l_out_b"], "g1": t["ln1_g"], "b1": t["ln1_b"],
        "fb1a": t["ff_b1"][:128], "fb1b": t["ff_b1"][128:], "fb2": t["ff_b2"], "g2": t["ln2_g"], "b2": t["ln2_b"],
        "bq2": mb[:D], "bk2": mb[D:2 * D], "bv2": mb[2 * D:], "bo2": t["m_out_b"],
    }
    a["biases"] = np.stack([cols[n] if cols[n].size == 128 else _twice(cols[n]) for n in BIAS], 1)
    wpk = np.asarray(i["L0_ffn_Wq_pk"]).reshape(D, 2, H, DKEY).transpose(3, 1, 2, 0)
    pk = np.asarray(i["L0_ffn_pk_keys"]).transpose(3, 0, 2, 1)
    a["pkw"] = np.concatenate([wpk, pk], 3).reshape(DKEY, 16 * 128)
    a["wq"] = np.asarray(i["L0_ffn_Wq"]).reshape(D, H, D)
    a["wo"] = np.asarray(i["L0_ffn_Wo"]).reshape(H, D, D).transpose(1, 0, 2)
    tab = np.concatenate([np.asarray(i["L0_ffn_keys_table"]), np.asarray(i["L0_ffn_values_table"])], 1)
    tab = tab.reshape(H, 2, 8, 4, 2, 32, 128)
    a["tables"] = tab.transpose(0, 3, 5, 4, 1, 2, 6).reshape(H, 128, NCH, 128)
    return {k: np.ascontiguousarray(v) for k, v in a.items()}


def kernel(**inputs):
    import concourse.bacc as _bacc
    from concourse.bass_utils import run_bass_kernel_spmd as _run

    nc = _bacc.Bacc("TRN2", target_bir_lowering=False, num_devices=1)
    arrays, args = {}, {}
    for name, a in _arrays(inputs).items():
        arrays[f"in_{name}"] = a
        args[name] = nc.dram_tensor(f"in_{name}", a.shape, mybir.dt.from_np(a.dtype), kind="ExternalInput").ap()
    args["out"] = nc.dram_tensor("out_0", (B, LOUT, D), F32, kind="ExternalOutput").ap()
    audio_tower(nc, **args)
    r = _run(nc, [arrays], core_ids=[0])
    return r.results[0]["out_0"]
```

```python
from contextlib import ExitStack

import concourse.bass as bass
from concourse import mybir
import numpy as np

ALU = mybir.AluOpType
ACT = mybir.ActivationFunctionType
AX = mybir.AxisListType
F32 = mybir.dt.float32
F16 = mybir.dt.float16
BF16 = mybir.dt.bfloat16

B, L, D = 8, 375, 64
NPAIR = B // 2
KSIZE = 32
LOUT = L - KSIZE + 1
NF = L // 2 + 1
S = NF + 1
XCH = 3
XROWS = L // XCH
H = 8
DH = D // H
QT = ((0, 95), (95, 94))
EPS = 1e-5
TT = ((0, 128), (128, 128), (256, 88))
NT = len(TT)
DFF = 4 * D
NKEY = 64
TOPK = 16
DKEY = 32
NCH = NKEY * NKEY // 128
NCAND = 100
NEG = -3.0e38
FAR = -30000.0
DELTA = 5e-7

CONST = {}
_at = 0
for _n, _w in (("dft", XCH * 2 * NF), ("pe", S), ("eye", 128), ("mean", 128), ("head", H), ("batch_head", 2 * H), ("rot", 128),
               ("cos", LOUT), ("sin", LOUT), ("decay", LOUT), ("causal", 128), ("sel", 2 * 8 * 128)):
    CONST[_n] = (_at, _at + _w)
    _at += _w
NCONST = _at
WT = {}
_at = 0
for _n, _w in (("q1", 128), ("k1", 128), ("v1", 128), ("o1", 128), ("q2", 128), ("k2", 128), ("v2", 128),
               ("o2", 128), ("f1", DFF), ("f2", 2 * D), ("rq", 128), ("rk", 128), ("rv", 128)):
    WT[_n] = (_at, _at + _w)
    _at += _w
NWT = _at
BIAS = {n: i for i, n in enumerate(("bq1", "bk1", "bv1", "bo1", "g1", "b1", "fb1a", "fb1b", "fb2", "g2", "b2",
                                    "bq2", "bk2", "bv2", "bo2"))}
NBIAS = len(BIAS)


def audio_tower(nc, consts, xrows, xcols, weights, biases, pkw, wq, wo, tables, out):
    with ExitStack() as ctx:
        def sb(name, shape, dt=F32):
            return ctx.enter_context(nc.sbuf_tensor(name, shape, dt))

        ps = ctx.enter_context(nc.psum_tensor("ps", [128, 8, 512], F32))
        hT = sb("hT", [128, NPAIR, LOUT])
        cst = sb("cst", [128, NCONST])
        wts = sb("wts", [128, NWT])
        bia = sb("bia", [128, NBIAS])
        epst = sb("epst", [128, 1])
        x2T = sb("x2T", [128, NPAIR, LOUT])

        def const(name):
            return cst[:, CONST[name][0]:CONST[name][1]]

        def weight(name):
            return wts[:, WT[name][0]:WT[name][1]]

        def bias(name):
            return bia[:, BIAS[name]:BIAS[name] + 1]

        token_mixer(nc, ps, hT, const, weight, bias, epst, cst, wts, bia, consts, xrows, xcols, weights, biases)
        retention(nc, ps, hT, x2T, epst, const, weight)
        product_key_attention(nc, ps, hT, x2T, const, pkw, wq, wo, tables, out)


def token_mixer(nc, ps, hT, const, weight, bias, epst, cst, wts, bia, consts, xrows, xcols, weights, biases):
    with ExitStack() as ctx:
        def sb(name, shape, dt=F32):
            return ctx.enter_context(nc.sbuf_tensor(name, shape, dt))

        def sem(name):
            return ctx.enter_context(nc.semaphore(name))

        xr = sb("xr", [XROWS, XCH, B * D])
        xT = sb("xT", [128, NPAIR, L])
        sq = sb("sq", [128, NPAIR, 2 * NF])
        amp = sb("amp", [128, NPAIR, NF])
        src = sb("src", [128, NPAIR, S])
        qT = sb("qT", [128, NPAIR, S])
        kT = sb("kT", [128, NPAIR, S])
        vt = sb("vt", [95, 2, NPAIR * 128])
        qz = sb("qz", [128, 2, 2, H, S])
        kp = sb("kp", [128, 2, S])
        vz = sb("vz", [95, 2, 2, H * (128 + DH)])
        negmax = sb("negmax", [95, 2, 4])
        ebias = sb("ebias", [95, 2, 4])
        P = sb("P", [95, 2, 4, S])
        Z = sb("Z", [95, 2, 4])
        rz = sb("rz", [95, 2, 4])
        PT = sb("PT", [95, 2, 2, 4 * 95])
        oT = sb("oT", [128, NPAIR, S])
        x1 = sb("x1", [128, NPAIR, S])
        cen = sb("cen", [128, NPAIR, S])
        sqr = sb("sqr", [128, NPAIR, S])
        rstd = sb("rstd", [128, NPAIR, S])
        hff = sb("hff", [128, 2, 2, NPAIR * S])
        q2 = sb("q2", [128, NPAIR])
        q2z = sb("q2z", [128, NPAIR, H])
        s2 = sb("s2", [H, B, S])
        m2 = sb("m2", [H, B])
        z2 = sb("z2", [H, B])
        p2T = sb("p2T", [95, 2, B * H])
        om = sb("om", [128, NPAIR, H])
        o2 = sb("o2", [128, NPAIR])
        sp = sb("sp", [128, 8, NPAIR])
        tau = sb("tau", [128, 5, NPAIR])
        tsum = sb("tsum", [128, 6, NPAIR])
        win = sb("win", [128, 2, NPAIR, L])

        s_const, s_x, s_w = sem("s_const"), sem("s_x"), sem("s_w")
        dft_done, sq_done, power_done, amp_done = sem("dft_done"), sem("sq_done"), sem("power_done"), sem("amp_done")
        last_done, src_done = sem("last_done"), sem("src_done")
        qk_mm, v_mm, q_ready, k_ready, v_ready = sem("qk_mm"), sem("v_mm"), sem("q_ready"), sem("k_ready"), sem("v_ready")
        qz_ready, score_done, max_done, ebias_done = sem("qz_ready"), sem("score_done"), sem("max_done"), sem("ebias_done")
        exp_done, ptr_done, pt0_ready, pt1_ready = sem("exp_done"), sem("ptr_done"), sem("pt0_ready"), sem("pt1_ready")
        rz_ready, pn_ready, pv_done, oT_ready = sem("rz_ready"), sem("pn_ready"), sem("pv_done"), sem("oT_ready")
        proj_mm, res_done = sem("proj_mm"), sem("res_done")
        mean_mm, cen_done, sqr_done, var_mm, rstd_done, norm_done, gain_done, ln_done = (
            sem("mean_mm"), sem("cen_done"), sem("sqr_done"), sem("var_mm"), sem("rstd_done"), sem("norm_done"),
            sem("gain_done"), sem("ln_done"))
        ff1_mm, relu_done, ff2_mm = sem("ff1_mm"), sem("relu_done"), sem("ff2_mm")
        kv2_mm, q2_mm, kv2_ready, q2_ready, q2z_ready = sem("kv2_mm"), sem("q2_mm"), sem("kv2_ready"), sem("q2_ready"), sem("q2z_ready")
        s2_mm, soft2, p2_mm, p2T_ready, o2_mm, om_done, o2_ready, tau_mm = (
            sem("s2_mm"), sem("soft2"), sem("p2_mm"), sem("p2T_ready"), sem("o2_mm"), sem("om_done"), sem("o2_ready"), sem("tau_mm"))
        plus_done, tau_step, win_step, tsum_step, mix_done = sem("plus_done"), sem("tau_step"), sem("win_step"), sem("tsum_step"), sem("mix_done")
        zero_done, vz_zeroed, kp_ready, vz_ready, std_done = sem("zero_done"), sem("vz_zeroed"), sem("kp_ready"), sem("vz_ready"), sem("std_done")

        AHEAD = {pt0_ready: 1, pt1_ready: 1, pv_done: 1, oT_ready: 2}
        two = [slice(0, 2), slice(2, 4)]

        def bank2(b, width=S):
            return ps[:, b, 0:2 * width].rearrange("p (a s) -> p a s", a=2)

        with nc.Block() as block:

            @block.sync
            def _(sp_):
                for count, n in AHEAD.items():
                    sp_.sem_inc(count, n)
                sp_.dma_start(xr[:, :, :].rearrange("p c n -> p (c n)"), xrows.rearrange("p c b d -> p (c b d)")).then_inc(s_x, 16)
                sp_.dma_start(cst[:, :], consts).then_inc(s_const, 16)
                sp_.dma_start(xT[:, :, :], xcols).then_inc(s_x, 16)

            @block.gpsimd
            def _(pool):
                pool.wait_ge(s_x, 32)
                nc.gpsimd.tensor_copy(src[:, :, 0:1], xT[:, :, L - 1:L]).then_inc(last_done, 1)
                nc.gpsimd.memset(vz[:, :, :, :], 0.0).then_inc(vz_zeroed, 1)

                def feed(par, p):
                    if isinstance(p, int):
                        q, k = qT[:, p:p + 1, :], kT[:, p, :]
                    else:
                        q, k = qT[:, bass.ds(p, 1), :], kT[:, bass.ds(p, 1), :].rearrange("p a s -> p (a s)")
                    nc.gpsimd.tensor_tensor(qz[:, par, :, :, :].rearrange("p b h s -> p (b h) s"), q.to_broadcast([128, 2 * H, S]),
                                            const("batch_head")[:, :, None].to_broadcast([128, 2 * H, S]), ALU.mult).then_inc(qz_ready, 1)
                    nc.gpsimd.tensor_copy(kp[:, par, :], k).then_inc(kp_ready, 1)

                def feed_values(par, p):
                    for kt, (k0, kn) in enumerate(QT):
                        blocks = vz[0:kn, par, kt, :].rearrange("p (h x) -> p h x", h=H)
                        for b2 in range(2):
                            c0 = 64 * b2
                            v = vt[0:kn, kt, 128 * p + c0:128 * p + c0 + 64] if isinstance(p, int) else \
                                vt[0:kn, kt, bass.ds(p * 128 + c0, 64)]
                            nc.gpsimd.tensor_copy(blocks[:, :, c0:c0 + DH], v.rearrange("p (h d) -> p h d", h=H)).then_inc(vz_ready, 1)

                pool.wait_ge(s_const, 16)
                pool.wait_ge(q_ready, 2)
                pool.wait_ge(k_ready, 2)
                feed(0, 0)
                pool.wait_ge(v_ready, 1)
                pool.wait_ge(vz_zeroed, 1)
                feed_values(0, 0)
                with pool.Fori(0, NPAIR // 2) as pp:
                    for par in range(2):
                        p = pp * 2 + par
                        following = (p + 1) % NPAIR
                        pool.wait_ge(score_done, 8 * p + 1)
                        feed(1 - par, following)
                        pool.wait_ge(pv_done, 8 * p + 1)
                        feed_values(1 - par, following)

            @block.tensor
            def _(pe):
                def layer_norm(k, x, ready, n_ready, n):
                    for g in range(2):
                        pe.wait_ge(ready, n_ready + g)
                        nc.tensor.matmul(ps[:, g, 0:2 * S], const("mean"), x[:, two[g], :], start=True, stop=True).then_inc(mean_mm, 1)
                    for g in range(2):
                        pe.wait_ge(sqr_done, 2 * k + g + 1)
                        nc.tensor.matmul(ps[:, 2 + g, 0:2 * S], const("mean"), sqr[:, two[g], :], start=True, stop=True).then_inc(var_mm, 1)

                pe.wait_ge(s_x, 32)
                pe.wait_ge(s_const, 16)
                pe.wait_ge(zero_done, 2)
                for p in range(NPAIR):
                    for c in range(XCH):
                        mm = nc.tensor.matmul(ps[:, p, 0:2 * NF], xr[:, c, 128 * p:128 * p + 128],
                                              const("dft")[0:XROWS, 2 * NF * c:2 * NF * (c + 1)],
                                              start=(c == 0), stop=(c == XCH - 1))
                    mm.then_inc(dft_done, 1)
                pe.wait_ge(s_w, 32)
                pe.wait_ge(src_done, 1)
                for g in range(2):
                    nc.tensor.matmul(ps[:, 4 + g, 0:2 * S], weight("q1"), src[:, two[g], :], start=True, stop=True).then_inc(qk_mm, 1)
                for g in range(2):
                    nc.tensor.matmul(ps[:, 6 + g, 0:2 * S], weight("k1"), src[:, two[g], :], start=True, stop=True).then_inc(qk_mm, 1)
                for kt, (k0, kn) in enumerate(QT):
                    for p in range(NPAIR):
                        mm = nc.tensor.matmul(ps[0:kn, kt, 128 * p:128 * p + 128], src[:, p, k0:k0 + kn], weight("v1"),
                                              start=True, stop=True)
                    mm.then_inc(v_mm, 1)
                pe.wait_ge(v_ready, 1)

                def scores(par, t):
                    qt, b2, hf = t // 4, (t // 2) % 2, t % 2
                    q0, n = QT[qt]
                    for j in range(4):
                        mm = nc.tensor.matmul(ps[0:n, 2 * hf + j // 2, (j % 2) * S:(j % 2 + 1) * S],
                                              qz[:, par, b2, 4 * hf + j, q0:q0 + n], kp[:, par, :], start=True, stop=True)
                    mm.then_inc(score_done, 1)

                def turn_probabilities(k, t):
                    hf, n = t % 2, QT[t // 4][1]
                    pe.wait_ge(pn_ready, k + 1)
                    pe.wait_ge(pt0_ready, k + 1)
                    pe.wait_ge(pt1_ready, k + 1)
                    for j in range(4):
                        for kt, (k0, kn) in enumerate(QT):
                            mm = nc.tensor.transpose(ps[0:kn, 4 + kt, 95 * j:95 * j + n],
                                                     P[0:n, hf, j, k0:k0 + kn], const("eye")[0:n, 0:n])
                    mm.then_inc(ptr_done, 1)

                def values(k, par, t):
                    qt, b2, hf = t // 4, (t // 2) % 2, t % 2
                    n = QT[qt][1]
                    pe.wait_ge(pt0_ready, k + 2)
                    pe.wait_ge(pt1_ready, k + 2)
                    for j in range(4):
                        for kt, (k0, kn) in enumerate(QT):
                            at = 128 * (4 * hf + j) + 64 * b2
                            mm = nc.tensor.matmul(ps[64 * b2:64 * b2 + 64, 6 + qt, 0:n], vz[0:kn, par, kt, at:at + 64],
                                                  PT[0:kn, hf, kt, 95 * j:95 * j + n],
                                                  start=(hf == 0 and j == 0 and kt == 0), stop=(hf == 1 and j == 3 and kt == 1))
                    mm.then_inc(pv_done, 1)

                pe.wait_ge(qz_ready, 1)
                pe.wait_ge(kp_ready, 1)
                scores(0, 0)
                scores(0, 1)
                with pe.Fori(0, NPAIR // 2) as pp:
                    for par in range(2):
                        p = pp * 2 + par
                        for t in range(8):
                            pe.wait_ge(exp_done, 8 * p + t + 1)
                            if t == 6:
                                pe.wait_ge(qz_ready, p + 2)
                                pe.wait_ge(kp_ready, p + 2)
                            if t < 6:
                                scores(par, t + 2)
                            else:
                                scores(1 - par, t - 6)
                            turn_probabilities(8 * p + t, t)
                            if t == 0:
                                pe.wait_ge(vz_ready, 4 * p + 4)
                            if t >= 1:
                                if t in (1, 5):
                                    pe.wait_ge(oT_ready, 2 * p + (t // 4 + 1))
                                values(8 * p + (t - 1), par, t - 1)
                        values(8 * p + 7, par, 7)
                pe.wait_ge(oT_ready, 2 * NPAIR + 2)
                pe.wait_ge(exp_done, 8 * NPAIR + 2)
                for g in range(2):
                    nc.tensor.matmul(ps[:, 4 + g, 0:2 * S], weight("o1"), oT[:, two[g], :], start=True, stop=True).then_inc(proj_mm, 1)
                layer_norm(0, x1, res_done, 1, 2)
                for b2 in range(2):
                    for hf in range(2):
                        for g in range(2):
                            if b2 == 0 and hf == 0:
                                pe.wait_ge(ln_done, g + 1)
                            bank = (4 * b2 + 2 * hf + g + 4) % 8
                            nc.tensor.matmul(ps[:, bank, 0:2 * S], weight("f1")[64 * b2:64 * b2 + 64, 128 * hf:128 * hf + 128],
                                             x1[64 * b2:64 * b2 + 64, two[g], :], start=True, stop=True).then_inc(ff1_mm, 1)
                for g in range(2):
                    for b2 in range(2):
                        pe.wait_ge(relu_done, 8)
                        for hf in range(2):
                            mm = nc.tensor.matmul(ps[64 * b2:64 * b2 + 64, 4 + g, 0:2 * S], weight("f2")[:, 64 * hf:64 * hf + 64],
                                                  hff[:, b2, hf, 2 * S * g:2 * S * (g + 1)], start=(hf == 0), stop=(hf == 1))
                        mm.then_inc(ff2_mm, 1)
                layer_norm(1, x1, res_done, 3, 2)
                pe.wait_ge(ln_done, 4)
                for g in range(2):
                    nc.tensor.matmul(ps[:, 4 + g, 0:2 * S], weight("k2"), x1[:, two[g], :], start=True, stop=True).then_inc(kv2_mm, 1)
                for kt, (k0, kn) in enumerate(QT):
                    for p in range(NPAIR):
                        mm = nc.tensor.matmul(ps[0:kn, kt, 128 * p:128 * p + 128], x1[:, p, k0:k0 + kn], weight("v2"),
                                              start=True, stop=True)
                    mm.then_inc(kv2_mm, 1)
                nc.tensor.matmul(ps[:, 6, 0:NPAIR], weight("q2"), x1[:, :, S - 1:S].rearrange("p a s -> p (a s)"), start=True, stop=True).then_inc(q2_mm, 1)
                pe.wait_ge(kv2_ready, 2)
                pe.wait_ge(q2z_ready, 1)
                for b2 in range(2):
                    for p in range(NPAIR):
                        rows = slice(64 * b2, 64 * b2 + 64)
                        mm = nc.tensor.matmul(ps[0:H, [4, 5, 2, 3][2 * b2 + p // 2], (p % 2) * S:(p % 2 + 1) * S],
                                              q2z[rows, p, :], kT[rows, p, :], start=True, stop=True)
                        if p % 2 == 1:
                            mm.then_inc(s2_mm, 1)
                pe.wait_ge(soft2, 6)
                for kt, (k0, kn) in enumerate(QT):
                    for b in range(B):
                        mm = nc.tensor.transpose(ps[0:kn, 6 + kt, H * b:H * b + H], s2[:, b, k0:k0 + kn], const("eye")[0:H, 0:H])
                mm.then_inc(p2_mm, 1)
                pe.wait_ge(p2T_ready, 2)
                pe.wait_ge(kv2_ready, 4)
                for b in range(B):
                    p, b2 = b // 2, b % 2
                    for kt, (k0, kn) in enumerate(QT):
                        mm = nc.tensor.matmul(ps[64 * b2:64 * b2 + 64, b2, H * p:H * p + H],
                                              vt[0:kn, kt, 128 * p + 64 * b2:128 * p + 64 * b2 + 64],
                                              p2T[0:kn, kt, H * (4 * b2 + p):H * (4 * b2 + p) + H], start=(kt == 0), stop=(kt == 1))
                mm.then_inc(o2_mm, 1)
                pe.wait_ge(o2_ready, 2)
                nc.tensor.matmul(ps[:, 2, 0:NPAIR], weight("o2"), o2[:, :], start=True, stop=True).then_inc(tau_mm, 1)

            @block.scalar
            def _(act):
                def deviations(k):
                    for g in range(2):
                        act.wait_ge(cen_done, 2 * k + g + 1)
                        nc.scalar.activation(sqr[:, two[g], :], cen[:, two[g], :], ACT.Square).then_inc(sqr_done, 1)
                    for g in range(2):
                        act.wait_ge(var_mm, 2 * k + g + 1)
                        nc.scalar.activation(rstd[:, two[g], :], bank2(2 + g), ACT.Sqrt, bias=epst[:, :]).then_inc(std_done, 1)

                act.dma_start(wts[:, :], weights).then_inc(s_w, 16)
                act.dma_start(bia[:, :], biases).then_inc(s_w, 16)
                for p in range(NPAIR):
                    act.wait_ge(dft_done, p + 1)
                    nc.scalar.activation(sq[:, p, :], ps[:, p, 0:2 * NF], ACT.Square).then_inc(sq_done, 1)
                act.wait_ge(power_done, NPAIR)
                nc.scalar.activation(src[:, :, 1:S], amp[:, :, :], ACT.Sqrt).then_inc(amp_done, 1)
                act.wait_ge(s_w, 32)
                for g in range(2):
                    act.wait_ge(qk_mm, g + 1)
                    nc.scalar.activation(qT[:, two[g], :], bank2(4 + g), ACT.Identity, bias=bias("bq1")).then_inc(q_ready, 1)
                act.wait_ge(v_mm, 2)
                nc.scalar.activation(vt[0:95, :, :], ps[0:95, 0:2, :], ACT.Copy).then_inc(v_ready, 1)

                def exponentials(t):
                    hf, n = t % 2, QT[t // 4][1]
                    for j in range(4):
                        a = nc.scalar.activation(P[0:n, hf, j, :], ps[0:n, 2 * hf + j // 2, (j % 2) * S:(j % 2 + 1) * S],
                                                 ACT.Exp, bias=ebias[0:n, hf, j:j + 1], scale=DH ** -0.5,
                                                 accum_out=Z[0:n, hf, j:j + 1])
                    a.then_inc(exp_done, 1)

                for t in range(2):
                    act.wait_ge(ebias_done, t + 1)
                    exponentials(t)
                with act.Fori(0, NPAIR) as p:
                    for t in range(8):
                        act.wait_ge(ptr_done, 8 * p + t + 1)
                        nc.scalar.activation(PT[:, t % 2, 1, :], ps[0:95, 5, 0:380], ACT.Copy).then_inc(pt1_ready, 1)
                        act.wait_ge(ebias_done, 8 * p + t + 3)
                        exponentials((t + 2) % 8)
                        if t in (4, 7):
                            qt = t // 4 if t == 7 else 0
                            q0, m = QT[qt]
                            act.wait_ge(pv_done, 8 * p + (4 * qt + 4) + 1)
                            nc.scalar.activation(oT[:, bass.ds(p, 1), q0:q0 + m].rearrange("p a s -> p (a s)"),
                                                 ps[:, 6 + qt, 0:m], ACT.Identity, bias=bias("bv1")).then_inc(oT_ready, 1)
                act.wait_ge(zero_done, 2)
                deviations(0)
                for k in range(8):
                    b2, hf, g = k // 4, (k // 2) % 2, k % 2
                    act.wait_ge(ff1_mm, k + 1)
                    nc.scalar.activation(hff[:, b2, hf, 2 * S * g:2 * S * (g + 1)], ps[:, (k + 4) % 8, 0:2 * S], ACT.Relu,
                                         bias=bias(("fb1a", "fb1b")[hf])).then_inc(relu_done, 1)
                deviations(1)
                act.wait_ge(vz_ready, 4 * (NPAIR + 1))
                for g in range(2):
                    act.wait_ge(kv2_mm, g + 1)
                    nc.scalar.activation(kT[:, two[g], :], bank2(4 + g), ACT.Identity, bias=bias("bk2")).then_inc(kv2_ready, 1)
                act.wait_ge(kv2_mm, 4)
                for kt in range(2):
                    nc.scalar.activation(vt[0:QT[kt][1], kt, :], ps[0:QT[kt][1], kt, :], ACT.Copy).then_inc(kv2_ready, 1)
                act.wait_ge(soft2, 2)
                nc.scalar.activation(s2[:, :, :], s2[:, :, :], ACT.Exp, scale=DH ** -0.5).then_inc(soft2, 1)
                act.wait_ge(plus_done, 3)
                nc.scalar.activation(sp[:, 3, :], sp[:, 2, :], ACT.Exp, scale=-1.0).then_inc(plus_done, 1)
                act.wait_ge(plus_done, 4)
                nc.scalar.activation(sp[:, 4, :], sp[:, 3, :], ACT.Ln, bias=1.0).then_inc(plus_done, 1)

            @block.vector
            def _(dve):
                V = nc.vector

                def layer_norm(k, gain, shift):
                    for g in range(2):
                        dve.wait_ge(mean_mm, 2 * k + g + 1)
                        V.tensor_tensor(cen[:, two[g], :], x1[:, two[g], :], bank2(g), ALU.subtract).then_inc(cen_done, 1)
                    for g in range(2):
                        dve.wait_ge(std_done, 2 * k + g + 1)
                        V.reciprocal(rstd[:, two[g], :], rstd[:, two[g], :]).then_inc(rstd_done, 1)
                        dve.wait_ge(rstd_done, 2 * k + g + 1)
                        V.scalar_tensor_tensor(sqr[:, two[g], :], cen[:, two[g], :], gain, rstd[:, two[g], :], ALU.mult, ALU.mult).then_inc(norm_done, 1)
                        dve.wait_ge(norm_done, 2 * k + g + 1)
                        V.tensor_scalar(x1[:, two[g], :], sqr[:, two[g], :], shift, None, ALU.add).then_inc(ln_done, 1)

                V.memset(epst[:, :], EPS).then_inc(zero_done, 1)
                V.memset(ps[:, :, :], 0.0).then_inc(zero_done, 1)
                for p in range(NPAIR):
                    dve.wait_ge(sq_done, p + 1)
                    V.tensor_tensor(amp[:, p, :], sq[:, p, 0:NF], sq[:, p, NF:2 * NF], ALU.add).then_inc(power_done, 1)
                dve.wait_ge(amp_done, 1)
                dve.wait_ge(last_done, 1)
                dve.wait_ge(s_const, 16)
                V.tensor_tensor(src[:, :, :], src[:, :, :], const("pe")[:, None, :].to_broadcast([128, NPAIR, S]), ALU.add).then_inc(src_done, 1)
                dve.wait_ge(s_w, 32)
                for g in range(2):
                    dve.wait_ge(qk_mm, 3 + g)
                    V.tensor_scalar(kT[:, two[g], :], bank2(6 + g), bias("bk1"), None, ALU.add).then_inc(k_ready, 1)

                def row_max(k, t):
                    hf, n = t % 2, QT[t // 4][1]
                    dve.wait_ge(score_done, k + 1)
                    V.tensor_reduce(negmax[0:n, hf, :].rearrange("p (b h) -> p b h", b=2),
                                    ps[0:n, 2 * hf:2 * hf + 2, 0:2 * S].rearrange("p b (h k) -> p b h k", h=2),
                                    AX.X, ALU.max, negate=True).then_inc(max_done, 1)
                    dve.wait_ge(max_done, k + 1)
                    V.tensor_scalar(ebias[0:n, hf, :], negmax[0:n, hf, :], DH ** -0.5, None, ALU.mult).then_inc(ebias_done, 1)

                row_max(0, 0)
                row_max(1, 1)
                with dve.Fori(0, NPAIR) as p:
                    for t in range(8):
                        hf, n = t % 2, QT[t // 4][1]
                        dve.wait_ge(exp_done, 8 * p + t + 1)
                        V.reciprocal(rz[0:n, hf, :], Z[0:n, hf, :]).then_inc(rz_ready, 1)
                        dve.wait_ge(rz_ready, 8 * p + t + 1)
                        V.tensor_tensor(P[0:n, hf, :, :], P[0:n, hf, :, :], rz[0:n, hf, :, None].to_broadcast([n, 4, S]), ALU.mult).then_inc(pn_ready, 1)
                        row_max(8 * p + (t + 2), (t + 2) % 8)
                        dve.wait_ge(ptr_done, 8 * p + t + 1)
                        V.tensor_copy(PT[:, hf, 0, :], ps[0:95, 4, 0:380]).then_inc(pt0_ready, 1)
                for g in range(2):
                    dve.wait_ge(proj_mm, g + 1)
                    V.scalar_tensor_tensor(x1[:, two[g], :], bank2(4 + g), bias("bo1"), src[:, two[g], :], ALU.add, ALU.add).then_inc(res_done, 1)
                layer_norm(0, bias("g1"), bias("b1"))
                for g in range(2):
                    dve.wait_ge(ff2_mm, 2 * g + 2)
                    V.scalar_tensor_tensor(x1[:, two[g], :], bank2(4 + g), bias("fb2"), x1[:, two[g], :], ALU.add, ALU.add).then_inc(res_done, 1)
                layer_norm(1, bias("g2"), bias("b2"))
                dve.wait_ge(q2_mm, 1)
                V.tensor_scalar(q2[:, :], ps[:, 6, 0:NPAIR], bias("bq2"), None, ALU.add).then_inc(q2_ready, 1)
                dve.wait_ge(q2_ready, 1)
                V.tensor_tensor(q2z[:, :, :], q2[:, :, None].to_broadcast([128, NPAIR, H]),
                                const("head")[:, None, :].to_broadcast([128, NPAIR, H]), ALU.mult).then_inc(q2z_ready, 1)
                for k, bank in enumerate((4, 5, 2, 3)):
                    dve.wait_ge(s2_mm, k + 1)
                    cp = V.tensor_copy(s2[:, 2 * k:2 * k + 2, :], ps[0:H, bank, 0:2 * S].rearrange("p (a s) -> p a s", a=2))
                cp.then_inc(om_done, 1)
                dve.wait_ge(om_done, 1)
                V.tensor_reduce(m2[:, :], s2[:, :, :], AX.X, ALU.max).then_inc(soft2, 1)
                dve.wait_ge(soft2, 1)
                V.tensor_tensor(s2[:, :, :], s2[:, :, :], m2[:, :, None].to_broadcast([H, B, S]), ALU.subtract).then_inc(soft2, 1)
                dve.wait_ge(soft2, 3)
                V.tensor_reduce(z2[:, :], s2[:, :, :], AX.X, ALU.add).then_inc(soft2, 1)
                dve.wait_ge(soft2, 4)
                V.reciprocal(m2[:, :], z2[:, :]).then_inc(soft2, 1)
                dve.wait_ge(soft2, 5)
                V.tensor_tensor(s2[:, :, :], s2[:, :, :], m2[:, :, None].to_broadcast([H, B, S]), ALU.mult).then_inc(soft2, 1)
                dve.wait_ge(p2_mm, 1)
                for kt, (k0, kn) in enumerate(QT):
                    V.tensor_copy(p2T[0:kn, kt, :], ps[0:kn, 6 + kt, 0:B * H]).then_inc(p2T_ready, 1)
                dve.wait_ge(o2_mm, 1)
                for b2 in range(2):
                    rows = slice(64 * b2, 64 * b2 + 64)
                    V.tensor_tensor(om[rows, :, :], ps[rows, b2, 0:NPAIR * H].rearrange("p (a h) -> p a h", a=NPAIR),
                                    const("head")[rows, None, :].to_broadcast([64, NPAIR, H]), ALU.mult).then_inc(om_done, 1)
                dve.wait_ge(om_done, 3)
                V.tensor_reduce(o2[:, :], om[:, :, :], AX.X, ALU.add).then_inc(o2_ready, 1)
                dve.wait_ge(o2_ready, 1)
                V.tensor_scalar(o2[:, :], o2[:, :], bias("bv2"), None, ALU.add).then_inc(o2_ready, 1)
                dve.wait_ge(tau_mm, 1)
                V.tensor_scalar(sp[:, 0, :], ps[:, 2, 0:NPAIR], bias("bo2"), None, ALU.add).then_inc(plus_done, 1)
                dve.wait_ge(plus_done, 1)
                V.tensor_scalar(sp[:, 1, :], sp[:, 0, :], 0.0, None, ALU.max).then_inc(plus_done, 1)
                dve.wait_ge(plus_done, 2)
                V.scalar_tensor_tensor(sp[:, 2, :], sp[:, 1, :], 2.0, sp[:, 0, :], ALU.mult, ALU.subtract).then_inc(plus_done, 1)
                dve.wait_ge(plus_done, 5)
                V.tensor_tensor(sp[:, 5, :], sp[:, 4, :], sp[:, 1, :], ALU.add).then_inc(plus_done, 1)
                dve.wait_ge(plus_done, 6)
                V.tensor_scalar(sp[:, 6, :], sp[:, 5, :], 0.1, 0.01, ALU.mult, ALU.max).then_inc(plus_done, 1)
                dve.wait_ge(plus_done, 7)
                V.tensor_scalar(tau[:, 0, :], sp[:, 6, :], 1.0, None, ALU.min).then_inc(tau_step, 1)
                for k in range(5):
                    n = 1 << k
                    dve.wait_ge(tau_step, k + 1)
                    if k < 4:
                        V.tensor_tensor(tau[:, k + 1, :], tau[:, k, :], tau[:, k, :], ALU.mult).then_inc(tau_step, 1)
                    if k == 0:
                        V.tensor_scalar(tsum[:, 0, :], tau[:, 0, :], 1.0, None, ALU.add).then_inc(tsum_step, 1)
                    else:
                        dve.wait_ge(tsum_step, k)
                        V.scalar_tensor_tensor(tsum[:, k, :], tau[:, k, :], 1.0, tsum[:, k - 1, :], ALU.add, ALU.mult).then_inc(tsum_step, 1)
                    width = L - 2 * n + 1
                    frm = xT if k == 0 else win[:, (k - 1) % 2]
                    if k > 0:
                        dve.wait_ge(win_step, NPAIR * k)
                    for p in range(NPAIR):
                        V.scalar_tensor_tensor(win[:, k % 2, p, 0:width], frm[:, p, 0:width], tau[:, k, p:p + 1],
                                               frm[:, p, n:n + width], ALU.mult, ALU.add).then_inc(win_step, 1)
                dve.wait_ge(tsum_step, 5)
                V.reciprocal(tsum[:, 5, :], tsum[:, 4, :]).then_inc(tsum_step, 1)
                dve.wait_ge(tsum_step, 6)
                dve.wait_ge(win_step, 5 * NPAIR)
                for p in range(NPAIR):
                    V.tensor_scalar(hT[:, p, :], win[:, 0, p, 0:LOUT], tsum[:, 5, p:p + 1], None, ALU.mult).then_inc(mix_done, 1)


def retention(nc, ps, hT, x2T, epst, const, weight):
    with ExitStack() as ctx:
        def sb(name, shape, dt=F32):
            return ctx.enter_context(nc.sbuf_tensor(name, shape, dt))

        def sem(name):
            return ctx.enter_context(nc.semaphore(name))

        cen = sb("r_cen", [128, NPAIR, LOUT])
        sqr = sb("r_sqr", [128, NPAIR, LOUT])
        rstd = sb("r_rstd", [128, NPAIR, LOUT])
        raw = sb("r_raw", [128, 2, NPAIR, LOUT])
        rcos = sb("r_cos", [128, NPAIR, LOUT])
        rqk = sb("r_qk", [128, 2, NPAIR, LOUT])
        rv = sb("r_v", [128, NT, NPAIR * 128])
        dec = sb("r_dec", [128, 2, NT, LOUT])

        mean_mm, cen_done, sqr_done, var_mm, std_done, rstd_done, ln_done = (
            sem("r_mean_mm"), sem("r_cen"), sem("r_sqr"), sem("r_var_mm"), sem("r_std"), sem("r_rstd"), sem("r_ln"))
        raw_mm, raw_ready, rot_mm, cos_done, sin_done, rot_ready = (
            sem("r_raw_mm"), sem("r_raw_ready"), sem("r_rot_mm"), sem("r_cos"), sem("r_sin"), sem("r_rot"))
        v_mm, v_ready, score_mm, dec_ready, ret_mm, ret_done = (
            sem("r_v_mm"), sem("r_v_ready"), sem("r_score_mm"), sem("r_dec"), sem("r_ret_mm"), sem("r_ret"))

        def flat(a):
            return a.rearrange("p a s -> p (a s)")

        with nc.Block() as block:

            @block.tensor
            def _(pe):
                def layer_norm(k, ready, first):
                    for p in range(NPAIR):
                        if ready is not None:
                            pe.wait_ge(ready, first + 2 * p)
                        nc.tensor.matmul(ps[:, p, 0:LOUT], const("mean"), hT[:, p, :], start=True, stop=True).then_inc(mean_mm, 1)
                    for p in range(NPAIR):
                        pe.wait_ge(sqr_done, NPAIR * k + p + 1)
                        nc.tensor.matmul(ps[:, 4 + p, 0:LOUT], const("mean"), sqr[:, p, :], start=True, stop=True).then_inc(var_mm, 1)

                layer_norm(0, None, 0)
                for w in range(2):
                    for p in range(NPAIR):
                        pe.wait_ge(ln_done, p + 1)
                        if w == 1:
                            pe.wait_ge(std_done, NPAIR)
                        nc.tensor.matmul(ps[:, 4 * w + p, 0:LOUT], weight(("rq", "rk")[w]), x2T[:, p, :],
                                         start=True, stop=True).then_inc(raw_mm, 1)
                for w in range(2):
                    for p in range(NPAIR):
                        pe.wait_ge(raw_ready, NPAIR * w + p + 1)
                        nc.tensor.matmul(ps[:, 4 * w + p, 0:LOUT], const("rot"), raw[:, w, p, :],
                                         start=True, stop=True).then_inc(rot_mm, 1)
                for t, (t0, n) in enumerate(TT):
                    pe.wait_ge(sin_done, t + 1)
                    for p in range(NPAIR):
                        mm = nc.tensor.matmul(ps[0:n, t, 128 * p:128 * p + 128], x2T[:, p, t0:t0 + n], weight("rv"),
                                              start=True, stop=True)
                    mm.then_inc(v_mm, 1)

                def scores(b):
                    p, rows = b // 2, slice(64 * (b % 2), 64 * (b % 2) + 64)
                    pe.wait_ge(rot_ready, NPAIR + p + 1)
                    if b == 0:
                        pe.wait_ge(v_ready, NT)
                        pe.wait_ge(sin_done, 2 * NPAIR)
                    if b >= 2:
                        pe.wait_ge(dec_ready, NT * (b - 1))
                    for t, (t0, n) in enumerate(TT):
                        nc.tensor.matmul(ps[0:n, 3 * (b % 2) + t, 0:LOUT - t0], rqk[rows, 1, p, t0:t0 + n],
                                         rqk[rows, 0, p, t0:LOUT], start=True, stop=True).then_inc(score_mm, 1)

                def mix(b):
                    p, b2 = b // 2, b % 2
                    pe.wait_ge(dec_ready, NT * (b + 1))
                    if b >= 2:
                        pe.wait_ge(ret_done, b - 1)
                    for t, (t0, n) in enumerate(TT):
                        mm = nc.tensor.matmul(ps[64 * b2:64 * b2 + 64, 6 + b2, t0:LOUT],
                                              rv[0:n, t, 128 * p + 64 * b2:128 * p + 64 * b2 + 64],
                                              dec[0:n, b2, t, 0:LOUT - t0], start=(t == 0), stop=(t == NT - 1))
                    mm.then_inc(ret_mm, 1)

                scores(0)
                for b in range(B):
                    if b + 1 < B:
                        scores(b + 1)
                    mix(b)
                layer_norm(1, ret_done, 2)

            @block.scalar
            def _(act):
                def deviations(k):
                    for p in range(NPAIR):
                        act.wait_ge(cen_done, NPAIR * k + p + 1)
                        nc.scalar.activation(sqr[:, p, :], cen[:, p, :], ACT.Square).then_inc(sqr_done, 1)
                    for p in range(NPAIR):
                        act.wait_ge(var_mm, NPAIR * k + p + 1)
                        nc.scalar.activation(rstd[:, p, :], ps[:, 4 + p, 0:LOUT], ACT.Sqrt, bias=epst[:, :]).then_inc(std_done, 1)

                deviations(0)
                for w in range(2):
                    for p in range(NPAIR):
                        act.wait_ge(raw_mm, NPAIR * w + p + 1)
                        nc.scalar.activation(raw[:, w, p, :], ps[:, 4 * w + p, 0:LOUT], ACT.Copy).then_inc(raw_ready, 1)
                for t, (t0, n) in enumerate(TT):
                    act.wait_ge(v_mm, t + 1)
                    nc.scalar.activation(rv[0:n, t, :], ps[0:n, t, :], ACT.Copy).then_inc(v_ready, 1)
                deviations(1)

            @block.gpsimd
            def _(pool):
                for w in range(2):
                    for p in range(NPAIR):
                        pool.wait_ge(raw_ready, NPAIR * w + p + 1)
                        if w == 1:
                            pool.wait_ge(rot_ready, p + 1)
                        nc.gpsimd.tensor_tensor(rcos[:, p, :], raw[:, w, p, :], const("cos"), ALU.mult).then_inc(cos_done, 1)

            @block.vector
            def _(dve):
                V = nc.vector

                def layer_norm(k):
                    for p in range(NPAIR):
                        dve.wait_ge(mean_mm, NPAIR * k + p + 1)
                        V.tensor_tensor(cen[:, p, :], hT[:, p, :], ps[:, p, 0:LOUT], ALU.subtract).then_inc(cen_done, 1)
                    for p in range(NPAIR):
                        dve.wait_ge(std_done, NPAIR * k + p + 1)
                        V.reciprocal(rstd[:, p, :], rstd[:, p, :]).then_inc(rstd_done, 1)
                        dve.wait_ge(rstd_done, NPAIR * k + p + 1)
                        V.tensor_tensor(x2T[:, p, :], cen[:, p, :], rstd[:, p, :], ALU.mult).then_inc(ln_done, 1)

                layer_norm(0)
                for w in range(2):
                    for p in range(NPAIR):
                        dve.wait_ge(rot_mm, NPAIR * w + p + 1)
                        dve.wait_ge(cos_done, NPAIR * w + p + 1)
                        V.tensor_tensor(raw[:, w, p, :], ps[:, 4 * w + p, 0:LOUT], const("sin"), ALU.mult).then_inc(sin_done, 1)
                        dve.wait_ge(sin_done, NPAIR * w + p + 1)
                        V.tensor_tensor(rqk[:, w, p, :], raw[:, w, p, :], rcos[:, p, :], ALU.add).then_inc(rot_ready, 1)

                def decay(b):
                    for t, (t0, n) in enumerate(TT):
                        dve.wait_ge(score_mm, NT * b + t + 1)
                        if b >= 2:
                            dve.wait_ge(ret_mm, b - 1)
                        V.tensor_tensor(dec[0:n, b % 2, t, 0:LOUT - t0], ps[0:n, 3 * (b % 2) + t, 0:LOUT - t0],
                                        const("decay")[0:n, 0:LOUT - t0], ALU.mult).then_inc(dec_ready, 1)

                def add(b):
                    rows = slice(64 * (b % 2), 64 * (b % 2) + 64)
                    dve.wait_ge(ret_mm, b + 1)
                    V.tensor_tensor(hT[rows, b // 2, :], hT[rows, b // 2, :], ps[rows, 6 + b % 2, 0:LOUT], ALU.add).then_inc(ret_done, 1)

                for b in range(B):
                    decay(b)
                    if b >= 1:
                        add(b - 1)
                add(B - 1)
                layer_norm(1)


def product_key_attention(nc, ps, hT, x2T, const, pkw, wq, wo, tables, out):
    with ExitStack() as ctx:
        def sb(name, shape, dt=F32):
            return ctx.enter_context(nc.sbuf_tensor("k_" + name, shape, dt))

        def sem(name):
            return ctx.enter_context(nc.semaphore("k_" + name))

        NDC = NCH // 2
        WINDOW = (0, 2, 3, 1)
        MID0, MID1 = 6, 7

        tab = sb("tab", [128, 2, NCH, 128])
        wqh = sb("wqh", [64, 2, D])
        wos = sb("wos", [64, H, D])
        pkw_sb = sb("pkw_sb", [DKEY, 16, 128])
        wf = sb("wf", [64, H + 1, 2, NKEY])
        sel = sb("sel", [128, 2, 8, 128], F16)
        eye16 = sb("eye16", [128, 128], F16)
        eyeb = sb("eyeb", [128, 128], BF16)
        causb = sb("causb", [128, 128], BF16)
        y = sb("y", [128, B, NT, D])
        xs = sb("xs", [64, 2, LOUT])
        sS = sb("sS", [128, NT, 2, NKEY])
        rp = sb("rp", [128, NT, 2, NKEY])
        top = sb("top", [128, NT, 2, TOPK])
        cand = sb("cand", [128, NT, NCAND])
        rc = sb("rc", [128, NT, NCAND])
        fin = sb("fin", [128, NT, TOPK])
        small = sb("small", [128, 6, NT])
        off = sb("off", [128, NT, 2])
        ecs = sb("ecs", [128, NT, NCAND])
        zs = sb("zs", [128, NT])
        gain = sb("gain", [128, 2, NT])
        aS = sb("aS", [128, NT, 2, 2, 32])
        spl = sb("spl", [128, NT, 5, 2, 32], F16)
        X = sb("X", [128, 2, 4, LOUT], F16)
        W = sb("W", [128, 4, 2, LOUT])
        kvs = sb("kvs", [128, LOUT])
        kv = sb("kv", [128, NT, 128])
        kT = sb("kT", [64, LOUT])
        qT = sb("qT", [64, 2, LOUT])
        P = sb("P", [128, NT, LOUT])
        nmax = sb("nmax", [128, NT])
        zz = sb("zz", [128, NT])
        rz = sb("rz", [128, NT])
        PT = sb("PT", [128, NT, LOUT])
        oT = sb("oT", [64, LOUT])

        s_tab = [sem("s_tab0"), sem("s_tab1")]
        s_load, s_out, passed = sem("s_load"), sem("s_out"), sem("passed")
        cast_done, zeroed, wf_mm, wf_ready, y_mm0, y_ready0 = (
            sem("cast_done"), sem("zeroed"), sem("wf_mm"), sem("wf_ready"), sem("y_mm0"), sem("y_ready0"))
        xs_ready, sim_mm, sim_ready, top_step, thr_ready, ecs_ready, z_done, rz_z, gain_ready = (
            sem("xs_ready"), sem("sim_mm"), sem("sim_ready"), sem("top_step"), sem("thr_ready"), sem("ecs_ready"),
            sem("z_done"), sem("rz_z"), sem("gain_ready"))
        a_step, low_step, high_ready, low_ready, x_mm, x_ready = (
            sem("a_step"), sem("low_step"), sem("high_ready"), sem("low_ready"), sem("x_mm"), sem("x_ready"))
        log_mm, e_done, w_done, main_done = sem("log_mm"), sem("e_done"), sem("w_done"), sem("main_done")
        kvs_ready, kvt_mm, kv_ready, kt_mm, kT_ready, q_mm, qT_ready = (
            sem("kvs_ready"), sem("kvt_mm"), sem("kv_ready"), sem("kt_mm"), sem("kT_ready"), sem("q_mm"), sem("qT_ready"))
        s_mm, nmax_done, p_done, rz_ready, pn_ready, pt_mm, pt_ready, pt1_ready = (
            sem("s_mm"), sem("nmax_done"), sem("p_done"), sem("prz_ready"), sem("pn_ready"), sem("ppt_mm"),
            sem("ppt_ready"), sem("pt1_ready"))
        o_mm, oT_ready, y_mm, y_done = sem("o_mm"), sem("poT_ready"), sem("y_mm"), sem("y_done")
        AHEAD = {q_mm: 1, gain_ready: 1, main_done: 4, kvs_ready: 1, y_done: 1}

        def ahead(s):
            return AHEAD[s]

        def wait_alone(eng, s, value):
            eng.wait_ge(s, value)
            eng.sem_inc(passed, 1)

        def score_area(t, pj):
            return ((4 + pj, 0), (4 + pj, 128), (MID1, 0))[t]

        def rounds(eng, body):
            with eng.Fori(0, H // 2) as hh:
                for slot in range(2):
                    body.head(hh, slot)
                    with eng.Fori(0, NPAIR) as pair:
                        for par in range(2):
                            g = hh * 8 + pair + 4 * slot
                            i = hh * 16 + pair * 2 + (8 * slot + par)
                            body.item(i, slot, par, g, pair)

        with nc.Block() as block:

            @block.sync
            def _(sync):
                def load(slot, head):
                    if isinstance(head, int):
                        t, q = tables[head], wq[:, head, :]
                        sync.dma_start(tab[:, slot, :, :], t).then_inc(s_tab[slot], 16)
                        sync.dma_start(wqh[:, slot, :], q).then_inc(s_tab[slot], 16)
                    else:
                        sync.dma_start(tab[:, slot, :, :], tables[bass.ds(head, 1)].rearrange("a p c d -> p (a c) d")).then_inc(s_tab[slot], 16)
                        sync.dma_start(wqh[:, slot, :], wq[:, bass.ds(head, 1), :].rearrange("p a d -> p (a d)")).then_inc(s_tab[slot], 16)

                for s, n in AHEAD.items():
                    sync.sem_inc(s, n)
                sync.dma_start(pkw_sb[:, :, :].rearrange("p a b -> p (a b)"), pkw).then_inc(s_load, 16)
                sync.dma_start(wos[:, :, :], wo).then_inc(s_load, 16)
                load(0, 0)
                load(1, 1)
                with sync.Fori(0, H // 2 - 1) as hh:
                    for slot in range(2):
                        wait_alone(sync, main_done, hh * (16 * NDC) + (8 * NDC * (slot + 1) + ahead(main_done)))
                        wait_alone(sync, q_mm, hh * 16 + (8 * (slot + 1) + ahead(q_mm)))
                        load(slot, hh * 2 + (slot + 2))

            @block.tensor
            def _(pe):
                mm_, tr_ = nc.tensor.matmul, nc.tensor.transpose
                eye = const("eye")

                def similarities(n, par, head):
                    wait_alone(pe, xs_ready, n + 1)
                    for t, (t0, m) in enumerate(TT):
                        rhs = (wf[:, head, :, :] if isinstance(head, int) else wf[:, bass.ds(head, 1), :, :].rearrange("p a b k -> p (a b) k"))
                        mm = mm_(ps[0:m, MID0, 128 * t:128 * t + 128], xs[:, par, t0:t0 + m], rhs, start=True, stop=True)
                    mm.then_inc(sim_mm, 1)

                def turn_scores(n, r):
                    if r == 0:
                        pe.wait_ge(low_ready, n + 1)
                    else:
                        pe.wait_ge(x_ready, 2 * n + 1)
                    bank = ps[:, MID0, :].bitcast(F16)
                    for k in range(2):
                        for t, (t0, m) in enumerate(TT):
                            mm = tr_(bank[:, LOUT * k + t0:LOUT * k + t0 + m],
                                     spl[0:m, t, 2 * r + k:2 * r + k + 2, :, :].rearrange("p b x j -> p (b x j)"), eye16[0:m, 0:m])
                    mm.then_inc(x_mm, 1)

                def log_weights(i, par, d):
                    for k in range(2):
                        c = 2 * d + k
                        mm = mm_(ps[:, 2 * (d % 2) + k, 0:LOUT], sel[:, (c // 8) % 2, c % 8, :], X[:, par, c // 8, :], start=True, stop=True)
                    mm.then_inc(log_mm, 1)

                def table_sum(i, slot, par, d):
                    for k in range(2):
                        c = 2 * d + k
                        mm = mm_(ps[:, 4 + par, 0:LOUT], tab[:, slot, 8 * WINDOW[c // 8] + c % 8, :], W[:, d % 4, k, :], start=(c == 0), stop=(c == NCH - 1))
                    mm.then_inc(main_done, 1)

                def turn_kv(i):
                    pe.wait_ge(y_done, i + ahead(y_done))
                    pe.wait_ge(kvs_ready, i + (1 + ahead(kvs_ready)))
                    for t, (t0, m) in enumerate(TT):
                        mm = tr_(ps[0:m, MID1, 128 * t:128 * t + 128], kvs[:, t0:t0 + m], eye)
                    mm.then_inc(kvt_mm, 1)

                def turn_keys(i):
                    wait_alone(pe, kv_ready, i + 1)
                    for t, (t0, m) in enumerate(TT):
                        mm = tr_(ps[0:64, MID1, t0:t0 + m], kv[0:m, t, 0:64], eye[0:m, 0:m])
                    mm.then_inc(kt_mm, 1)

                def queries(i, slot, par, pj):
                    mm_(ps[0:64, 4 + pj, 0:LOUT], wqh[:, slot, :], xs[:, par, :], start=True, stop=True).then_inc(q_mm, 1)

                def attention_scores(i, pj, last=False):
                    if not last:
                        pe.wait_ge(qT_ready, i + 1)
                    wait_alone(pe, kT_ready, i + 1)
                    for t, (t0, m) in enumerate(TT):
                        keys = t0 + m
                        bank, c0 = score_area(t, pj)
                        mm_(ps[0:m, bank, c0:c0 + keys], qT[:, pj, t0:t0 + m], kT[:, 0:keys], start=True, stop=False)
                        mm = mm_(ps[0:m, bank, c0 + t0:c0 + keys], eyeb[0:m, 0:m], causb[0:m, 0:m], start=False, stop=True)
                    mm.then_inc(s_mm, 1)

                def turn_probabilities(i, pj):
                    pe.wait_ge(p_done, i + 1)
                    for kt, (k0, kn) in enumerate(TT):
                        bank, c0 = ((MID1, 0), (4 + pj, 0), (MID1, LOUT))[kt]
                        for t, (t0, m) in enumerate(TT):
                            if t >= kt:
                                mm = tr_(ps[0:kn, bank, c0 + t0 - k0:c0 + t0 - k0 + m], P[0:m, t, k0:k0 + kn], eye[0:m, 0:m])
                    mm.then_inc(pt_mm, 1)

                def attention_output(i):
                    pe.wait_ge(pt_ready, i + 1)
                    pe.wait_ge(pt1_ready, i + 1)
                    for kt, (k0, kn) in enumerate(TT):
                        mm = mm_(ps[0:64, MID1, k0:LOUT], kv[0:kn, kt, 64:128], PT[0:kn, kt, 0:LOUT - k0], start=(kt == 0), stop=(kt == NT - 1))
                    mm.then_inc(o_mm, 1)

                def project(i, head):
                    wait_alone(pe, oT_ready, i + 1)
                    rhs = wos[:, head, :] if isinstance(head, int) else wos[:, bass.ds(head, 1), :].rearrange("p a d -> p (a d)")
                    for t, (t0, m) in enumerate(TT):
                        mm = mm_(ps[0:m, MID1, 64 * t:64 * t + 64], oT[:, t0:t0 + m], rhs, start=True, stop=True)
                    mm.then_inc(y_mm, 1)

                pe.wait_ge(s_load, 32)
                for p in range(2):
                    for h in range(H):
                        mm = mm_(ps[0:64, p, 64 * h:64 * h + 64], pkw_sb[:, 8 * p + h, 0:64], pkw_sb[:, 8 * p + h, 64:128], start=True, stop=True)
                    mm.then_inc(wf_mm, 1)
                for t, (t0, m) in enumerate(TT):
                    for p in range(NPAIR):
                        mm = tr_(ps[0:m, 2 + t, 128 * p:128 * p + 128], hT[:, p, t0:t0 + m], eye)
                    mm.then_inc(y_mm0, 1)
                pe.wait_ge(cast_done, 4)
                pe.wait_ge(zeroed, 6)
                pe.wait_ge(wf_ready, 3)
                similarities(0, 0, 0)
                turn_scores(0, 0)
                turn_scores(0, 1)
                pe.wait_ge(y_ready0, NT)
                log_weights(0, 0, 0)
                log_weights(0, 0, 1)
                pe.wait_ge(e_done, 1)
                log_weights(0, 0, 2)
                pe.wait_ge(x_ready, 2)
                similarities(1, 1, 0)

                class Body:
                    @staticmethod
                    def head(hh, slot):
                        wait_alone(pe, s_tab[slot], hh * 32 + 32)

                    @staticmethod
                    def item(i, slot, par, g, pair):
                        nj = 1 - par
                        for d in range(NDC):
                            pe.wait_ge(e_done, i * NDC + (d + 2))
                            if d + 3 < NDC:
                                log_weights(i, par, d + 3)
                            else:
                                if d == NDC - 3:
                                    pe.wait_ge(x_ready, i * 2 + 3)
                                log_weights(i + 1, nj, d + 3 - NDC)
                            pe.wait_ge(w_done, i * NDC + (d + 1))
                            table_sum(i, slot, par, d)
                            if d == 1:
                                turn_kv(i)
                            if d == 2:
                                queries(i, slot, par, nj)
                            if d == 3:
                                turn_keys(i)
                            if d == 5:
                                attention_scores(i, nj)
                            if d == 8:
                                turn_probabilities(i, nj)
                            if d == 10:
                                attention_output(i)
                                turn_scores(i + 1, 0)
                            if d == 12:
                                turn_scores(i + 1, 1)
                                project(i, g // 4 if par else ((g + 31) // 4) % 8)
                            if d == 14:
                                pe.wait_ge(x_ready, i * 2 + 4)
                                similarities(i + 2, par, (g + 1) // 4)

                rounds(pe, Body)
                n = H * B
                turn_kv(n)
                turn_keys(n)
                attention_scores(n, 1, last=True)
                turn_probabilities(n, 1)
                attention_output(n)
                project(n, H - 1)

            @block.scalar
            def _(act):
                A = nc.scalar.activation

                def copy_similarities(n):
                    act.wait_ge(sim_mm, n + 1)
                    A(sS[:, 0:2, :, :], ps[:, MID0, 0:256], ACT.Copy)
                    A(sS[0:88, 2, :, :], ps[0:88, MID0, 256:384], ACT.Copy).then_inc(sim_ready, 1)

                def candidate_weights(n):
                    act.wait_ge(thr_ready, n * 6 + 6)
                    A(ecs[:, :, :], rc[:, :, :], ACT.Exp)
                    A(small[:, 4, :], small[:, 3, :], ACT.Exp).then_inc(ecs_ready, 1)

                def high_part(n):
                    act.wait_ge(a_step, n * 3 + 3)
                    A(spl[:, :, 0:4, 0, :], aS[:, :, :, :, :].rearrange("p t u a j -> p t (u a) j"), ACT.Copy).then_inc(high_ready, 1)

                def copy_turned(n, par, r):
                    act.wait_ge(x_mm, n * 2 + (r + 1))
                    A(X[:, par, 2 * r:2 * r + 2, :], ps[:, MID0, :].bitcast(F16)[:, 0:2 * LOUT], ACT.Copy).then_inc(x_ready, 1)

                def exponentials(i, d):
                    act.wait_ge(main_done, i * NDC + (d - 3 + ahead(main_done)))
                    act.wait_ge(log_mm, i * NDC + (d + 1))
                    A(W[:, d % 4, :, :], ps[:, 2 * (d % 2):2 * (d % 2) + 2, 0:LOUT], ACT.Exp).then_inc(e_done, 1)

                def take_sums(i, pj):
                    act.wait_ge(main_done, i * NDC + ahead(main_done))
                    A(kvs[:, :], ps[:, 4 + pj, 0:LOUT], ACT.Copy).then_inc(kvs_ready, 1)

                def scale_kv(i, pj):
                    act.wait_ge(gain_ready, i + ahead(gain_ready))
                    act.wait_ge(kvt_mm, i + 1)
                    for t, (t0, m) in enumerate(TT):
                        a = A(kv[0:m, t, :], ps[0:m, MID1, 128 * t:128 * t + 128], ACT.Copy, scale=gain[0:m, pj, t:t + 1])
                    a.then_inc(kv_ready, 1)

                def copy_keys(i):
                    act.wait_ge(kt_mm, i + 1)
                    A(kT[:, :], ps[0:64, MID1, 0:LOUT], ACT.Copy).then_inc(kT_ready, 1)

                def copy_queries(i, par, pj):
                    act.wait_ge(q_mm, i + (1 + ahead(q_mm)))
                    A(qT[:, par, :], ps[0:64, 4 + pj, 0:LOUT], ACT.Copy, scale=D ** -0.5).then_inc(qT_ready, 1)

                def probabilities(i, pj):
                    act.wait_ge(nmax_done, i * 3 + 3)
                    for t, (t0, m) in enumerate(TT):
                        bank, c0 = score_area(t, pj)
                        a = A(P[0:m, t, 0:t0 + m], ps[0:m, bank, c0:c0 + t0 + m], ACT.Exp, bias=nmax[0:m, t:t + 1],
                              accum_out=zz[0:m, t:t + 1])
                    a.then_inc(p_done, 1)

                def copy_turned_probabilities(i):
                    act.wait_ge(pt_mm, i + 1)
                    A(PT[:, 0, :], ps[:, MID1, 0:LOUT], ACT.Copy)
                    A(PT[0:88, 2, 0:88], ps[0:88, MID1, LOUT:LOUT + 88], ACT.Copy).then_inc(pt_ready, 1)

                def copy_output(i):
                    act.wait_ge(o_mm, i + 1)
                    A(oT[:, :], ps[0:64, MID1, 0:LOUT], ACT.Copy).then_inc(oT_ready, 1)

                for p in range(2):
                    act.wait_ge(wf_mm, p + 1)
                    A(wf[:, 0:H, p, :], ps[0:64, p, :].rearrange("p (h k) -> p h k", h=H), ACT.Copy).then_inc(wf_ready, 1)
                for t, (t0, m) in enumerate(TT):
                    act.wait_ge(y_mm0, t + 1)
                    A(y[0:m, :, t, :], ps[0:m, 2 + t, :].rearrange("p (b d) -> p b d", b=B), ACT.Copy).then_inc(y_ready0, 1)
                act.wait_ge(zeroed, 6)
                copy_similarities(0)
                candidate_weights(0)
                high_part(0)
                copy_turned(0, 0, 0)

                class Body:
                    @staticmethod
                    def head(hh, slot):
                        pass

                    @staticmethod
                    def item(i, slot, par, g, pair):
                        nj = 1 - par
                        for d in range(NDC):
                            exponentials(i, d)
                            if d == 0:
                                copy_turned(i, par, 1)
                            if d == 2:
                                copy_similarities(i + 1)
                            if d == 3:
                                take_sums(i, nj)
                            if d == 5:
                                scale_kv(i, nj)
                            if d == 6:
                                copy_queries(i, par, nj)
                            if d == 7:
                                copy_keys(i)
                            if d == 10:
                                probabilities(i, nj)
                                candidate_weights(i + 1)
                            if d == 11:
                                high_part(i + 1)
                            if d == 12:
                                copy_turned_probabilities(i)
                            if d == 14:
                                copy_output(i)
                                copy_turned(i + 1, nj, 0)

                rounds(act, Body)
                n = H * B
                exponentials(n, 0)
                copy_turned(n, 0, 1)
                take_sums(n, 1)
                scale_kv(n, 1)
                copy_keys(n)
                probabilities(n, 1)
                copy_turned_probabilities(n)
                copy_output(n)
                act.wait_ge(y_done, n + 1 + ahead(y_done))
                for t, (t0, m) in enumerate(TT):
                    act.dma_start(out[:, t0:t0 + m, :].rearrange("b t d -> t b d"), y[0:m, :, t, :]).then_inc(s_out, 16)
                act.wait_ge(s_out, 16 * NT)

            @block.gpsimd
            def _(pool):
                G = nc.gpsimd

                def centre_scores(n):
                    pool.wait_ge(thr_ready, n * 6 + 6)
                    for a in range(2):
                        G.tensor_tensor(aS[:, :, :, a, :], sS[:, :, a, :].rearrange("p t (u j) -> p t u j", u=2),
                                        off[:, :, a, None, None].to_broadcast([128, NT, 2, 32]), ALU.subtract).then_inc(a_step, 1)
                    wait_alone(pool, a_step, n * 3 + 2)
                    G.tensor_scalar(aS[:, :, :, :, :], aS[:, :, :, :, :], -NEG, FAR, ALU.min, ALU.max).then_inc(a_step, 1)
                    pool.wait_ge(high_ready, n + 1)
                    G.tensor_tensor(spl[:, :, 0:4, 1, :], aS[:, :, :, :, :].rearrange("p t u a j -> p t (u a) j"),
                                    spl[:, :, 0:4, 0, :], ALU.subtract).then_inc(low_step, 1)
                    wait_alone(pool, low_step, n + 1)
                    G.tensor_copy(spl[:, :, 4, :, :], spl[:, :, 0, :, :]).then_inc(low_ready, 1)

                pool.wait_ge(zeroed, 6)
                centre_scores(0)

                class Body:
                    @staticmethod
                    def head(hh, slot):
                        pass

                    @staticmethod
                    def item(i, slot, par, g, pair):
                        centre_scores(i + 1)

                rounds(pool, Body)
            @block.vector
            def _(dve):
                V = nc.vector
                MX, AM, LOW, DT, EDT = 0, 1, 2, 3, 4

                def take_tokens(par, pair):
                    s = x2T[64 * par:64 * par + 64, pair, :] if isinstance(pair, int) else \
                        x2T[64 * par:64 * par + 64, bass.ds(pair, 1), :].rearrange("p a s -> p (a s)")
                    V.tensor_copy(xs[:, par, :], s).then_inc(xs_ready, 1)

                STEPS = 6 + 6 + 6 + 2 + 3 + 3 + 3

                def halves_max(n, second):
                    if second:
                        wait_alone(dve, top_step, n * STEPS + 12)
                    else:
                        wait_alone(dve, sim_ready, n + 1)
                    for t, (t0, m) in enumerate(TT):
                        for p in range(2):
                            o = top[0:m, t, p, 8:16] if second else top[0:m, t, p, 0:8]
                            V.max(o, (rp if second else sS)[0:m, t, p, :]).then_inc(top_step, 1)

                def halves_drop(n):
                    wait_alone(dve, top_step, n * STEPS + 6)
                    for t, (t0, m) in enumerate(TT):
                        for p in range(2):
                            V.match_replace(rp[0:m, t, p, :], top[0:m, t, p, 0:8], sS[0:m, t, p, :], NEG).then_inc(top_step, 1)

                def candidates(n):
                    dve.wait_ge(top_step, n * STEPS + 18)
                    for r, c, lo, hi, k in ((0, 0, 0, 4, 16), (1, 64, 4, 16, 3)):
                        V.tensor_tensor(cand[:, :, c:c + (hi - lo) * k].rearrange("p t (a b) -> p t a b", b=k),
                                        top[:, :, 1, lo:hi, None].to_broadcast([128, NT, hi - lo, k]),
                                        top[:, :, 0, None, 0:k].to_broadcast([128, NT, hi - lo, k]), ALU.add).then_inc(top_step, 1)

                def sums_max(n, second):
                    wait_alone(dve, top_step, n * STEPS + (26 if second else 20))
                    for t in range(NT):
                        o = fin[:, t, 8:16] if second else fin[:, t, 0:8]
                        V.max(o, (rc if second else cand)[:, t, :]).then_inc(top_step, 1)

                def sums_drop(n):
                    wait_alone(dve, top_step, n * STEPS + 23)
                    for t in range(NT):
                        V.match_replace(rc[:, t, :], fin[:, t, 0:8], cand[:, t, :], NEG).then_inc(top_step, 1)

                def threshold(n):
                    dve.wait_ge(top_step, n * STEPS + STEPS)
                    mx = fin[:, :, 0]
                    V.tensor_reduce(small[:, AM, :], top[:, :, :, :].rearrange("p t a k -> p t (a k)"), AX.X, ALU.max,
                                    apply_absolute_value=True).then_inc(thr_ready, 1)
                    V.tensor_tensor(rc[:, :, :], cand[:, :, :], fin[:, :, 0:1].to_broadcast([128, NT, NCAND]), ALU.subtract).then_inc(thr_ready, 1)
                    dve.wait_ge(thr_ready, n * 6 + 1)
                    V.scalar_tensor_tensor(small[:, LOW, :], small[:, AM, :], -DELTA, fin[:, :, 15], ALU.mult, ALU.add).then_inc(thr_ready, 1)
                    dve.wait_ge(thr_ready, n * 6 + 3)
                    V.scalar_tensor_tensor(small[:, MX, :], mx, -80.0, small[:, LOW, :], ALU.add, ALU.max).then_inc(thr_ready, 1)
                    dve.wait_ge(thr_ready, n * 6 + 4)
                    V.tensor_tensor(small[:, DT, :], small[:, MX, :], mx, ALU.subtract)
                    V.tensor_copy(off[:, :, 1], top[:, :, 1, 0]).then_inc(thr_ready, 1)
                    V.tensor_tensor(off[:, :, 0], small[:, MX, :], top[:, :, 1, 0], ALU.subtract).then_inc(thr_ready, 1)

                def softmax_sum(n):
                    dve.wait_ge(ecs_ready, n + 1)
                    for t in range(NT):
                        V.scalar_tensor_tensor(ecs[:, t, :], cand[:, t, :], small[:, MX, t:t + 1], ecs[:, t, :], ALU.is_ge, ALU.mult,
                                               accum_out=zs[:, t:t + 1]).then_inc(z_done, 1)

                def token_gain(n, par):
                    dve.wait_ge(z_done, n * 3 + 3)
                    V.reciprocal(zs[:, :], zs[:, :]).then_inc(rz_z, 1)
                    dve.wait_ge(rz_z, n + 1)
                    V.tensor_tensor(gain[:, par, :], small[:, EDT, :], zs[:, :], ALU.mult).then_inc(gain_ready, 1)

                def weights(i, d):
                    dve.wait_ge(e_done, i * NDC + (d + 1))
                    V.scalar_tensor_tensor(W[:, d % 4, :, :], W[:, d % 4, :, :], 1.0, W[:, d % 4, :, :],
                                           ALU.is_ge, ALU.mult).then_inc(w_done, 1)

                def row_max(i, pj):
                    dve.wait_ge(s_mm, i + 1)
                    for t, (t0, m) in enumerate(TT):
                        bank, c0 = score_area(t, pj)
                        V.tensor_reduce(nmax[0:m, t:t + 1], ps[0:m, bank, c0:c0 + t0 + m], AX.X, ALU.max, negate=True).then_inc(nmax_done, 1)

                def row_sum(i):
                    dve.wait_ge(p_done, i + 1)
                    V.reciprocal(rz[:, :], zz[:, :]).then_inc(rz_ready, 1)

                def copy_turned_probabilities(i, pj):
                    dve.wait_ge(pt_mm, i + 1)
                    V.tensor_copy(PT[:, 1, 0:216], ps[:, 4 + pj, 0:216]).then_inc(pt1_ready, 1)

                def add_output(i, b):
                    dve.wait_ge(y_mm, i + 1)
                    for t, (t0, m) in enumerate(TT):
                        o = y[0:m, b, t, :] if isinstance(b, int) else y[0:m, bass.ds(b, 1), t, :].rearrange("p a d -> p (a d)")
                        a = V.scalar_tensor_tensor(o, ps[0:m, MID1, 64 * t:64 * t + 64], rz[0:m, t:t + 1], o, ALU.mult, ALU.add)
                    a.then_inc(y_done, 1)

                def cast(o, name):
                    V.tensor_copy(o, const(name)).then_inc(cast_done, 1)

                cast(sel[:, :, :, :].rearrange("p w c m -> p (w c m)"), "sel")
                cast(eye16[:, :], "eye")
                cast(eyeb[:, :], "eye")
                cast(causb[:, :], "causal")
                V.memset(wf[:, H, :, :], 0.0).then_inc(wf_ready, 1)
                V.memset(ps[:, 5, :], 0.0).then_inc(zeroed, 1)
                V.memset(qT[:, 1, :], 0.0).then_inc(zeroed, 1)
                V.memset(sS[:, 2, :, :], 0.0).then_inc(zeroed, 1)
                V.memset(top[:, 2, :, :], 0.0).then_inc(zeroed, 1)
                V.memset(gain[:, :, :], 0.0).then_inc(zeroed, 1)
                V.memset(zz[:, :], 1.0).then_inc(zeroed, 1)
                dve.wait_ge(zeroed, 6)
                take_tokens(0, 0)
                take_tokens(1, 0)
                halves_max(0, False)
                halves_drop(0)
                halves_max(0, True)
                candidates(0)
                sums_max(0, False)
                sums_drop(0)
                sums_max(0, True)
                threshold(0)
                softmax_sum(0)
                token_gain(0, 0)

                class Body:
                    @staticmethod
                    def head(hh, slot):
                        pass

                    @staticmethod
                    def item(i, slot, par, g, pair):
                        nj = 1 - par
                        for d in range(NDC):
                            weights(i, d)
                            if d == 2:
                                halves_max(i + 1, False)
                            if d == 3:
                                halves_drop(i + 1)
                            if d == 4:
                                halves_max(i + 1, True)
                            if d == 5:
                                candidates(i + 1)
                                sums_max(i + 1, False)
                            if d == 6:
                                sums_drop(i + 1)
                                sums_max(i + 1, True)
                            if d == 7:
                                threshold(i + 1)
                            if d == 8:
                                row_max(i, nj)
                            if d == 9:
                                dve.wait_ge(q_mm, i + 1 + ahead(q_mm))
                                take_tokens(par, (pair + 1) % 4)
                            if d == 10:
                                row_sum(i)
                            if d == 11:
                                copy_turned_probabilities(i, nj)
                            if d == 12:
                                softmax_sum(i + 1)
                            if d == 13:
                                token_gain(i + 1, nj)
                            if d == 15:
                                add_output(i, pair * 2 if par else ((pair + 3) % 4) * 2 + 1)

                rounds(dve, Body)
                n = H * B
                row_max(n, 1)
                row_sum(n)
                copy_turned_probabilities(n, 1)
                add_output(n, B - 1)


def _constants():
    c = np.zeros((128, NCONST), np.float32)

    def put(name, a):
        lo, hi = CONST[name]
        a = np.asarray(a, np.float64 if a.dtype == np.float64 else np.float32)
        c[:a.shape[0], lo:hi] = a.reshape(a.shape[0], -1)

    l = np.arange(L).reshape(XCH, XROWS)[:, :, None]
    ang = 2.0 * np.pi * ((l * np.arange(NF)[None, None, :]) % L) / L
    put("dft", np.concatenate([np.cos(ang), np.sin(ang)], 2).transpose(1, 0, 2))
    pos = np.arange(S)[:, None].astype(np.float64)
    div = np.exp(np.arange(0, D, 2) * (-np.log(10000.0) / D))
    pe = np.zeros((S, D), np.float32)
    pe[:, 0::2] = np.sin(pos * div)
    pe[:, 1::2] = np.cos(pos * div)
    put("pe", np.concatenate([pe.T, pe.T], 0))
    put("eye", np.eye(128, dtype=np.float32))
    p = np.arange(128)
    put("mean", (p[:, None] // D == p[None, :] // D) / np.float32(D))
    put("head", ((p[:, None] % D) // DH == np.arange(H)[None, :]).astype(np.float32))
    put("batch_head", (p[:, None] // DH == np.arange(2 * H)[None, :]).astype(np.float32))
    rot = np.zeros((128, 128), np.float32)
    rot[p[1::2], p[0::2]] = -1.0
    rot[p[0::2], p[1::2]] = 1.0
    put("rot", rot)
    inv = (np.float32(1.0) / np.float32(10000.0) ** (np.arange(0, D, 2, dtype=np.float32) / np.float32(D))).astype(np.float32)
    angles = np.arange(LOUT, dtype=np.float32)[None, :] * np.repeat(inv, 2)[:, None]
    put("cos", np.tile(np.cos(angles), (2, 1)))
    put("sin", np.tile(np.sin(angles), (2, 1)))
    diff = np.arange(LOUT)[None, :] - p[:, None]
    put("decay", np.where(diff >= 0, np.exp(np.maximum(diff, 0).astype(np.float32) * np.float32(np.log(0.96875))), 0.0).astype(np.float32))
    put("causal", np.where(p[None, :] > p[:, None], -1.0e30, 0.0).astype(np.float32))
    m = np.arange(128)
    sel = np.zeros((128, 2, 8, 128), np.float32)
    for swapped in range(2):
        for c8 in range(8):
            for part in (0, 32):
                sel[64 * swapped + part + m % 32, swapped, c8, m] = 1.0
                sel[64 * (1 - swapped) + part + 4 * c8 + m // 32, swapped, c8, m] = 1.0
    put("sel", sel)
    return c


def _pair(w):
    z = np.zeros((128, 128), w.dtype)
    z[:64, :64] = w
    z[64:, 64:] = w
    return z


def _twice(w):
    return np.concatenate([w, w], 0)


def _arrays(i):
    t = {k[7:]: np.asarray(v) for k, v in i.items() if k.startswith("L0_tok_")}
    x = np.asarray(i["x"])
    a = {}
    a["consts"] = _constants()
    a["xrows"] = x.reshape(B, XCH, XROWS, D).transpose(2, 1, 0, 3)
    a["xcols"] = x.transpose(0, 2, 1).reshape(NPAIR, 128, L).transpose(1, 0, 2)
    li, mi = t["l_in_w"], t["m_in_w"]
    blocks = {
        "q1": _pair(li[:D].T), "k1": _pair(li[D:2 * D].T), "v1": _pair(li[2 * D:].T), "o1": _pair(t["l_out_w"].T),
        "q2": _pair(mi[:D].T), "k2": _pair(mi[D:2 * D].T), "v2": _pair(mi[2 * D:].T), "o2": _pair(t["m_out_w"].T),
        "f1": _twice(t["ff_w1"].T), "f2": t["ff_w2"].T.reshape(2, 128, D).transpose(1, 0, 2).reshape(128, 2 * D),
        "rq": _pair(np.asarray(i["L0_attn_W_Q"])), "rk": _pair(np.asarray(i["L0_attn_W_K"])),
        "rv": _pair(np.asarray(i["L0_attn_W_V"])),
    }
    a["weights"] = np.concatenate([blocks[n] for n in WT], 1)
    lb, mb = t["l_in_b"], t["m_in_b"]
    cols = {
        "bq1": lb[:D], "bk1": lb[D:2 * D], "bv1": lb[2 * D:], "bo1": t["l_out_b"], "g1": t["ln1_g"], "b1": t["ln1_b"],
        "fb1a": t["ff_b1"][:128], "fb1b": t["ff_b1"][128:], "fb2": t["ff_b2"], "g2": t["ln2_g"], "b2": t["ln2_b"],
        "bq2": mb[:D], "bk2": mb[D:2 * D], "bv2": mb[2 * D:], "bo2": t["m_out_b"],
    }
    a["biases"] = np.stack([cols[n] if cols[n].size == 128 else _twice(cols[n]) for n in BIAS], 1)
    wpk = np.asarray(i["L0_ffn_Wq_pk"]).reshape(D, 2, H, DKEY).transpose(3, 1, 2, 0)
    pk = np.asarray(i["L0_ffn_pk_keys"]).transpose(3, 0, 2, 1)
    a["pkw"] = np.concatenate([wpk, pk], 3).reshape(DKEY, 16 * 128)
    a["wq"] = np.asarray(i["L0_ffn_Wq"]).reshape(D, H, D)
    a["wo"] = np.asarray(i["L0_ffn_Wo"]).reshape(H, D, D).transpose(1, 0, 2)
    tab = np.concatenate([np.asarray(i["L0_ffn_keys_table"]), np.asarray(i["L0_ffn_values_table"])], 1)
    tab = tab.reshape(H, 2, 8, 4, 2, 32, 128)
    a["tables"] = tab.transpose(0, 3, 5, 4, 1, 2, 6).reshape(H, 128, NCH, 128)
    return {k: np.ascontiguousarray(v) for k, v in a.items()}


def kernel(**inputs):
    import concourse.bacc as _bacc
    from concourse.bass_utils import run_bass_kernel_spmd as _run

    nc = _bacc.Bacc("TRN2", target_bir_lowering=False, num_devices=1)
    arrays, args = {}, {}
    for name, a in _arrays(inputs).items():
        arrays[f"in_{name}"] = a
        args[name] = nc.dram_tensor(f"in_{name}", a.shape, mybir.dt.from_np(a.dtype), kind="ExternalInput").ap()
    args["out"] = nc.dram_tensor("out_0", (B, LOUT, D), F32, kind="ExternalOutput").ap()
    audio_tower(nc, **args)
    r = _run(nc, [arrays], core_ids=[0])
    return r.results[0]["out_0"]
```

```python
from contextlib import ExitStack

import concourse.bass as bass
from concourse import mybir
import numpy as np

ALU = mybir.AluOpType
ACT = mybir.ActivationFunctionType
AX = mybir.AxisListType
F32 = mybir.dt.float32
F32R = mybir.dt.float32r
F16 = mybir.dt.float16
BF16 = mybir.dt.bfloat16

B, L, D = 8, 375, 64
NPAIR = B // 2
KSIZE = 32
LOUT = L - KSIZE + 1
NF = L // 2 + 1
S = NF + 1
XCH = 3
XROWS = L // XCH
H = 8
DH = D // H
QT = ((0, 95), (95, 94))
EPS = 1e-5
TT = ((0, 128), (128, 128), (256, 88))
NT = len(TT)
DFF = 4 * D
NKEY = 64
TOPK = 16
DKEY = 32
NCH = NKEY * NKEY // 128
NCAND = 100
NEG = -3.0e38
FAR = -30000.0
DELTA = 5e-7

CONST = {}
_at = 0
for _n, _w in (("dft", XCH * 2 * NF), ("pe", S), ("eye", 128), ("mean", 128), ("batch_head", 2 * H), ("rot", 128),
               ("cos", LOUT), ("sin", LOUT), ("decay", LOUT), ("causal", 128), ("sel", 2 * 8 * 128)):
    CONST[_n] = (_at, _at + _w)
    _at += _w
NCONST = _at
WT = {}
_at = 0
for _n, _w in (("q1", 128), ("k1", 128), ("v1", 128), ("o1", 128), ("q2", 128), ("k2", 128), ("v2", 128),
               ("o2", 128), ("f1", DFF), ("f2", 2 * D), ("rq", 128), ("rk", 128), ("rv", 128)):
    WT[_n] = (_at, _at + _w)
    _at += _w
NWT = _at
BIAS = {n: i for i, n in enumerate(("bq1", "bk1", "bv1", "bo1", "g1", "b1", "fb1a", "fb1b", "fb2", "g2", "b2",
                                    "bq2", "bk2", "bv2", "bo2"))}
NBIAS = len(BIAS)


def audio_tower(nc, consts, xrows, xcols, weights, biases, pkw, wq, wo, tables, out):
    with ExitStack() as ctx:
        def sb(name, shape, dt=F32):
            return ctx.enter_context(nc.sbuf_tensor(name, shape, dt))

        ps = ctx.enter_context(nc.psum_tensor("ps", [128, 8, 512], F32))
        hT = sb("hT", [128, NPAIR, LOUT])
        cst = sb("cst", [128, NCONST])
        wts = sb("wts", [128, NWT])
        bia = sb("bia", [128, NBIAS])
        epst = sb("epst", [128, 1])
        x2T = sb("x2T", [128, NPAIR, LOUT])

        def const(name):
            return cst[:, CONST[name][0]:CONST[name][1]]

        def weight(name):
            return wts[:, WT[name][0]:WT[name][1]]

        def bias(name):
            return bia[:, BIAS[name]:BIAS[name] + 1]

        token_mixer(nc, ps, hT, const, weight, bias, epst, cst, wts, bia, consts, xrows, xcols, weights, biases)
        retention(nc, ps, hT, x2T, epst, const, weight)
        product_key_attention(nc, ps, hT, x2T, const, pkw, wq, wo, tables, out)


def token_mixer(nc, ps, hT, const, weight, bias, epst, cst, wts, bia, consts, xrows, xcols, weights, biases):
    with ExitStack() as ctx:
        def sb(name, shape, dt=F32):
            return ctx.enter_context(nc.sbuf_tensor(name, shape, dt))

        def sem(name):
            return ctx.enter_context(nc.semaphore(name))

        xr = sb("xr", [XROWS, XCH, B * D])
        xT = sb("xT", [128, NPAIR, L])
        sq = sb("sq", [128, NPAIR, 2 * NF])
        amp = sb("amp", [128, NPAIR, NF])
        src = sb("src", [128, NPAIR, S])
        qT = sb("qT", [128, NPAIR, S])
        kT = sb("kT", [128, NPAIR, S])
        vt = sb("vt", [95, 2, NPAIR * 128])
        qz = sb("qz", [128, 2, 2, H, S])
        kp = sb("kp", [128, 2, S])
        vz = sb("vz", [95, 2, 2, H * (128 + DH)])
        negmax = sb("negmax", [95, 2, 4])
        ebias = sb("ebias", [95, 2, 4])
        P = sb("P", [95, 4, 4, S])
        Z = sb("Z", [95, 4, 4])
        rz = sb("rz", [95, 4, 4])
        PT = sb("PT", [95, 2, 2, 4 * 95])
        oT = sb("oT", [128, NPAIR, S])
        x1 = sb("x1", [128, NPAIR, S])
        cen = sb("cen", [128, NPAIR, S])
        sqr = sb("sqr", [128, NPAIR, S])
        rstd = sb("rstd", [128, NPAIR, S])
        hff = sb("hff", [128, 2, 2, NPAIR * S])
        q2 = sb("q2", [128, NPAIR])
        q2z = sb("q2z", [128, NPAIR, 32])
        s2 = sb("s2", [128, S])
        m2 = sb("m2", [128, 2])
        z2 = sb("z2", [128, 2])
        p2T = sb("p2T", [95, 2, 128])
        om = sb("om", [128, NPAIR, 2 * H])
        o2 = sb("o2", [128, NPAIR])
        sp = sb("sp", [128, 8, NPAIR])
        tau = sb("tau", [128, 5, NPAIR])
        tsum = sb("tsum", [128, 6, NPAIR])
        win = sb("win", [128, 2, NPAIR, L])

        s_const, s_dft, s_sel, s_x, s_xT, s_w = sem("s_const"), sem("s_dft"), sem("s_sel"), sem("s_x"), sem("s_xT"), sem("s_w")
        dft_done, sq_done, power_done, amp_done = sem("dft_done"), sem("sq_done"), sem("power_done"), sem("amp_done")
        last_done, src_done = sem("last_done"), sem("src_done")
        qk_mm, v_mm, q_ready, k_ready, v_ready = sem("qk_mm"), sem("v_mm"), sem("q_ready"), sem("k_ready"), sem("v_ready")
        qz_ready, score_done, max_done, ebias_done = sem("qz_ready"), sem("score_done"), sem("max_done"), sem("ebias_done")
        exp_done, ptr_done, pt0_ready, pt1_ready = sem("exp_done"), sem("ptr_done"), sem("pt0_ready"), sem("pt1_ready")
        rz_ready, pn_ready, pv_done, oT_ready = sem("rz_ready"), sem("pn_ready"), sem("pv_done"), sem("oT_ready")
        proj_mm, res_done = sem("proj_mm"), sem("res_done")
        mean_mm, cen_done, sqr_done, var_mm, rstd_done, norm_done, ln_done = (
            sem("mean_mm"), sem("cen_done"), sem("sqr_done"), sem("var_mm"), sem("rstd_done"), sem("norm_done"), sem("ln_done"))
        ff1_mm, relu_done, ff2_mm = sem("ff1_mm"), sem("relu_done"), sem("ff2_mm")
        kv2_mm, q2_mm, kv2_ready, q2_ready, q2z_ready = sem("kv2_mm"), sem("q2_mm"), sem("kv2_ready"), sem("q2_ready"), sem("q2z_ready")
        s2_mm, soft2, p2_mm, p2T_ready, o2_mm, om_done, o2_ready, tau_mm = (
            sem("s2_mm"), sem("soft2"), sem("p2_mm"), sem("p2T_ready"), sem("o2_mm"), sem("om_done"), sem("o2_ready"), sem("tau_mm"))
        plus_done, tau_step, win_step, tsum_step, mix_done = sem("plus_done"), sem("tau_step"), sem("win_step"), sem("tsum_step"), sem("mix_done")
        zero_done, vz_zeroed, kp_ready, vz_ready, log_done = sem("zero_done"), sem("vz_zeroed"), sem("kp_ready"), sem("vz_ready"), sem("log_done")

        AHEAD = {pt0_ready: 1, pt1_ready: 1, pv_done: 1, oT_ready: 2}
        two = [slice(0, 2), slice(2, 4)]

        def bank2(b, width=S):
            return ps[:, b, 0:2 * width].rearrange("p (a s) -> p a s", a=2)

        with nc.Block() as block:

            @block.sync
            def _(sp_):
                for count, n in AHEAD.items():
                    sp_.sem_inc(count, n)
                d1, s0 = CONST["dft"][1], CONST["sel"][0]
                sp_.dma_start(xr[:, :, :].rearrange("p c n -> p (c n)"), xrows.rearrange("p c b d -> p (c b d)")).then_inc(s_x, 16)
                sp_.dma_start(cst[:, 0:d1], consts[:, 0:d1]).then_inc(s_dft, 16)
                sp_.dma_start(xT[:, :, :], xcols).then_inc(s_xT, 16)
                sp_.dma_start(cst[:, d1:s0], consts[:, d1:s0]).then_inc(s_const, 16)
                sp_.dma_start(wts[:, :], weights).then_inc(s_w, 16)
                sp_.dma_start(bia[:, :], biases).then_inc(s_w, 16)
                sp_.dma_start(cst[:, s0:NCONST], consts[:, s0:NCONST]).then_inc(s_sel, 16)
                sp_.wait_ge(s_sel, 16)

            @block.gpsimd
            def _(pool):
                pool.wait_ge(s_xT, 16)
                nc.gpsimd.tensor_copy(src[:, :, 0:1], xT[:, :, L - 1:L]).then_inc(last_done, 1)
                nc.gpsimd.memset(vz[:, :, :, :], 0.0).then_inc(vz_zeroed, 1)

                def feed_keys(par, p):
                    k = kT[:, p, :] if isinstance(p, int) else kT[:, bass.ds(p, 1), :].rearrange("p a s -> p (a s)")
                    nc.gpsimd.tensor_copy(kp[:, par, :], k).then_inc(kp_ready, 1)

                def feed_values(par, p):
                    for kt, (k0, kn) in enumerate(QT):
                        blocks = vz[0:kn, par, kt, :].rearrange("p (h x) -> p h x", h=H)
                        for b2 in range(2):
                            c0 = 64 * b2
                            v = vt[0:kn, kt, 128 * p + c0:128 * p + c0 + 64] if isinstance(p, int) else \
                                vt[0:kn, kt, bass.ds(p * 128 + c0, 64)]
                            nc.gpsimd.tensor_copy(blocks[:, :, c0:c0 + DH], v.rearrange("p (h d) -> p h d", h=H)).then_inc(vz_ready, 1)

                pool.wait_ge(k_ready, 2)
                feed_keys(0, 0)
                pool.wait_ge(v_ready, 1)
                pool.wait_ge(vz_zeroed, 1)
                feed_values(0, 0)
                with pool.Fori(0, NPAIR // 2) as pp:
                    for par in range(2):
                        p = pp * 2 + par
                        following = (p + 1) % NPAIR
                        for t in range(8):
                            n = QT[t // 4][1]
                            pool.wait_ge(rz_ready, 8 * p + t + 1)
                            nc.gpsimd.tensor_tensor(P[0:n, t % 4, :, :], P[0:n, t % 4, :, :],
                                                    rz[0:n, t % 4, :, None].to_broadcast([n, 4, S]), ALU.mult).then_inc(pn_ready, 1)
                            if t == 2:
                                pool.wait_ge(score_done, 8 * p + 1)
                                feed_keys(1 - par, following)
                            if t == 4:
                                pool.wait_ge(pv_done, 8 * p + 1)
                                feed_values(1 - par, following)

            @block.tensor
            def _(pe):
                def layer_norm(k, x, ready, n_ready, n):
                    for g in range(2):
                        pe.wait_ge(ready, n_ready + g)
                        nc.tensor.matmul(ps[:, g, 0:2 * S], const("mean"), x[:, two[g], :], start=True, stop=True).then_inc(mean_mm, 1)
                    for g in range(2):
                        pe.wait_ge(sqr_done, 2 * k + g + 1)
                        nc.tensor.matmul(ps[:, 2 + g, 0:2 * S], const("mean"), sqr[:, two[g], :], start=True, stop=True).then_inc(var_mm, 1)

                pe.wait_ge(s_x, 16)
                pe.wait_ge(s_dft, 16)
                pe.wait_ge(zero_done, 2)
                for p in range(NPAIR):
                    for c in range(XCH):
                        mm = nc.tensor.matmul(ps[:, p, 0:2 * NF], xr[:, c, 128 * p:128 * p + 128],
                                              const("dft")[0:XROWS, 2 * NF * c:2 * NF * (c + 1)],
                                              start=(c == 0), stop=(c == XCH - 1))
                    mm.then_inc(dft_done, 1)
                pe.wait_ge(s_w, 32)
                pe.wait_ge(src_done, 1)
                for g in range(2):
                    nc.tensor.matmul(ps[:, 4 + g, 0:2 * S], weight("q1"), src[:, two[g], :], start=True, stop=True).then_inc(qk_mm, 1)
                for g in range(2):
                    nc.tensor.matmul(ps[:, 6 + g, 0:2 * S], weight("k1"), src[:, two[g], :], start=True, stop=True).then_inc(qk_mm, 1)
                for kt, (k0, kn) in enumerate(QT):
                    for p in range(NPAIR):
                        mm = nc.tensor.matmul(ps[0:kn, kt, 128 * p:128 * p + 128], src[:, p, k0:k0 + kn], weight("v1"),
                                              start=True, stop=True)
                    mm.then_inc(v_mm, 1)
                pe.wait_ge(v_ready, 1)

                def scores(par, t):
                    qt, b2, hf = t // 4, (t // 2) % 2, t % 2
                    q0, n = QT[qt]
                    for j in range(4):
                        mm = nc.tensor.matmul(ps[0:n, 2 * hf + j // 2, (j % 2) * S:(j % 2 + 1) * S],
                                              qz[:, par, b2, 4 * hf + j, q0:q0 + n], kp[:, par, :], start=True, stop=True)
                    mm.then_inc(score_done, 1)

                def turn_probabilities(k, t):
                    hf, n = t % 2, QT[t // 4][1]
                    pe.wait_ge(pn_ready, k + 1)
                    pe.wait_ge(pt0_ready, k + 1)
                    pe.wait_ge(pt1_ready, k + 1)
                    for j in range(4):
                        for kt, (k0, kn) in enumerate(QT):
                            mm = nc.tensor.transpose(ps[0:kn, 4 + kt, 95 * j:95 * j + n],
                                                     P[0:n, t % 4, j, k0:k0 + kn], const("eye")[0:n, 0:n])
                    mm.then_inc(ptr_done, 1)

                def values(k, par, t):
                    qt, b2, hf = t // 4, (t // 2) % 2, t % 2
                    n = QT[qt][1]
                    pe.wait_ge(pt0_ready, k + 2)
                    pe.wait_ge(pt1_ready, k + 2)
                    for j in range(4):
                        for kt, (k0, kn) in enumerate(QT):
                            at = 128 * (4 * hf + j) + 64 * b2
                            mm = nc.tensor.matmul(ps[64 * b2:64 * b2 + 64, 6 + qt, 0:n], vz[0:kn, par, kt, at:at + 64],
                                                  PT[0:kn, hf, kt, 95 * j:95 * j + n],
                                                  start=(hf == 0 and j == 0 and kt == 0), stop=(hf == 1 and j == 3 and kt == 1))
                    mm.then_inc(pv_done, 1)

                pe.wait_ge(qz_ready, 2)
                pe.wait_ge(kp_ready, 1)
                scores(0, 0)
                scores(0, 1)
                with pe.Fori(0, NPAIR // 2) as pp:
                    for par in range(2):
                        p = pp * 2 + par
                        for t in range(8):
                            pe.wait_ge(exp_done, 8 * p + t + 1)
                            if t == 6:
                                pe.wait_ge(qz_ready, 2 * p + 4)
                                pe.wait_ge(kp_ready, p + 2)
                            if t < 6:
                                scores(par, t + 2)
                            else:
                                scores(1 - par, t - 6)
                            if t >= 1:
                                turn_probabilities(8 * p + (t - 1), t - 1)
                            if t == 1:
                                pe.wait_ge(vz_ready, 4 * p + 4)
                            if t >= 2:
                                if t in (2, 6):
                                    pe.wait_ge(oT_ready, 2 * p + (t // 4 + 1))
                                values(8 * p + (t - 2), par, t - 2)
                        turn_probabilities(8 * p + 7, 7)
                        values(8 * p + 6, par, 6)
                        values(8 * p + 7, par, 7)
                pe.wait_ge(oT_ready, 2 * NPAIR + 2)
                pe.wait_ge(exp_done, 8 * NPAIR + 2)
                for g in range(2):
                    nc.tensor.matmul(ps[:, 4 + g, 0:2 * S], weight("o1"), oT[:, two[g], :], start=True, stop=True).then_inc(proj_mm, 1)
                layer_norm(0, x1, res_done, 1, 2)
                for b2 in range(2):
                    for hf in range(2):
                        for g in range(2):
                            if b2 == 0 and hf == 0:
                                pe.wait_ge(ln_done, g + 1)
                            bank = (4 * b2 + 2 * hf + g + 4) % 8
                            nc.tensor.matmul(ps[:, bank, 0:2 * S], weight("f1")[64 * b2:64 * b2 + 64, 128 * hf:128 * hf + 128],
                                             x1[64 * b2:64 * b2 + 64, two[g], :], start=True, stop=True).then_inc(ff1_mm, 1)
                for g in range(2):
                    for b2 in range(2):
                        pe.wait_ge(relu_done, 8)
                        for hf in range(2):
                            mm = nc.tensor.matmul(ps[64 * b2:64 * b2 + 64, 4 + g, 0:2 * S], weight("f2")[:, 64 * hf:64 * hf + 64],
                                                  hff[:, b2, hf, 2 * S * g:2 * S * (g + 1)], start=(hf == 0), stop=(hf == 1))
                        mm.then_inc(ff2_mm, 1)
                layer_norm(1, x1, res_done, 3, 2)
                pe.wait_ge(ln_done, 4)
                for g in range(2):
                    nc.tensor.matmul(ps[:, 4 + g, 0:2 * S], weight("k2"), x1[:, two[g], :], start=True, stop=True).then_inc(kv2_mm, 1)
                for kt, (k0, kn) in enumerate(QT):
                    for p in range(NPAIR):
                        mm = nc.tensor.matmul(ps[0:kn, kt, 128 * p:128 * p + 128], x1[:, p, k0:k0 + kn], weight("v2"),
                                              start=True, stop=True)
                    mm.then_inc(kv2_mm, 1)
                nc.tensor.matmul(ps[:, 6, 0:NPAIR], weight("q2"), x1[:, :, S - 1:S].rearrange("p a s -> p (a s)"), start=True, stop=True).then_inc(q2_mm, 1)
                pe.wait_ge(kv2_ready, 2)
                pe.wait_ge(q2z_ready, 1)
                for p in range(NPAIR):
                    mm = nc.tensor.matmul(ps[32 * p:32 * p + 32, 7, 0:S], q2z[:, p, :], kT[:, p, :], start=True, stop=True,
                                          tile_position=(0, 32 * p))
                mm.then_inc(s2_mm, 1)
                pe.wait_ge(soft2, 5)
                for kt, (k0, kn) in enumerate(QT):
                    mm = nc.tensor.transpose(ps[0:kn, 2 + kt, 0:128], s2[:, k0:k0 + kn], const("eye"))
                mm.then_inc(p2_mm, 1)
                pe.wait_ge(p2T_ready, 2)
                pe.wait_ge(kv2_ready, 4)
                for p in range(NPAIR):
                    for kt, (k0, kn) in enumerate(QT):
                        mm = nc.tensor.matmul(ps[:, 5, 2 * H * p:2 * H * (p + 1)], vt[0:kn, kt, 128 * p:128 * p + 128],
                                              p2T[0:kn, kt, 32 * p:32 * p + 2 * H], start=(kt == 0), stop=(kt == 1))
                mm.then_inc(o2_mm, 1)
                pe.wait_ge(o2_ready, 2)
                nc.tensor.matmul(ps[:, 2, 0:NPAIR], weight("o2"), o2[:, :], start=True, stop=True).then_inc(tau_mm, 1)

            @block.scalar
            def _(act):
                def deviations(k):
                    for g in range(2):
                        act.wait_ge(cen_done, 2 * k + g + 1)
                        nc.scalar.activation(sqr[:, two[g], :], cen[:, two[g], :], ACT.Square).then_inc(sqr_done, 1)
                    for g in range(2):
                        act.wait_ge(var_mm, 2 * k + g + 1)
                        nc.scalar.activation(rstd[:, two[g], :], bank2(2 + g), ACT.Ln, bias=epst[:, :]).then_inc(log_done, 1)
                    for g in range(2):
                        act.wait_ge(log_done, 2 * k + g + 1)
                        nc.scalar.activation(rstd[:, two[g], :], rstd[:, two[g], :], ACT.Exp, scale=-0.5).then_inc(rstd_done, 1)

                for p in range(NPAIR):
                    act.wait_ge(dft_done, p + 1)
                    nc.scalar.activation(sq[:, p, :], ps[:, p, 0:2 * NF], ACT.Square).then_inc(sq_done, 1)
                act.wait_ge(power_done, NPAIR)
                nc.scalar.activation(src[:, :, 1:S], amp[:, :, :], ACT.Sqrt).then_inc(amp_done, 1)
                act.wait_ge(s_w, 32)
                for g in range(2):
                    act.wait_ge(qk_mm, g + 1)
                    nc.scalar.activation(qT[:, two[g], :], bank2(4 + g), ACT.Identity, bias=bias("bq1")).then_inc(q_ready, 1)
                act.wait_ge(v_mm, 2)
                nc.scalar.activation(vt[0:95, :, :], ps[0:95, 0:2, :], ACT.Copy).then_inc(v_ready, 1)

                def exponentials(t):
                    hf, n = t % 2, QT[t // 4][1]
                    for j in range(4):
                        a = nc.scalar.activation(P[0:n, t % 4, j, :], ps[0:n, 2 * hf + j // 2, (j % 2) * S:(j % 2 + 1) * S],
                                                 ACT.Exp, bias=ebias[0:n, hf, j:j + 1], scale=DH ** -0.5,
                                                 accum_out=Z[0:n, t % 4, j:j + 1])
                    a.then_inc(exp_done, 1)

                for t in range(2):
                    act.wait_ge(ebias_done, t + 1)
                    exponentials(t)
                with act.Fori(0, NPAIR) as p:
                    def copy_turned(t):
                        act.wait_ge(ptr_done, 8 * p + t + 1)
                        nc.scalar.activation(PT[:, t % 2, 1, :], ps[0:95, 5, 0:380], ACT.Copy).then_inc(pt1_ready, 1)

                    def copy_output(qt):
                        q0, m = QT[qt]
                        act.wait_ge(pv_done, 8 * p + (4 * qt + 4) + 1)
                        nc.scalar.activation(oT[:, bass.ds(p, 1), q0:q0 + m].rearrange("p a s -> p (a s)"),
                                             ps[:, 6 + qt, 0:m], ACT.Identity, bias=bias("bv1")).then_inc(oT_ready, 1)

                    for t in range(8):
                        if t >= 1:
                            copy_turned(t - 1)
                        act.wait_ge(ebias_done, 8 * p + t + 3)
                        exponentials((t + 2) % 8)
                        if t == 6:
                            copy_output(0)
                    copy_turned(7)
                    copy_output(1)
                act.wait_ge(zero_done, 2)
                deviations(0)
                for k in range(8):
                    b2, hf, g = k // 4, (k // 2) % 2, k % 2
                    act.wait_ge(ff1_mm, k + 1)
                    nc.scalar.activation(hff[:, b2, hf, 2 * S * g:2 * S * (g + 1)], ps[:, (k + 4) % 8, 0:2 * S], ACT.Relu,
                                         bias=bias(("fb1a", "fb1b")[hf])).then_inc(relu_done, 1)
                deviations(1)
                act.wait_ge(vz_ready, 4 * (NPAIR + 1))
                for g in range(2):
                    act.wait_ge(kv2_mm, g + 1)
                    nc.scalar.activation(kT[:, two[g], :], bank2(4 + g), ACT.Identity, bias=bias("bk2")).then_inc(kv2_ready, 1)
                act.wait_ge(kv2_mm, 4)
                for kt in range(2):
                    nc.scalar.activation(vt[0:QT[kt][1], kt, :], ps[0:QT[kt][1], kt, :], ACT.Copy).then_inc(kv2_ready, 1)
                act.wait_ge(soft2, 2)
                nc.scalar.activation(s2[:, :], ps[:, 7, 0:S], ACT.Exp, bias=m2[:, 1:2], scale=DH ** -0.5,
                                     accum_out=z2[:, 0:1]).then_inc(soft2, 1)
                act.wait_ge(plus_done, 3)
                nc.scalar.activation(sp[:, 3, :], sp[:, 2, :], ACT.Exp, scale=-1.0).then_inc(plus_done, 1)
                act.wait_ge(plus_done, 4)
                nc.scalar.activation(sp[:, 4, :], sp[:, 3, :], ACT.Ln, bias=1.0).then_inc(plus_done, 1)

            @block.vector
            def _(dve):
                V = nc.vector

                def layer_norm(k, gain, shift):
                    for g in range(2):
                        dve.wait_ge(mean_mm, 2 * k + g + 1)
                        V.tensor_tensor(cen[:, two[g], :], x1[:, two[g], :], bank2(g), ALU.subtract).then_inc(cen_done, 1)
                    for g in range(2):
                        dve.wait_ge(rstd_done, 2 * k + g + 1)
                        V.scalar_tensor_tensor(sqr[:, two[g], :], cen[:, two[g], :], gain, rstd[:, two[g], :], ALU.mult, ALU.mult).then_inc(norm_done, 1)
                        dve.wait_ge(norm_done, 2 * k + g + 1)
                        V.tensor_scalar(x1[:, two[g], :], sqr[:, two[g], :], shift, None, ALU.add).then_inc(ln_done, 1)

                V.memset(epst[:, :], EPS).then_inc(zero_done, 1)
                V.memset(ps[:, :, :], 0.0).then_inc(zero_done, 1)
                V.memset(q2z[:, :, :], 0.0).then_inc(zero_done, 1)
                for p in range(NPAIR):
                    dve.wait_ge(sq_done, p + 1)
                    V.tensor_tensor(amp[:, p, :], sq[:, p, 0:NF], sq[:, p, NF:2 * NF], ALU.add).then_inc(power_done, 1)
                dve.wait_ge(amp_done, 1)
                dve.wait_ge(last_done, 1)
                dve.wait_ge(s_const, 16)
                V.tensor_tensor(src[:, :, :], src[:, :, :], const("pe")[:, None, :].to_broadcast([128, NPAIR, S]), ALU.add).then_inc(src_done, 1)
                dve.wait_ge(s_w, 32)
                for g in range(2):
                    dve.wait_ge(qk_mm, 3 + g)
                    V.tensor_scalar(kT[:, two[g], :], bank2(6 + g), bias("bk1"), None, ALU.add).then_inc(k_ready, 1)

                def row_max(k, t):
                    hf, n = t % 2, QT[t // 4][1]
                    dve.wait_ge(score_done, k + 1)
                    V.tensor_reduce(negmax[0:n, hf, :].rearrange("p (b h) -> p b h", b=2),
                                    ps[0:n, 2 * hf:2 * hf + 2, 0:2 * S].rearrange("p b (h k) -> p b h k", h=2),
                                    AX.X, ALU.max, negate=True).then_inc(max_done, 1)
                    dve.wait_ge(max_done, k + 1)
                    V.tensor_scalar(ebias[0:n, hf, :], negmax[0:n, hf, :], DH ** -0.5, None, ALU.mult).then_inc(ebias_done, 1)

                def mask_queries(par, p, b2):
                    q = qT[:, p:p + 1, :] if isinstance(p, int) else qT[:, bass.ds(p, 1), :]
                    V.tensor_tensor(qz[:, par, b2, :, :], q.to_broadcast([128, H, S]),
                                    const("batch_head")[:, H * b2:H * b2 + H, None].to_broadcast([128, H, S]), ALU.mult).then_inc(qz_ready, 1)

                dve.wait_ge(q_ready, 2)
                for b2 in range(2):
                    mask_queries(0, 0, b2)
                row_max(0, 0)
                row_max(1, 1)
                with dve.Fori(0, NPAIR // 2) as pp:
                    for par in range(2):
                        p = pp * 2 + par

                        def copy_turned(t):
                            dve.wait_ge(ptr_done, 8 * p + t + 1)
                            V.tensor_copy(PT[:, t % 2, 0, :], ps[0:95, 4, 0:380]).then_inc(pt0_ready, 1)

                        for t in range(8):
                            n = QT[t // 4][1]
                            dve.wait_ge(exp_done, 8 * p + t + 1)
                            V.reciprocal(rz[0:n, t % 4, :], Z[0:n, t % 4, :]).then_inc(rz_ready, 1)
                            row_max(8 * p + (t + 2), (t + 2) % 8)
                            if t >= 1:
                                copy_turned(t - 1)
                            if t in (1, 3):
                                mask_queries(1 - par, (p + 1) % NPAIR, t // 2)
                        copy_turned(7)
                for g in range(2):
                    dve.wait_ge(proj_mm, g + 1)
                    V.scalar_tensor_tensor(x1[:, two[g], :], bank2(4 + g), bias("bo1"), src[:, two[g], :], ALU.add, ALU.add).then_inc(res_done, 1)
                layer_norm(0, bias("g1"), bias("b1"))
                for g in range(2):
                    dve.wait_ge(ff2_mm, 2 * g + 2)
                    V.scalar_tensor_tensor(x1[:, two[g], :], bank2(4 + g), bias("fb2"), x1[:, two[g], :], ALU.add, ALU.add).then_inc(res_done, 1)
                layer_norm(1, bias("g2"), bias("b2"))
                dve.wait_ge(q2_mm, 1)
                V.tensor_scalar(q2[:, :], ps[:, 6, 0:NPAIR], bias("bq2"), None, ALU.add).then_inc(q2_ready, 1)
                dve.wait_ge(q2_ready, 1)
                dve.wait_ge(zero_done, 3)
                V.tensor_tensor(q2z[:, :, 0:2 * H], q2[:, :, None].to_broadcast([128, NPAIR, 2 * H]),
                                const("batch_head")[:, None, :].to_broadcast([128, NPAIR, 2 * H]), ALU.mult).then_inc(q2z_ready, 1)
                dve.wait_ge(s2_mm, 1)
                V.tensor_reduce(m2[:, 0:1], ps[:, 7, 0:S], AX.X, ALU.max, negate=True).then_inc(soft2, 1)
                dve.wait_ge(soft2, 1)
                V.tensor_scalar(m2[:, 1:2], m2[:, 0:1], DH ** -0.5, None, ALU.mult).then_inc(soft2, 1)
                dve.wait_ge(soft2, 3)
                V.reciprocal(z2[:, 1:2], z2[:, 0:1]).then_inc(soft2, 1)
                dve.wait_ge(soft2, 4)
                V.tensor_scalar(s2[:, :], s2[:, :], z2[:, 1:2], None, ALU.mult).then_inc(soft2, 1)
                dve.wait_ge(p2_mm, 1)
                for kt, (k0, kn) in enumerate(QT):
                    V.tensor_copy(p2T[0:kn, kt, :], ps[0:kn, 2 + kt, 0:128]).then_inc(p2T_ready, 1)
                dve.wait_ge(o2_mm, 1)
                V.tensor_tensor(om[:, :, :], ps[:, 5, 0:2 * H * NPAIR].rearrange("p (a h) -> p a h", a=NPAIR),
                                const("batch_head")[:, None, :].to_broadcast([128, NPAIR, 2 * H]), ALU.mult).then_inc(om_done, 1)
                dve.wait_ge(om_done, 1)
                V.tensor_reduce(o2[:, :], om[:, :, :], AX.X, ALU.add).then_inc(o2_ready, 1)
                dve.wait_ge(o2_ready, 1)
                V.tensor_scalar(o2[:, :], o2[:, :], bias("bv2"), None, ALU.add).then_inc(o2_ready, 1)
                dve.wait_ge(tau_mm, 1)
                V.tensor_scalar(sp[:, 0, :], ps[:, 2, 0:NPAIR], bias("bo2"), None, ALU.add).then_inc(plus_done, 1)
                dve.wait_ge(plus_done, 1)
                V.tensor_scalar(sp[:, 1, :], sp[:, 0, :], 0.0, None, ALU.max).then_inc(plus_done, 1)
                dve.wait_ge(plus_done, 2)
                V.scalar_tensor_tensor(sp[:, 2, :], sp[:, 1, :], 2.0, sp[:, 0, :], ALU.mult, ALU.subtract).then_inc(plus_done, 1)
                dve.wait_ge(plus_done, 5)
                V.tensor_tensor(sp[:, 5, :], sp[:, 4, :], sp[:, 1, :], ALU.add).then_inc(plus_done, 1)
                dve.wait_ge(plus_done, 6)
                V.tensor_scalar(sp[:, 6, :], sp[:, 5, :], 0.1, 0.01, ALU.mult, ALU.max).then_inc(plus_done, 1)
                dve.wait_ge(plus_done, 7)
                V.tensor_scalar(tau[:, 0, :], sp[:, 6, :], 1.0, None, ALU.min).then_inc(tau_step, 1)
                for k in range(5):
                    n = 1 << k
                    dve.wait_ge(tau_step, k + 1)
                    if k < 4:
                        V.tensor_tensor(tau[:, k + 1, :], tau[:, k, :], tau[:, k, :], ALU.mult).then_inc(tau_step, 1)
                    if k == 0:
                        V.tensor_scalar(tsum[:, 0, :], tau[:, 0, :], 1.0, None, ALU.add).then_inc(tsum_step, 1)
                    else:
                        dve.wait_ge(tsum_step, k)
                        V.scalar_tensor_tensor(tsum[:, k, :], tau[:, k, :], 1.0, tsum[:, k - 1, :], ALU.add, ALU.mult).then_inc(tsum_step, 1)
                    width = L - 2 * n + 1
                    frm = xT if k == 0 else win[:, (k - 1) % 2]
                    if k > 0:
                        dve.wait_ge(win_step, NPAIR * k)
                    for p in range(NPAIR):
                        V.scalar_tensor_tensor(win[:, k % 2, p, 0:width], frm[:, p, 0:width], tau[:, k, p:p + 1],
                                               frm[:, p, n:n + width], ALU.mult, ALU.add).then_inc(win_step, 1)
                dve.wait_ge(tsum_step, 5)
                V.reciprocal(tsum[:, 5, :], tsum[:, 4, :]).then_inc(tsum_step, 1)
                dve.wait_ge(tsum_step, 6)
                dve.wait_ge(win_step, 5 * NPAIR)
                for p in range(NPAIR):
                    V.tensor_scalar(hT[:, p, :], win[:, 0, p, 0:LOUT], tsum[:, 5, p:p + 1], None, ALU.mult).then_inc(mix_done, 1)


def retention(nc, ps, hT, x2T, epst, const, weight):
    with ExitStack() as ctx:
        def sb(name, shape, dt=F32):
            return ctx.enter_context(nc.sbuf_tensor(name, shape, dt))

        def sem(name):
            return ctx.enter_context(nc.semaphore(name))

        cen = sb("r_cen", [128, NPAIR, LOUT])
        sqr = sb("r_sqr", [128, NPAIR, LOUT])
        rstd = sb("r_rstd", [128, NPAIR, LOUT])
        raw = sb("r_raw", [128, 2, NPAIR, LOUT])
        rcos = sb("r_cos", [128, NPAIR, LOUT])
        rqk = sb("r_qk", [128, 2, NPAIR, LOUT])
        rv = sb("r_v", [128, NT, NPAIR * 128])
        dec = sb("r_dec", [128, 2, NT, LOUT])

        mean_mm, cen_done, sqr_done, var_mm, log_done, rlog_done, ln_done = (
            sem("r_mean_mm"), sem("r_cen"), sem("r_sqr"), sem("r_var_mm"), sem("r_log"), sem("r_rstd"), sem("r_ln"))
        raw_mm, raw_ready, rot_mm, cos_done, sin_done, rot_ready = (
            sem("r_raw_mm"), sem("r_raw_ready"), sem("r_rot_mm"), sem("r_cos"), sem("r_sin"), sem("r_rot"))
        v_mm, v_ready, score_mm, dec_ready, ret_mm, ret_done = (
            sem("r_v_mm"), sem("r_v_ready"), sem("r_score_mm"), sem("r_dec"), sem("r_ret_mm"), sem("r_ret"))

        def flat(a):
            return a.rearrange("p a s -> p (a s)")

        with nc.Block() as block:

            @block.tensor
            def _(pe):
                def layer_norm(k, ready, first):
                    for p in range(NPAIR):
                        if ready is not None:
                            pe.wait_ge(ready, first + 2 * p)
                        nc.tensor.matmul(ps[:, p, 0:LOUT], const("mean"), hT[:, p, :], start=True, stop=True).then_inc(mean_mm, 1)
                    for p in range(NPAIR):
                        pe.wait_ge(sqr_done, NPAIR * k + p + 1)
                        nc.tensor.matmul(ps[:, 4 + p, 0:LOUT], const("mean"), sqr[:, p, :], start=True, stop=True).then_inc(var_mm, 1)

                layer_norm(0, None, 0)
                for w in range(2):
                    for p in range(NPAIR):
                        pe.wait_ge(ln_done, p + 1)
                        if w == 1:
                            pe.wait_ge(log_done, NPAIR)
                        nc.tensor.matmul(ps[:, 4 * w + p, 0:LOUT], weight(("rq", "rk")[w]), x2T[:, p, :],
                                         start=True, stop=True).then_inc(raw_mm, 1)
                for w in range(2):
                    for p in range(NPAIR):
                        pe.wait_ge(raw_ready, NPAIR * w + p + 1)
                        nc.tensor.matmul(ps[:, 4 * w + p, 0:LOUT], const("rot"), raw[:, w, p, :],
                                         start=True, stop=True).then_inc(rot_mm, 1)
                for t, (t0, n) in enumerate(TT):
                    pe.wait_ge(sin_done, t + 1)
                    for p in range(NPAIR):
                        mm = nc.tensor.matmul(ps[0:n, t, 128 * p:128 * p + 128], x2T[:, p, t0:t0 + n], weight("rv"),
                                              start=True, stop=True)
                    mm.then_inc(v_mm, 1)

                def scores(b):
                    p, rows = b // 2, slice(64 * (b % 2), 64 * (b % 2) + 64)
                    pe.wait_ge(rot_ready, NPAIR + p + 1)
                    if b == 0:
                        pe.wait_ge(v_ready, NT)
                        pe.wait_ge(sin_done, 2 * NPAIR)
                    if b >= 2:
                        pe.wait_ge(dec_ready, NT * (b - 1))
                    for t, (t0, n) in enumerate(TT):
                        nc.tensor.matmul(ps[0:n, 3 * (b % 2) + t, 0:LOUT - t0], rqk[rows, 1, p, t0:t0 + n],
                                         rqk[rows, 0, p, t0:LOUT], start=True, stop=True).then_inc(score_mm, 1)

                def mix(b):
                    p, b2 = b // 2, b % 2
                    pe.wait_ge(dec_ready, NT * (b + 1))
                    if b >= 2:
                        pe.wait_ge(ret_done, b - 1)
                    for t, (t0, n) in enumerate(TT):
                        mm = nc.tensor.matmul(ps[64 * b2:64 * b2 + 64, 6 + b2, t0:LOUT],
                                              rv[0:n, t, 128 * p + 64 * b2:128 * p + 64 * b2 + 64],
                                              dec[0:n, b2, t, 0:LOUT - t0], start=(t == 0), stop=(t == NT - 1))
                    mm.then_inc(ret_mm, 1)

                scores(0)
                for b in range(B):
                    if b + 1 < B:
                        scores(b + 1)
                    mix(b)
                layer_norm(1, ret_done, 2)

            @block.scalar
            def _(act):
                def deviations(k):
                    for p in range(NPAIR):
                        act.wait_ge(cen_done, NPAIR * k + p + 1)
                        nc.scalar.activation(sqr[:, p, :], cen[:, p, :], ACT.Square).then_inc(sqr_done, 1)
                    for p in range(NPAIR):
                        act.wait_ge(var_mm, NPAIR * k + p + 1)
                        nc.scalar.activation(rstd[:, p, :], ps[:, 4 + p, 0:LOUT], ACT.Ln, bias=epst[:, :]).then_inc(log_done, 1)
                    for p in range(NPAIR):
                        act.wait_ge(log_done, NPAIR * k + p + 1)
                        nc.scalar.activation(rstd[:, p, :], rstd[:, p, :], ACT.Exp, scale=-0.5).then_inc(rlog_done, 1)

                deviations(0)
                for w in range(2):
                    for p in range(NPAIR):
                        act.wait_ge(raw_mm, NPAIR * w + p + 1)
                        nc.scalar.activation(raw[:, w, p, :], ps[:, 4 * w + p, 0:LOUT], ACT.Copy).then_inc(raw_ready, 1)
                for t, (t0, n) in enumerate(TT):
                    act.wait_ge(v_mm, t + 1)
                    nc.scalar.activation(rv[0:n, t, :], ps[0:n, t, :], ACT.Copy).then_inc(v_ready, 1)
                deviations(1)

            @block.gpsimd
            def _(pool):
                for w in range(2):
                    for p in range(NPAIR):
                        pool.wait_ge(raw_ready, NPAIR * w + p + 1)
                        if w == 1:
                            pool.wait_ge(rot_ready, p + 1)
                        nc.gpsimd.tensor_tensor(rcos[:, p, :], raw[:, w, p, :], const("cos"), ALU.mult).then_inc(cos_done, 1)

            @block.vector
            def _(dve):
                V = nc.vector

                def layer_norm(k):
                    for p in range(NPAIR):
                        dve.wait_ge(mean_mm, NPAIR * k + p + 1)
                        V.tensor_tensor(cen[:, p, :], hT[:, p, :], ps[:, p, 0:LOUT], ALU.subtract).then_inc(cen_done, 1)
                    for p in range(NPAIR):
                        dve.wait_ge(rlog_done, NPAIR * k + p + 1)
                        V.tensor_tensor(x2T[:, p, :], cen[:, p, :], rstd[:, p, :], ALU.mult).then_inc(ln_done, 1)

                layer_norm(0)
                for w in range(2):
                    for p in range(NPAIR):
                        dve.wait_ge(rot_mm, NPAIR * w + p + 1)
                        dve.wait_ge(cos_done, NPAIR * w + p + 1)
                        V.tensor_tensor(raw[:, w, p, :], ps[:, 4 * w + p, 0:LOUT], const("sin"), ALU.mult).then_inc(sin_done, 1)
                        dve.wait_ge(sin_done, NPAIR * w + p + 1)
                        V.tensor_tensor(rqk[:, w, p, :], raw[:, w, p, :], rcos[:, p, :], ALU.add).then_inc(rot_ready, 1)

                def decay(b):
                    for t, (t0, n) in enumerate(TT):
                        dve.wait_ge(score_mm, NT * b + t + 1)
                        if b >= 2:
                            dve.wait_ge(ret_mm, b - 1)
                        V.tensor_tensor(dec[0:n, b % 2, t, 0:LOUT - t0], ps[0:n, 3 * (b % 2) + t, 0:LOUT - t0],
                                        const("decay")[0:n, 0:LOUT - t0], ALU.mult).then_inc(dec_ready, 1)

                def add(b):
                    rows = slice(64 * (b % 2), 64 * (b % 2) + 64)
                    dve.wait_ge(ret_mm, b + 1)
                    V.tensor_tensor(hT[rows, b // 2, :], hT[rows, b // 2, :], ps[rows, 6 + b % 2, 0:LOUT], ALU.add).then_inc(ret_done, 1)

                for b in range(B):
                    decay(b)
                    if b >= 1:
                        add(b - 1)
                add(B - 1)
                layer_norm(1)


def product_key_attention(nc, ps, hT, x2T, const, pkw, wq, wo, tables, out):
    with ExitStack() as ctx:
        def sb(name, shape, dt=F32):
            return ctx.enter_context(nc.sbuf_tensor("k_" + name, shape, dt))

        def sem(name):
            return ctx.enter_context(nc.semaphore("k_" + name))

        NDC = NCH // 2
        NSPLIT = NDC // 2
        WINDOW = (0, 2, 3, 1)
        MID0, MID1 = 6, 7

        tab = sb("tab", [128, 2, NCH, 128])
        tab_high = sb("tab_high", [128, 2, NSPLIT, 2, 128], F32R)
        tab_low = sb("tab_low", [128, 2, NSPLIT, 2, 128], F32R)
        wqh = sb("wqh", [64, 2, D])
        wos = sb("wos", [64, H, D])
        pkw_sb = sb("pkw_sb", [DKEY, H, 128])
        pkw0 = const("dft")[0:DKEY, 0:128 * H].rearrange("p (h x) -> p h x", h=H)
        wf = sb("wf", [64, H + 1, 2, NKEY])
        sel = sb("sel", [128, 2, 8, 128], F16)
        eye16 = sb("eye16", [128, 128], F16)
        eyeb = sb("eyeb", [128, 128], BF16)
        causb = sb("causb", [128, 128], BF16)
        y = sb("y", [128, B, NT, D])
        xs = sb("xs", [64, 2, LOUT])
        sS = sb("sS", [128, NT, 2, NKEY])
        rp = sb("rp", [128, NT, 2, NKEY])
        top = sb("top", [128, NT, 2, TOPK])
        cand = sb("cand", [128, NT, NCAND])
        rc = sb("rc", [128, NT, NCAND])
        fin = sb("fin", [128, NT, TOPK])
        small = sb("small", [128, 5, NT])
        MX, AM, LOW, DT, EDT = range(5)
        off = sb("off", [128, NT, 2])
        ecs = sb("ecs", [128, NT, NCAND])
        zs = sb("zs", [128, NT])
        gain = sb("gain", [128, 2, NT])
        aS = sb("aS", [128, NT, 2, 2, 32])
        spl = sb("spl", [128, NT, 5, 2, 32], F16)
        X = sb("X", [128, 2, 4, LOUT], F16)
        W = sb("W", [128, 8, 2, LOUT])
        W_high = sb("W_high", [128, 2, 2, LOUT], F32R)
        W_low = sb("W_low", [128, 2, 2, LOUT], F32R)
        gains = sb("gains", [128, LOUT])
        kv = sb("kv", [128, LOUT])
        vw = sb("vw", [128, NT, D])
        qT = sb("qT", [128, 2, LOUT])
        P = sb("P", [128, NT, LOUT])
        nmax = sb("nmax", [128, NT])
        zz = sb("zz", [128, NT])
        rz = sb("rz", [128, NT])
        PT = sb("PT", [128, NT, LOUT])

        s_tab, tab_high_ready, tab_low_ready = [sem("s_tab0"), sem("s_tab1")], sem("tab_high_ready"), sem("tab_low_ready")
        high_done, low_done = sem("high_done"), sem("low_done")
        s_load, s_wo, s_out, passed = sem("s_load"), sem("s_wo"), sem("s_out"), sem("passed")
        cast_done, zeroed, wf_mm, wf_ready, y_mm0, y_ready0 = (
            sem("cast_done"), sem("zeroed"), sem("wf_mm"), sem("wf_ready"), sem("y_mm0"), sem("y_ready0"))
        xs_ready, sim_mm, sim_ready, top_step, thr_ready, ecs_ready, z_done, rz_z, gain_ready = (
            sem("xs_ready"), sem("sim_mm"), sem("sim_ready"), sem("top_step"), sem("thr_ready"), sem("ecs_ready"),
            sem("z_done"), sem("rz_z"), sem("gain_ready"))
        a_step, low_step, high_ready, low_ready, x_mm, x_ready = (
            sem("a_step"), sem("low_step"), sem("high_ready"), sem("low_ready"), sem("x_mm"), sem("x_ready"))
        log_mm, e_done, w_done, main_done = sem("log_mm"), sem("e_done"), sem("w_done"), sem("main_done")
        gains_mm, gains_ready, kv_ready, vw_mm, vw_ready, q_mm, qT_ready = (
            sem("gains_mm"), sem("gains_ready"), sem("kv_ready"), sem("vw_mm"), sem("vw_ready"), sem("q_mm"), sem("qT_ready"))
        s_mm, nmax_done, p_done, rz_ready, pn_ready, pt_mm, pt_ready, pt1_ready = (
            sem("s_mm"), sem("nmax_done"), sem("p_done"), sem("prz_ready"), sem("pn_ready"), sem("ppt_mm"),
            sem("ppt_ready"), sem("pt1_ready"))
        y_mm, y_done = sem("y_mm"), sem("y_done")
        AHEAD = {q_mm: 1, gain_ready: 1, main_done: 8, y_done: 1}

        def ahead(s):
            return AHEAD[s]

        def wait_alone(eng, s, value):
            eng.wait_ge(s, value)
            eng.sem_inc(passed, 1)

        def score_area(t, pj):
            return ((4 + pj, 0), (4 + pj, 128), (MID1, 0))[t]

        def rounds(eng, body):
            with eng.Fori(0, H // 2) as hh:
                for slot in range(2):
                    body.head(hh, slot)
                    with eng.Fori(0, NPAIR) as pair:
                        for par in range(2):
                            g = hh * 8 + pair + 4 * slot
                            i = hh * 16 + pair * 2 + (8 * slot + par)
                            body.item(i, slot, par, g, pair)

        with nc.Block() as block:

            @block.sync
            def _(sync):
                def load(slot, head):
                    if isinstance(head, int):
                        t, q = tables[head], wq[:, head, :]
                    else:
                        t = tables[bass.ds(head, 1)].rearrange("a p c d -> p (a c) d")
                        q = wq[:, bass.ds(head, 1), :].rearrange("p a d -> p (a d)")
                    sync.dma_start(tab[:, slot, :, :], t).then_inc(s_tab[slot], 16)
                    sync.dma_start(wqh[:, slot, :], q).then_inc(s_tab[slot], 16)

                for s, n in AHEAD.items():
                    sync.sem_inc(s, n)
                sync.dma_start(const("dft")[0:DKEY, 0:128 * H], pkw[:, 0:128 * H]).then_inc(s_load, 16)
                sync.dma_start(pkw_sb[:, :, :].rearrange("p a b -> p (a b)"), pkw[:, 128 * H:256 * H]).then_inc(s_load, 16)
                load(0, 0)
                sync.dma_start(wos[:, :, :], wo).then_inc(s_wo, 16)
                load(1, 1)
                with sync.Fori(0, H // 2 - 1) as hh:
                    for slot in range(2):
                        wait_alone(sync, main_done, hh * (16 * NDC) + (8 * NDC * (slot + 1) + ahead(main_done)))
                        wait_alone(sync, q_mm, hh * 16 + (8 * (slot + 1) + ahead(q_mm)))
                        load(slot, hh * 2 + (slot + 2))
                sync.wait_ge(s_tab[0], 32 * (H // 2))
                sync.sem_inc(s_tab[0], 32)

            @block.tensor
            def _(pe):
                mm_, tr_ = nc.tensor.matmul, nc.tensor.transpose
                eye = const("eye")

                def similarities(n, par, head):
                    wait_alone(pe, xs_ready, n + 1)
                    for t, (t0, m) in enumerate(TT):
                        rhs = (wf[:, head, :, :] if isinstance(head, int) else wf[:, bass.ds(head, 1), :, :].rearrange("p a b k -> p (a b) k"))
                        mm = mm_(ps[0:m, MID0, 128 * t:128 * t + 128], xs[:, par, t0:t0 + m], rhs, start=True, stop=True)
                    mm.then_inc(sim_mm, 1)

                def turn_scores(n, r):
                    if r == 0:
                        pe.wait_ge(low_ready, n + 1)
                    else:
                        pe.wait_ge(x_ready, 2 * n + 1)
                    bank = ps[:, MID0, :].bitcast(F16)
                    for k in range(2):
                        for t, (t0, m) in enumerate(TT):
                            mm = tr_(bank[:, LOUT * k + t0:LOUT * k + t0 + m],
                                     spl[0:m, t, 2 * r + k:2 * r + k + 2, :, :].rearrange("p b x j -> p (b x j)"), eye16[0:m, 0:m])
                    mm.then_inc(x_mm, 1)

                def log_weights(i, par, d):
                    for k in range(2):
                        c = 2 * d + k
                        mm = mm_(ps[:, 2 * (d % 2) + k, 0:LOUT], sel[:, (c // 8) % 2, c % 8, :], X[:, par, c // 8, :], start=True, stop=True)
                    mm.then_inc(log_mm, 1)

                def table_sum(i, slot, par, d):
                    sums = ps[:, 4 + par, 0:LOUT]
                    at = 8 * WINDOW[d // 4] + 2 * (d % 4)
                    if d % 2 == 0:
                        pe.wait_ge(w_done, i * NDC + (d + 1))
                        for k in range(2):
                            mm = mm_(sums, tab[:, slot, at + k, :], W[:, d % 8, k, :], start=(d == 0 and k == 0), stop=False)
                    else:
                        pe.wait_ge(high_done, i * NSPLIT + (d // 2 + 1))
                        for k in range(2):
                            for t in (tab_high, tab_low):
                                mm_(sums, t[:, slot, at // 4, k, :], W_high[:, (d // 2) % 2, k, :], start=False, stop=False)
                        pe.wait_ge(low_done, i * NSPLIT + (d // 2 + 1))
                        for k in range(2):
                            mm = mm_(sums, tab_high[:, slot, at // 4, k, :], W_low[:, (d // 2) % 2, k, :], start=False,
                                     stop=(d == NDC - 1 and k == 1))
                    mm.then_inc(main_done, 1)

                def spread_gains(i, pj):
                    pe.wait_ge(y_done, i + ahead(y_done))
                    pe.wait_ge(gain_ready, i + ahead(gain_ready))
                    for t, (t0, m) in enumerate(TT):
                        mm = tr_(ps[:, MID1, t0:t0 + m], gain[0:m, pj, t:t + 1].to_broadcast([m, 128]), eye[0:m, 0:m])
                    mm.then_inc(gains_mm, 1)

                def queries(i, slot, par, pj):
                    wait_alone(pe, kv_ready, i + 1)
                    mm_(ps[64:128, 4 + pj, 0:LOUT], wqh[:, slot, :], xs[:, par, :], start=True, stop=True).then_inc(q_mm, 1)

                def project_values(i, head):
                    wait_alone(pe, kv_ready, i + 1)
                    rhs = wos[:, head, :] if isinstance(head, int) else wos[:, bass.ds(head, 1), :].rearrange("p a d -> p (a d)")
                    for t, (t0, m) in enumerate(TT):
                        mm = mm_(ps[0:m, MID1, 64 * t:64 * t + 64], kv[0:64, t0:t0 + m], rhs, start=True, stop=True)
                    mm.then_inc(vw_mm, 1)

                def attention_scores(i, pj, last=False):
                    if not last:
                        pe.wait_ge(qT_ready, i + 1)
                    wait_alone(pe, vw_ready, i + 1)
                    for t, (t0, m) in enumerate(TT):
                        keys = t0 + m
                        bank, c0 = score_area(t, pj)
                        mm_(ps[0:m, bank, c0:c0 + keys], qT[64:128, pj, t0:t0 + m], kv[64:128, 0:keys], start=True, stop=False)
                        mm = mm_(ps[0:m, bank, c0 + t0:c0 + keys], eyeb[0:m, 0:m], causb[0:m, 0:m], start=False, stop=True)
                    mm.then_inc(s_mm, 1)

                def turn_probabilities(i, pj):
                    pe.wait_ge(p_done, i + 1)
                    for kt, (k0, kn) in enumerate(TT):
                        bank, c0 = ((MID1, 0), (4 + pj, 0), (MID1, LOUT))[kt]
                        for t, (t0, m) in enumerate(TT):
                            if t >= kt:
                                mm = tr_(ps[0:kn, bank, c0 + t0 - k0:c0 + t0 - k0 + m], P[0:m, t, k0:k0 + kn], eye[0:m, 0:m])
                    mm.then_inc(pt_mm, 1)

                def attention_output(i):
                    pe.wait_ge(pt_ready, i + 1)
                    pe.wait_ge(pt1_ready, i + 1)
                    for t, (t0, m) in enumerate(TT):
                        for kt, (k0, kn) in enumerate(TT[:t + 1]):
                            mm = mm_(ps[0:m, MID1, 64 * t:64 * t + 64], PT[0:kn, kt, t0 - k0:t0 - k0 + m], vw[0:kn, kt, :],
                                     start=(kt == 0), stop=(kt == t))
                    mm.then_inc(y_mm, 1)

                pe.wait_ge(s_load, 32)
                for p in range(2):
                    mm = mm_(ps[0:64, p, 0:64], (pkw0, pkw_sb)[p][:, 0, 0:64], (pkw0, pkw_sb)[p][:, 0, 64:128], start=True, stop=True)
                mm.then_inc(wf_mm, 1)
                pe.wait_ge(wf_ready, 2)
                similarities(0, 0, 0)
                for p in range(2):
                    for h in range(1, H):
                        mm = mm_(ps[0:64, 2 + p, 64 * h:64 * h + 64], (pkw0, pkw_sb)[p][:, h, 0:64], (pkw0, pkw_sb)[p][:, h, 64:128], start=True, stop=True)
                    mm.then_inc(wf_mm, 1)
                pe.wait_ge(wf_ready, 3)
                for t, (t0, m) in enumerate(TT):
                    for p in range(NPAIR):
                        mm = tr_(ps[0:m, (0, 1, 4)[t], 128 * p:128 * p + 128], hT[:, p, t0:t0 + m], eye)
                    mm.then_inc(y_mm0, 1)
                pe.wait_ge(cast_done, 4)
                pe.wait_ge(zeroed, 6)
                pe.wait_ge(wf_ready, 4)
                turn_scores(0, 0)
                turn_scores(0, 1)
                pe.wait_ge(y_ready0, NT)
                log_weights(0, 0, 0)
                log_weights(0, 0, 1)
                for d in range(2):
                    pe.wait_ge(e_done, d + 1)
                    log_weights(0, 0, d + 2)
                pe.wait_ge(x_ready, 2)
                similarities(1, 1, 0)
                pe.wait_ge(s_wo, 16)

                class Body:
                    @staticmethod
                    def head(hh, slot):
                        wait_alone(pe, s_tab[slot], hh * 32 + 32)
                        wait_alone(pe, tab_low_ready, hh * 16 + (8 * slot + 8))

                    @staticmethod
                    def item(i, slot, par, g, pair):
                        nj = 1 - par
                        for d in range(NDC):
                            pe.wait_ge(e_done, i * NDC + (d + 3))
                            if d + 4 < NDC:
                                log_weights(i, par, d + 4)
                            else:
                                if d == NDC - 4:
                                    pe.wait_ge(x_ready, i * 2 + 3)
                                log_weights(i + 1, nj, d + 4 - NDC)
                            table_sum(i, slot, par, d)
                            if d == 0:
                                spread_gains(i, nj)
                            if d == 3:
                                queries(i, slot, par, nj)
                                project_values(i, g // 4 if par else ((g + 31) // 4) % 8)
                            if d == 6:
                                attention_scores(i, nj)
                            if d == 9:
                                turn_scores(i + 1, 0)
                            if d == 10:
                                turn_probabilities(i, nj)
                            if d == 12:
                                turn_scores(i + 1, 1)
                                attention_output(i)
                            if d == 14:
                                pe.wait_ge(x_ready, i * 2 + 4)
                                similarities(i + 2, par, (g + 1) // 4)

                rounds(pe, Body)
                n = H * B
                spread_gains(n, 1)
                project_values(n, H - 1)
                attention_scores(n, 1, last=True)
                turn_probabilities(n, 1)
                attention_output(n)

            @block.scalar
            def _(act):
                A = nc.scalar.activation

                def copy_similarities(n):
                    act.wait_ge(sim_mm, n + 1)
                    A(sS[:, 0:2, :, :], ps[:, MID0, 0:256], ACT.Copy)
                    A(sS[0:88, 2, :, :], ps[0:88, MID0, 256:384], ACT.Copy).then_inc(sim_ready, 1)

                def candidate_weights(n):
                    act.wait_ge(thr_ready, n * 6 + 6)
                    A(ecs[:, :, :], rc[:, :, :], ACT.Exp)
                    A(small[:, EDT, :], small[:, DT, :], ACT.Exp).then_inc(ecs_ready, 1)

                def high_part(n):
                    act.wait_ge(a_step, n * 3 + 3)
                    A(spl[:, :, 0:4, 0, :], aS[:, :, :, :, :].rearrange("p t u a j -> p t (u a) j"), ACT.Copy).then_inc(high_ready, 1)

                def copy_turned(n, par, r):
                    act.wait_ge(x_mm, n * 2 + (r + 1))
                    A(X[:, par, 2 * r:2 * r + 2, :], ps[:, MID0, :].bitcast(F16)[:, 0:2 * LOUT], ACT.Copy).then_inc(x_ready, 1)

                def exponentials(i, d):
                    act.wait_ge(main_done, i * NDC + (d - 7 + ahead(main_done)))
                    act.wait_ge(log_mm, i * NDC + (d + 1))
                    A(W[:, d % 8, :, :], ps[:, 2 * (d % 2):2 * (d % 2) + 2, 0:LOUT], ACT.Exp).then_inc(e_done, 1)

                def weights_high(i, d):
                    act.wait_ge(main_done, i * NDC + (d - 3 + ahead(main_done)))
                    act.wait_ge(w_done, i * NDC + (d + 1))
                    A(W_high[:, (d // 2) % 2, :, :], W[:, d % 8, :, :], ACT.Copy).then_inc(high_done, 1)

                def table_high(slot, loads, part):
                    act.wait_ge(s_tab[slot], loads * 32)
                    if isinstance(part, int):
                        o, rows = tab_high[:, slot, part, :, :], tab[:, slot, 4 * part + 2:4 * part + 4, :]
                    else:
                        o = tab_high[:, slot, bass.ds(part, 1), :, :].rearrange("p a k x -> p (a k) x")
                        rows = tab[:, slot, bass.ds(part * 4 + 2, 2), :]
                    A(o, rows, ACT.Copy).then_inc(tab_high_ready, 1)

                def copy_gains(i):
                    act.wait_ge(gains_mm, i + 1)
                    A(gains[:, :], ps[:, MID1, 0:LOUT], ACT.Copy).then_inc(gains_ready, 1)

                def copy_projected_values(i):
                    act.wait_ge(vw_mm, i + 1)
                    A(vw[:, 0:2, :], ps[:, MID1, 0:128], ACT.Copy)
                    A(vw[0:88, 2, :], ps[0:88, MID1, 128:192], ACT.Copy).then_inc(vw_ready, 1)

                def copy_queries(i, par, pj):
                    act.wait_ge(q_mm, i + (1 + ahead(q_mm)))
                    A(qT[64:128, par, :], ps[64:128, 4 + pj, 0:LOUT], ACT.Copy, scale=D ** -0.5).then_inc(qT_ready, 1)

                def probabilities(i, pj):
                    act.wait_ge(nmax_done, i * 3 + 3)
                    for t, (t0, m) in enumerate(TT):
                        bank, c0 = score_area(t, pj)
                        a = A(P[0:m, t, 0:t0 + m], ps[0:m, bank, c0:c0 + t0 + m], ACT.Exp, bias=nmax[0:m, t:t + 1],
                              accum_out=zz[0:m, t:t + 1])
                    a.then_inc(p_done, 1)

                def copy_turned_probabilities(i):
                    act.wait_ge(pt_mm, i + 1)
                    A(PT[:, 0, :], ps[:, MID1, 0:LOUT], ACT.Copy)
                    A(PT[0:88, 2, 0:88], ps[0:88, MID1, LOUT:LOUT + 88], ACT.Copy).then_inc(pt_ready, 1)

                act.wait_ge(wf_mm, 1)
                A(wf[:, 0, :, :], ps[0:64, 0:2, 0:64], ACT.Copy).then_inc(wf_ready, 1)
                act.wait_ge(zeroed, 6)
                copy_similarities(0)
                for p in range(2):
                    act.wait_ge(wf_mm, p + 2)
                    A(wf[:, 1:H, p, :], ps[0:64, 2 + p, 64:512].rearrange("p (h k) -> p h k", h=H - 1), ACT.Copy).then_inc(wf_ready, 1)
                for t, (t0, m) in enumerate(TT):
                    act.wait_ge(y_mm0, t + 1)
                    A(y[0:m, :, t, :], ps[0:m, (0, 1, 4)[t], :].rearrange("p (b d) -> p b d", b=B), ACT.Copy).then_inc(y_ready0, 1)
                candidate_weights(0)
                for part in range(8):
                    table_high(0, 1, part)
                high_part(0)
                copy_turned(0, 0, 0)
                exponentials(0, 0)

                class Body:
                    @staticmethod
                    def head(hh, slot):
                        pass

                    @staticmethod
                    def item(i, slot, par, g, pair):
                        nj = 1 - par
                        for d in range(NDC):
                            if d + 1 < NDC:
                                exponentials(i, d + 1)
                            else:
                                exponentials(i + 1, 0)
                            if d == 0:
                                copy_turned(i, par, 1)
                            if d == 2:
                                copy_similarities(i + 1)
                            if d == 4:
                                copy_gains(i)
                            if d == 7:
                                copy_queries(i, par, nj)
                                copy_projected_values(i)
                            if d == 9:
                                table_high(1 - slot, i // 16 + (1 + slot), pair * 2 + par)
                            if d == 10:
                                candidate_weights(i + 1)
                                high_part(i + 1)
                            if d == 11:
                                probabilities(i, nj)
                            if d == 13:
                                copy_turned(i + 1, nj, 0)
                            if d == 14:
                                copy_turned_probabilities(i)
                            if d % 2 == 1:
                                weights_high(i, d)

                rounds(act, Body)
                n = H * B
                exponentials(n, 1)
                copy_turned(n, 0, 1)
                copy_gains(n)
                copy_projected_values(n)
                probabilities(n, 1)
                copy_turned_probabilities(n)
                act.wait_ge(y_done, n + 1 + ahead(y_done))
                for t, (t0, m) in enumerate(TT):
                    act.dma_start(out[:, t0:t0 + m, :].rearrange("b t d -> t b d"), y[0:m, :, t, :]).then_inc(s_out, 16)
                act.wait_ge(s_out, 16 * NT)

            @block.gpsimd
            def _(pool):
                G = nc.gpsimd

                def centre_scores(n):
                    pool.wait_ge(thr_ready, n * 6 + 6)
                    for a in range(2):
                        G.tensor_tensor(aS[:, :, :, a, :], sS[:, :, a, :].rearrange("p t (u j) -> p t u j", u=2),
                                        off[:, :, a, None, None].to_broadcast([128, NT, 2, 32]), ALU.subtract).then_inc(a_step, 1)

                def low_part(n):
                    pool.wait_ge(high_ready, n + 1)
                    G.tensor_tensor(spl[:, :, 0:4, 1, :], aS[:, :, :, :, :].rearrange("p t u a j -> p t (u a) j"),
                                    spl[:, :, 0:4, 0, :], ALU.subtract).then_inc(low_step, 1)

                def weights_low(i, d):
                    pool.wait_ge(high_done, i * NSPLIT + (d // 2 + 1))
                    G.tensor_tensor(W_low[:, (d // 2) % 2, :, :], W[:, d % 8, :, :], W_high[:, (d // 2) % 2, :, :].bitcast(F32),
                                    ALU.subtract).then_inc(low_done, 1)

                def table_low(slot, head, part):
                    pool.wait_ge(tab_high_ready, head * 8 + (part + 1))
                    o, high = (a[:, slot, bass.ds(part, 1), :, :].rearrange("p a k x -> p (a k) x") for a in (tab_low, tab_high))
                    G.tensor_tensor(o, tab[:, slot, bass.ds(part * 4 + 2, 2), :], high.bitcast(F32), ALU.subtract).then_inc(tab_low_ready, 1)

                pool.wait_ge(zeroed, 6)
                centre_scores(0)
                low_part(0)

                class Body:
                    @staticmethod
                    def head(hh, slot):
                        pass

                    @staticmethod
                    def item(i, slot, par, g, pair):
                        for d in range(NDC):
                            if d % 2 == 1:
                                weights_low(i, d)
                            if d == 7:
                                centre_scores(i + 1)
                            if d == 9:
                                low_part(i + 1)
                            if d == 13:
                                table_low(1 - slot, i // 8 + 1, pair * 2 + par)

                rounds(pool, Body)

            @block.vector
            def _(dve):
                V = nc.vector
                def take_tokens(par, pair):
                    s = x2T[64 * par:64 * par + 64, pair, :] if isinstance(pair, int) else \
                        x2T[64 * par:64 * par + 64, bass.ds(pair, 1), :].rearrange("p a s -> p (a s)")
                    V.tensor_copy(xs[:, par, :], s).then_inc(xs_ready, 1)

                STEPS = 6 + 6 + 6 + 2 + 3 + 3 + 3

                def halves_max(n, second):
                    if second:
                        wait_alone(dve, top_step, n * STEPS + 12)
                    else:
                        wait_alone(dve, sim_ready, n + 1)
                    for t, (t0, m) in enumerate(TT):
                        for p in range(2):
                            o = top[0:m, t, p, 8:16] if second else top[0:m, t, p, 0:8]
                            V.max(o, (rp if second else sS)[0:m, t, p, :]).then_inc(top_step, 1)

                def halves_drop(n):
                    wait_alone(dve, top_step, n * STEPS + 6)
                    for t, (t0, m) in enumerate(TT):
                        for p in range(2):
                            V.match_replace(rp[0:m, t, p, :], top[0:m, t, p, 0:8], sS[0:m, t, p, :], NEG).then_inc(top_step, 1)

                def candidates(n):
                    dve.wait_ge(top_step, n * STEPS + 18)
                    for r, c, lo, hi, k in ((0, 0, 0, 4, 16), (1, 64, 4, 16, 3)):
                        V.tensor_tensor(cand[:, :, c:c + (hi - lo) * k].rearrange("p t (a b) -> p t a b", b=k),
                                        top[:, :, 1, lo:hi, None].to_broadcast([128, NT, hi - lo, k]),
                                        top[:, :, 0, None, 0:k].to_broadcast([128, NT, hi - lo, k]), ALU.add).then_inc(top_step, 1)

                def sums_max(n, second):
                    wait_alone(dve, top_step, n * STEPS + (26 if second else 20))
                    for t in range(NT):
                        o = fin[:, t, 8:16] if second else fin[:, t, 0:8]
                        V.max(o, (rc if second else cand)[:, t, :]).then_inc(top_step, 1)

                def sums_drop(n):
                    wait_alone(dve, top_step, n * STEPS + 23)
                    for t in range(NT):
                        V.match_replace(rc[:, t, :], fin[:, t, 0:8], cand[:, t, :], NEG).then_inc(top_step, 1)

                def threshold(n):
                    dve.wait_ge(top_step, n * STEPS + STEPS)
                    mx = fin[:, :, 0]
                    V.tensor_reduce(small[:, AM, :], top[:, :, :, :].rearrange("p t a k -> p t (a k)"), AX.X, ALU.max,
                                    apply_absolute_value=True).then_inc(thr_ready, 1)
                    V.tensor_tensor(rc[:, :, :], cand[:, :, :], fin[:, :, 0:1].to_broadcast([128, NT, NCAND]), ALU.subtract).then_inc(thr_ready, 1)
                    dve.wait_ge(thr_ready, n * 6 + 1)
                    V.scalar_tensor_tensor(small[:, LOW, :], small[:, AM, :], -DELTA, fin[:, :, 15], ALU.mult, ALU.add).then_inc(thr_ready, 1)
                    dve.wait_ge(thr_ready, n * 6 + 3)
                    V.scalar_tensor_tensor(small[:, MX, :], mx, -80.0, small[:, LOW, :], ALU.add, ALU.max).then_inc(thr_ready, 1)
                    dve.wait_ge(thr_ready, n * 6 + 4)
                    V.tensor_tensor(small[:, DT, :], small[:, MX, :], mx, ALU.subtract)
                    V.tensor_copy(off[:, :, 1], top[:, :, 1, 0]).then_inc(thr_ready, 1)
                    V.tensor_tensor(off[:, :, 0], small[:, MX, :], top[:, :, 1, 0], ALU.subtract).then_inc(thr_ready, 1)

                def clamp_scores(n):
                    dve.wait_ge(a_step, n * 3 + 2)
                    V.tensor_scalar(aS[:, :, :, :, :], aS[:, :, :, :, :], -NEG, FAR, ALU.min, ALU.max).then_inc(a_step, 1)

                def repeat_block(n):
                    dve.wait_ge(low_step, n + 1)
                    V.tensor_copy(spl[:, :, 4, :, :], spl[:, :, 0, :, :]).then_inc(low_ready, 1)

                def softmax_sum(n):
                    dve.wait_ge(ecs_ready, n + 1)
                    for t in range(NT):
                        V.scalar_tensor_tensor(ecs[:, t, :], cand[:, t, :], small[:, MX, t:t + 1], ecs[:, t, :], ALU.is_ge, ALU.mult,
                                               accum_out=zs[:, t:t + 1]).then_inc(z_done, 1)

                def token_gain(n, par):
                    dve.wait_ge(z_done, n * 3 + 3)
                    V.reciprocal(zs[:, :], zs[:, :]).then_inc(rz_z, 1)
                    dve.wait_ge(rz_z, n + 1)
                    V.tensor_tensor(gain[:, par, :], small[:, EDT, :], zs[:, :], ALU.mult).then_inc(gain_ready, 1)

                def weights(i, d):
                    dve.wait_ge(e_done, i * NDC + (d + 1))
                    V.scalar_tensor_tensor(W[:, d % 8, :, :], W[:, d % 8, :, :], 1.0, W[:, d % 8, :, :],
                                           ALU.is_ge, ALU.mult).then_inc(w_done, 1)

                def scale_sums(i, pj):
                    dve.wait_ge(gains_ready, i + 1)
                    dve.wait_ge(main_done, i * NDC + ahead(main_done))
                    V.tensor_tensor(kv[:, :], ps[:, 4 + pj, 0:LOUT], gains[:, :], ALU.mult).then_inc(kv_ready, 1)

                def row_max(i, pj):
                    dve.wait_ge(s_mm, i + 1)
                    for t, (t0, m) in enumerate(TT):
                        bank, c0 = score_area(t, pj)
                        V.tensor_reduce(nmax[0:m, t:t + 1], ps[0:m, bank, c0:c0 + t0 + m], AX.X, ALU.max, negate=True).then_inc(nmax_done, 1)

                def row_sum(i):
                    dve.wait_ge(p_done, i + 1)
                    V.reciprocal(rz[:, :], zz[:, :]).then_inc(rz_ready, 1)

                def copy_turned_probabilities(i, pj):
                    dve.wait_ge(pt_mm, i + 1)
                    V.tensor_copy(PT[:, 1, 0:216], ps[:, 4 + pj, 0:216]).then_inc(pt1_ready, 1)

                def add_output(i, b):
                    dve.wait_ge(y_mm, i + 1)
                    for t, (t0, m) in enumerate(TT):
                        o = y[0:m, b, t, :] if isinstance(b, int) else y[0:m, bass.ds(b, 1), t, :].rearrange("p a d -> p (a d)")
                        a = V.scalar_tensor_tensor(o, ps[0:m, MID1, 64 * t:64 * t + 64], rz[0:m, t:t + 1], o, ALU.mult, ALU.add)
                    a.then_inc(y_done, 1)

                def cast(o, name):
                    V.tensor_copy(o, const(name)).then_inc(cast_done, 1)

                take_tokens(0, 0)
                take_tokens(1, 0)
                V.memset(wf[:, H, :, :], 0.0).then_inc(wf_ready, 1)
                V.memset(ps[:, 5, :], 0.0).then_inc(zeroed, 1)
                V.memset(qT[:, 1, :], 0.0).then_inc(zeroed, 1)
                V.memset(sS[:, 2, :, :], 0.0).then_inc(zeroed, 1)
                V.memset(top[:, 2, :, :], 0.0).then_inc(zeroed, 1)
                V.memset(gain[:, :, :], 0.0).then_inc(zeroed, 1)
                V.memset(zz[:, :], 1.0).then_inc(zeroed, 1)
                cast(sel[:, :, :, :].rearrange("p w c m -> p (w c m)"), "sel")
                cast(eye16[:, :], "eye")
                cast(eyeb[:, :], "eye")
                cast(causb[:, :], "causal")
                dve.wait_ge(zeroed, 6)
                halves_max(0, False)
                halves_drop(0)
                halves_max(0, True)
                candidates(0)
                sums_max(0, False)
                sums_drop(0)
                sums_max(0, True)
                threshold(0)
                clamp_scores(0)
                softmax_sum(0)
                token_gain(0, 0)
                repeat_block(0)
                dve.wait_ge(tab_high_ready, 8)
                for part in range(8):
                    V.tensor_tensor(tab_low[:, 0, part, :, :], tab[:, 0, 4 * part + 2:4 * part + 4, :],
                                    tab_high[:, 0, part, :, :].bitcast(F32), ALU.subtract).then_inc(tab_low_ready, 1)

                class Body:
                    @staticmethod
                    def head(hh, slot):
                        pass

                    @staticmethod
                    def item(i, slot, par, g, pair):
                        nj = 1 - par
                        for d in range(NDC):
                            weights(i, d)
                            if d == 2:
                                halves_max(i + 1, False)
                            if d == 3:
                                halves_drop(i + 1)
                            if d == 4:
                                halves_max(i + 1, True)
                            if d == 5:
                                scale_sums(i, nj)
                                candidates(i + 1)
                            if d == 6:
                                sums_max(i + 1, False)
                                sums_drop(i + 1)
                            if d == 7:
                                sums_max(i + 1, True)
                            if d == 8:
                                threshold(i + 1)
                            if d == 9:
                                clamp_scores(i + 1)
                            if d == 10:
                                row_max(i, nj)
                            if d == 11:
                                repeat_block(i + 1)
                            if d == 12:
                                row_sum(i)
                                softmax_sum(i + 1)
                            if d == 13:
                                token_gain(i + 1, nj)
                                dve.wait_ge(q_mm, i + 1 + ahead(q_mm))
                                take_tokens(par, (pair + 1) % 4)
                            if d == 14:
                                copy_turned_probabilities(i, nj)
                            if d == 15:
                                add_output(i, pair * 2 if par else ((pair + 3) % 4) * 2 + 1)

                rounds(dve, Body)
                n = H * B
                scale_sums(n, 1)
                row_max(n, 1)
                row_sum(n)
                copy_turned_probabilities(n, 1)
                add_output(n, B - 1)


def _constants():
    c = np.zeros((128, NCONST), np.float32)

    def put(name, a):
        lo, hi = CONST[name]
        a = np.asarray(a, np.float64 if a.dtype == np.float64 else np.float32)
        c[:a.shape[0], lo:hi] = a.reshape(a.shape[0], -1)

    l = np.arange(L).reshape(XCH, XROWS)[:, :, None]
    ang = 2.0 * np.pi * ((l * np.arange(NF)[None, None, :]) % L) / L
    put("dft", np.concatenate([np.cos(ang), np.sin(ang)], 2).transpose(1, 0, 2))
    pos = np.arange(S)[:, None].astype(np.float64)
    div = np.exp(np.arange(0, D, 2) * (-np.log(10000.0) / D))
    pe = np.zeros((S, D), np.float32)
    pe[:, 0::2] = np.sin(pos * div)
    pe[:, 1::2] = np.cos(pos * div)
    put("pe", np.concatenate([pe.T, pe.T], 0))
    put("eye", np.eye(128, dtype=np.float32))
    p = np.arange(128)
    put("mean", (p[:, None] // D == p[None, :] // D) / np.float32(D))
    put("batch_head", (p[:, None] // DH == np.arange(2 * H)[None, :]).astype(np.float32))
    rot = np.zeros((128, 128), np.float32)
    rot[p[1::2], p[0::2]] = -1.0
    rot[p[0::2], p[1::2]] = 1.0
    put("rot", rot)
    inv = (np.float32(1.0) / np.float32(10000.0) ** (np.arange(0, D, 2, dtype=np.float32) / np.float32(D))).astype(np.float32)
    angles = np.arange(LOUT, dtype=np.float32)[None, :] * np.repeat(inv, 2)[:, None]
    put("cos", np.tile(np.cos(angles), (2, 1)))
    put("sin", np.tile(np.sin(angles), (2, 1)))
    diff = np.arange(LOUT)[None, :] - p[:, None]
    put("decay", np.where(diff >= 0, np.exp(np.maximum(diff, 0).astype(np.float32) * np.float32(np.log(0.96875))), 0.0).astype(np.float32))
    put("causal", np.where(p[None, :] > p[:, None], -1.0e30, 0.0).astype(np.float32))
    m = np.arange(128)
    sel = np.zeros((128, 2, 8, 128), np.float32)
    for swapped in range(2):
        for c8 in range(8):
            for part in (0, 32):
                sel[64 * swapped + part + m % 32, swapped, c8, m] = 1.0
                sel[64 * (1 - swapped) + part + 4 * c8 + m // 32, swapped, c8, m] = 1.0
    put("sel", sel)
    return c


def _pair(w):
    z = np.zeros((128, 128), w.dtype)
    z[:64, :64] = w
    z[64:, 64:] = w
    return z


def _twice(w):
    return np.concatenate([w, w], 0)


def _arrays(i):
    t = {k[7:]: np.asarray(v) for k, v in i.items() if k.startswith("L0_tok_")}
    x = np.asarray(i["x"])
    a = {}
    a["consts"] = _constants()
    a["xrows"] = x.reshape(B, XCH, XROWS, D).transpose(2, 1, 0, 3)
    a["xcols"] = x.transpose(0, 2, 1).reshape(NPAIR, 128, L).transpose(1, 0, 2)
    li, mi = t["l_in_w"], t["m_in_w"]
    blocks = {
        "q1": _pair(li[:D].T), "k1": _pair(li[D:2 * D].T), "v1": _pair(li[2 * D:].T), "o1": _pair(t["l_out_w"].T),
        "q2": _pair(mi[:D].T), "k2": _pair(mi[D:2 * D].T), "v2": _pair(mi[2 * D:].T), "o2": _pair(t["m_out_w"].T),
        "f1": _twice(t["ff_w1"].T), "f2": t["ff_w2"].T.reshape(2, 128, D).transpose(1, 0, 2).reshape(128, 2 * D),
        "rq": _pair(np.asarray(i["L0_attn_W_Q"])), "rk": _pair(np.asarray(i["L0_attn_W_K"])),
        "rv": _pair(np.asarray(i["L0_attn_W_V"])),
    }
    a["weights"] = np.concatenate([blocks[n] for n in WT], 1)
    lb, mb = t["l_in_b"], t["m_in_b"]
    cols = {
        "bq1": lb[:D], "bk1": lb[D:2 * D], "bv1": lb[2 * D:], "bo1": t["l_out_b"], "g1": t["ln1_g"], "b1": t["ln1_b"],
        "fb1a": t["ff_b1"][:128], "fb1b": t["ff_b1"][128:], "fb2": t["ff_b2"], "g2": t["ln2_g"], "b2": t["ln2_b"],
        "bq2": mb[:D], "bk2": mb[D:2 * D], "bv2": mb[2 * D:], "bo2": t["m_out_b"],
    }
    a["biases"] = np.stack([cols[n] if cols[n].size == 128 else _twice(cols[n]) for n in BIAS], 1)
    wpk = np.asarray(i["L0_ffn_Wq_pk"]).reshape(D, 2, H, DKEY).transpose(3, 1, 2, 0)
    pk = np.asarray(i["L0_ffn_pk_keys"]).transpose(3, 0, 2, 1)
    a["pkw"] = np.concatenate([wpk, pk], 3).reshape(DKEY, 16 * 128)
    a["wq"] = np.asarray(i["L0_ffn_Wq"]).reshape(D, H, D)
    a["wo"] = np.asarray(i["L0_ffn_Wo"]).reshape(H, D, D).transpose(1, 0, 2)
    tab = np.concatenate([np.asarray(i["L0_ffn_values_table"]), np.asarray(i["L0_ffn_keys_table"])], 1)
    tab = tab.reshape(H, 2, 8, 4, 2, 32, 128)
    a["tables"] = tab.transpose(0, 3, 5, 4, 1, 2, 6).reshape(H, 128, NCH, 128)
    return {k: np.ascontiguousarray(v) for k, v in a.items()}


def kernel(**inputs):
    import concourse.bacc as _bacc
    from concourse.bass_utils import run_bass_kernel_spmd as _run

    nc = _bacc.Bacc("TRN2", target_bir_lowering=False, num_devices=1)
    arrays, args = {}, {}
    for name, a in _arrays(inputs).items():
        arrays[f"in_{name}"] = a
        args[name] = nc.dram_tensor(f"in_{name}", a.shape, mybir.dt.from_np(a.dtype), kind="ExternalInput").ap()
    args["out"] = nc.dram_tensor("out_0", (B, LOUT, D), F32, kind="ExternalOutput").ap()
    audio_tower(nc, **args)
    r = _run(nc, [arrays], core_ids=[0])
    return r.results[0]["out_0"]
```
